# Optimizing a Trainium2 kernel written in Bass

```python
import numpy as np
import jax
import jax.numpy as jnp

def _softmax(x, axis=-1):
    return jax.nn.softmax(x, axis=axis)

def _gelu(x):
    return jax.nn.gelu(x, approximate=True)

def _silu(x):
    return jax.nn.silu(x)

def _sigmoid(x):
    return jax.nn.sigmoid(x)

def _layernorm(x, axis=-1, eps=1e-05):
    m = jnp.mean(x, axis=axis, keepdims=True)
    v = jnp.var(x, axis=axis, keepdims=True)
    return (x - m) / jnp.sqrt(v + eps)

def _scatter_add(tgt, idx, src, axis=0):
    return tgt.at[idx].add(src)

def _segment_sum(src, seg, n):
    return jax.ops.segment_sum(src, seg, n)
kernel_name = 'mk_adaln_ffn_d2_seqx_r4_b99792'

def setup_inputs(seed: int=0):
    np.random.seed(seed)
    _w = jnp.asarray

    def _rec_inputs():
        import jax
        import jax.numpy as jnp
        _rk = jax.random.key(seed)
        x = -0.000125 + 0.9999 * jax.random.normal(jax.random.fold_in(_rk, 1), (4, 512, 512), jnp.float32)
        _lenS = 512 - jax.random.randint(jax.random.fold_in(_rk, 7), (4,), 0, max(1, 512 // 4) + 1, jnp.int32)
        _lenS2 = 512 - jax.random.randint(jax.random.fold_in(_rk, 8), (4,), 0, max(1, 512 // 4) + 1, jnp.int32)
        fside_BxSxS_0 = -1.52775e-05 + 0.999936 * jax.random.normal(jax.random.fold_in(_rk, 11), (4, 512, 512), jnp.float32)
        cond_512 = -5.03954e-05 + 1.00559 * jax.random.normal(jax.random.fold_in(_rk, 12), (4, 128), jnp.float32)
        return (x, fside_BxSxS_0, cond_512)
    x, fside_BxSxS_0, cond_512 = _rec_inputs()

    def _L0_cond_setup():
        import jax, jax.numpy as jnp
        from jax import lax
        import numpy as np
        B, T, C, TD = (8, 512, 512, 128)

        def _bi_wkv(r, k, v, w, u, time_emb):
            tf = jax.nn.sigmoid(jnp.sum(time_emb, axis=-1))[:, None, None]
            decay = jnp.exp(-jnp.exp(w.astype(jnp.float32)))[None, :] * (0.5 + 0.5 * tf[:, :, 0])
            kf = k.astype(jnp.float32)
            vf = v.astype(jnp.float32)
            ek = jnp.exp(jnp.minimum(kf, 30.0))
            ekv = ek * vf

            def step(carry, x):
                a, b = carry
                ekv_t, ek_t = x
                a = a * decay + ekv_t
                b = b * decay + ek_t
                return ((a, b), (a, b))
            ekv_t = jnp.swapaxes(ekv, 0, 1)
            ek_t = jnp.swapaxes(ek, 0, 1)
            init = (jnp.zeros_like(decay), jnp.zeros_like(decay))
            _, (nf, df) = lax.scan(step, init, (ekv_t, ek_t))
            _, (nb, db) = lax.scan(step, init, (ekv_t, ek_t), reverse=True)
            nf = jnp.swapaxes(nf, 0, 1)
            df = jnp.swapaxes(df, 0, 1)
            nb = jnp.swapaxes(nb, 0, 1)
            db = jnp.swapaxes(db, 0, 1)
            euk = jnp.exp(jnp.minimum(u.astype(jnp.float32)[None, None, :] + kf, 30.0))
            num = nf + nb - ekv + euk * vf
            den = df + db - ek + euk
            base = jax.nn.sigmoid(r.astype(jnp.float32)) * (num / jnp.maximum(den, 1e-08))
            out = base * (0.8 + 0.2 * tf)
            return out.astype(r.dtype)
        key = jax.random.key(seed)
        ks = jax.random.split(key, 6)
        return {'r': jax.random.normal(ks[0], (B, T, C), dtype=jnp.float32), 'k': jax.random.normal(ks[1], (B, T, C), dtype=jnp.float32), 'v': jax.random.normal(ks[2], (B, T, C), dtype=jnp.float32), 'w': jax.random.normal(ks[3], (C,), dtype=jnp.float32), 'u': jax.random.normal(ks[4], (C,), dtype=jnp.float32), 'time_emb': jax.random.normal(ks[5], (B, TD), dtype=jnp.float32)}
    _L0_cond_all = _L0_cond_setup()
    _L0_cond_in = {k: v for k, v in _L0_cond_all.items() if k in ('w', 'u')}
    del _L0_cond_all

    def _L0_ffn_setup():
        import jax, jax.numpy as jnp
        import numpy as np
        EPS = 1e-05
        RMS_EPS = 1e-06

        def activation_quant(x, num_bits=8):
            qn = -2 ** (num_bits - 1)
            qp = 2 ** (num_bits - 1) - 1
            xf = x.astype(jnp.float32)
            s = qp / jnp.clip(jnp.max(jnp.abs(xf), axis=-1, keepdims=True), EPS, None)
            return (jnp.clip(jnp.round(xf * s), qn, qp) / s).astype(x.dtype)

        def weight_quant(w):
            wf = w.astype(jnp.float32)
            s = 1.0 / jnp.clip(jnp.mean(jnp.abs(wf)), EPS, None)
            return (jnp.clip(jnp.round(wf * s), -1.0, 1.0) / s).astype(w.dtype)

        def bit_linear(x, w):
            qx = x + jax.lax.stop_gradient(activation_quant(x) - x)
            qw = w + jax.lax.stop_gradient(weight_quant(w) - w)
            return jnp.einsum('bsh,oh->bso', qx, qw)

        def rms_norm(x, weight, eps=RMS_EPS):
            xf = x.astype(jnp.float32)
            var = jnp.mean(xf * xf, axis=-1, keepdims=True)
            return weight * (xf * jax.lax.rsqrt(var + eps)).astype(x.dtype)
        key = jax.random.key(seed)
        k1, k2, k3, k4 = jax.random.split(key, 4)
        B, S, H, I = (2, 512, 512, 2048)
        scale = 1.0 / np.sqrt(H)
        return {'x': jax.random.normal(k1, (B, S, H), dtype=jnp.float32), 'w_gate': jax.random.normal(k2, (I, H), dtype=jnp.float32) * scale, 'w_up': jax.random.normal(k3, (I, H), dtype=jnp.float32) * scale, 'w_down': jax.random.normal(k4, (H, I), dtype=jnp.float32) * (1.0 / np.sqrt(I)), 'ln_weight': jnp.ones((I,), dtype=jnp.float32)}
    _L0_ffn_all = _L0_ffn_setup()
    _L0_ffn_in = {k: v for k, v in _L0_ffn_all.items() if k in ('w_gate', 'w_up', 'w_down', 'ln_weight')}
    del _L0_ffn_all

    def _L1_cond_setup():
        import jax, jax.numpy as jnp
        from jax import lax
        import numpy as np
        B, T, C, TD = (8, 512, 512, 128)

        def _bi_wkv(r, k, v, w, u, time_emb):
            tf = jax.nn.sigmoid(jnp.sum(time_emb, axis=-1))[:, None, None]
            decay = jnp.exp(-jnp.exp(w.astype(jnp.float32)))[None, :] * (0.5 + 0.5 * tf[:, :, 0])
            kf = k.astype(jnp.float32)
            vf = v.astype(jnp.float32)
            ek = jnp.exp(jnp.minimum(kf, 30.0))
            ekv = ek * vf

            def step(carry, x):
                a, b = carry
                ekv_t, ek_t = x
                a = a * decay + ekv_t
                b = b * decay + ek_t
                return ((a, b), (a, b))
            ekv_t = jnp.swapaxes(ekv, 0, 1)
            ek_t = jnp.swapaxes(ek, 0, 1)
            init = (jnp.zeros_like(decay), jnp.zeros_like(decay))
            _, (nf, df) = lax.scan(step, init, (ekv_t, ek_t))
            _, (nb, db) = lax.scan(step, init, (ekv_t, ek_t), reverse=True)
            nf = jnp.swapaxes(nf, 0, 1)
            df = jnp.swapaxes(df, 0, 1)
            nb = jnp.swapaxes(nb, 0, 1)
            db = jnp.swapaxes(db, 0, 1)
            euk = jnp.exp(jnp.minimum(u.astype(jnp.float32)[None, None, :] + kf, 30.0))
            num = nf + nb - ekv + euk * vf
            den = df + db - ek + euk
            base = jax.nn.sigmoid(r.astype(jnp.float32)) * (num / jnp.maximum(den, 1e-08))
            out = base * (0.8 + 0.2 * tf)
            return out.astype(r.dtype)
        key = jax.random.key(seed)
        ks = jax.random.split(key, 6)
        return {'r': jax.random.normal(ks[0], (B, T, C), dtype=jnp.float32), 'k': jax.random.normal(ks[1], (B, T, C), dtype=jnp.float32), 'v': jax.random.normal(ks[2], (B, T, C), dtype=jnp.float32), 'w': jax.random.normal(ks[3], (C,), dtype=jnp.float32), 'u': jax.random.normal(ks[4], (C,), dtype=jnp.float32), 'time_emb': jax.random.normal(ks[5], (B, TD), dtype=jnp.float32)}
    _L1_cond_all = _L1_cond_setup()
    _L1_cond_in = {k: v for k, v in _L1_cond_all.items() if k in ('w', 'u')}
    del _L1_cond_all

    def _L1_ffn_setup():
        import jax, jax.numpy as jnp
        import numpy as np
        HIDDEN = 512
        NUM_EXPERTS = 32
        TOP_K = 4
        MOE_INTER = 192
        GROUP = 2
        NUM_CHUNK = NUM_EXPERTS // GROUP
        CHUNK_INTER = 128
        SMALL_SCALE = 0.05

        def _routing(x2d, gate_w):
            logits = x2d @ gate_w.T
            rw = jax.nn.softmax(logits.astype(jnp.float32), axis=-1)
            scores = jax.nn.sigmoid(logits.astype(jnp.float32))
            _, sel = jax.lax.top_k(scores, TOP_K)
            w = jnp.take_along_axis(rw, sel, axis=-1)
            w = w / w.sum(axis=-1, keepdims=True)
            return (w.astype(x2d.dtype), sel)

        def _moe(x2d, Wg, Wu, Wd, cw):
            g = jnp.einsum('th,ehi->eti', x2d, Wg)
            u = jnp.einsum('th,ehi->eti', x2d, Wu)
            a = jax.nn.silu(g) * u * cw.T[:, :, None]
            return jnp.einsum('eti,eih->th', a, Wd)
        key = jax.random.key(seed)
        ks = jax.random.split(key, 8)
        s = 0.02
        B, S = (2, 512)
        return {'hidden_states': jax.random.normal(ks[0], (B, S, HIDDEN), jnp.float32), 'gate_w': jax.random.normal(ks[1], (NUM_EXPERTS, HIDDEN), jnp.float32) * s, 'Wg': jax.random.normal(ks[2], (NUM_EXPERTS, HIDDEN, MOE_INTER), jnp.float32) * s, 'Wu': jax.random.normal(ks[3], (NUM_EXPERTS, HIDDEN, MOE_INTER), jnp.float32) * s, 'Wd': jax.random.normal(ks[4], (NUM_EXPERTS, MOE_INTER, HIDDEN), jnp.float32) * s, 'cWg': jax.random.normal(ks[5], (NUM_CHUNK, HIDDEN, CHUNK_INTER), jnp.float32) * s, 'cWu': jax.random.normal(ks[6], (NUM_CHUNK, HIDDEN, CHUNK_INTER), jnp.float32) * s, 'cWd': jax.random.normal(ks[7], (NUM_CHUNK, CHUNK_INTER, HIDDEN), jnp.float32) * s}
    _L1_ffn_all = _L1_ffn_setup()
    _L1_ffn_in = {k: v for k, v in _L1_ffn_all.items() if k in ('gate_w', 'Wg', 'Wu', 'Wd', 'cWg', 'cWu', 'cWd')}
    del _L1_ffn_all
    return {'x': x, 'fside_BxSxS_0': fside_BxSxS_0, 'cond_512': cond_512, 'L0_cond_w': _L0_cond_in['w'], 'L0_cond_u': _L0_cond_in['u'], 'L0_ffn_w_gate': _L0_ffn_in['w_gate'], 'L0_ffn_w_up': _L0_ffn_in['w_up'], 'L0_ffn_w_down': _L0_ffn_in['w_down'], 'L0_ffn_ln_weight': _L0_ffn_in['ln_weight'], 'L1_cond_w': _L1_cond_in['w'], 'L1_cond_u': _L1_cond_in['u'], 'L1_ffn_gate_w': _L1_ffn_in['gate_w'], 'L1_ffn_Wg': _L1_ffn_in['Wg'], 'L1_ffn_Wu': _L1_ffn_in['Wu'], 'L1_ffn_Wd': _L1_ffn_in['Wd'], 'L1_ffn_cWg': _L1_ffn_in['cWg'], 'L1_ffn_cWu': _L1_ffn_in['cWu'], 'L1_ffn_cWd': _L1_ffn_in['cWd']}

def reference(x, fside_BxSxS_0, cond_512, L0_cond_w, L0_cond_u, L0_ffn_w_gate, L0_ffn_w_up, L0_ffn_w_down, L0_ffn_ln_weight, L1_cond_w, L1_cond_u, L1_ffn_gate_w, L1_ffn_Wg, L1_ffn_Wu, L1_ffn_Wd, L1_ffn_cWg, L1_ffn_cWu, L1_ffn_cWd):
    import jax
    import jax.numpy as jnp

    def _L0_cond_ref(r, k, v, w, u, time_emb):
        import jax, jax.numpy as jnp
        from jax import lax
        import numpy as np
        B, T, C, TD = (8, 512, 512, 128)

        def _bi_wkv(r, k, v, w, u, time_emb):
            tf = jax.nn.sigmoid(jnp.sum(time_emb, axis=-1))[:, None, None]
            decay = jnp.exp(-jnp.exp(w.astype(jnp.float32)))[None, :] * (0.5 + 0.5 * tf[:, :, 0])
            kf = k.astype(jnp.float32)
            vf = v.astype(jnp.float32)
            ek = jnp.exp(jnp.minimum(kf, 30.0))
            ekv = ek * vf

            def step(carry, x):
                a, b = carry
                ekv_t, ek_t = x
                a = a * decay + ekv_t
                b = b * decay + ek_t
                return ((a, b), (a, b))
            ekv_t = jnp.swapaxes(ekv, 0, 1)
            ek_t = jnp.swapaxes(ek, 0, 1)
            init = (jnp.zeros_like(decay), jnp.zeros_like(decay))
            _, (nf, df) = lax.scan(step, init, (ekv_t, ek_t))
            _, (nb, db) = lax.scan(step, init, (ekv_t, ek_t), reverse=True)
            nf = jnp.swapaxes(nf, 0, 1)
            df = jnp.swapaxes(df, 0, 1)
            nb = jnp.swapaxes(nb, 0, 1)
            db = jnp.swapaxes(db, 0, 1)
            euk = jnp.exp(jnp.minimum(u.astype(jnp.float32)[None, None, :] + kf, 30.0))
            num = nf + nb - ekv + euk * vf
            den = df + db - ek + euk
            base = jax.nn.sigmoid(r.astype(jnp.float32)) * (num / jnp.maximum(den, 1e-08))
            out = base * (0.8 + 0.2 * tf)
            return out.astype(r.dtype)
        return _bi_wkv(r, k, v, w, u, time_emb)

    def _L0_ffn_ref(x, w_gate, w_up, w_down, ln_weight):
        import jax, jax.numpy as jnp
        import numpy as np
        EPS = 1e-05
        RMS_EPS = 1e-06

        def activation_quant(x, num_bits=8):
            qn = -2 ** (num_bits - 1)
            qp = 2 ** (num_bits - 1) - 1
            xf = x.astype(jnp.float32)
            s = qp / jnp.clip(jnp.max(jnp.abs(xf), axis=-1, keepdims=True), EPS, None)
            return (jnp.clip(jnp.round(xf * s), qn, qp) / s).astype(x.dtype)

        def weight_quant(w):
            wf = w.astype(jnp.float32)
            s = 1.0 / jnp.clip(jnp.mean(jnp.abs(wf)), EPS, None)
            return (jnp.clip(jnp.round(wf * s), -1.0, 1.0) / s).astype(w.dtype)

        def bit_linear(x, w):
            qx = x + jax.lax.stop_gradient(activation_quant(x) - x)
            qw = w + jax.lax.stop_gradient(weight_quant(w) - w)
            return jnp.einsum('bsh,oh->bso', qx, qw)

        def rms_norm(x, weight, eps=RMS_EPS):
            xf = x.astype(jnp.float32)
            var = jnp.mean(xf * xf, axis=-1, keepdims=True)
            return weight * (xf * jax.lax.rsqrt(var + eps)).astype(x.dtype)
        h = jax.nn.silu(bit_linear(x, w_gate)) * bit_linear(x, w_up)
        h = rms_norm(h, ln_weight)
        return bit_linear(h, w_down)

    def _L1_cond_ref(r, k, v, w, u, time_emb):
        import jax, jax.numpy as jnp
        from jax import lax
        import numpy as np
        B, T, C, TD = (8, 512, 512, 128)

        def _bi_wkv(r, k, v, w, u, time_emb):
            tf = jax.nn.sigmoid(jnp.sum(time_emb, axis=-1))[:, None, None]
            decay = jnp.exp(-jnp.exp(w.astype(jnp.float32)))[None, :] * (0.5 + 0.5 * tf[:, :, 0])
            kf = k.astype(jnp.float32)
            vf = v.astype(jnp.float32)
            ek = jnp.exp(jnp.minimum(kf, 30.0))
            ekv = ek * vf

            def step(carry, x):
                a, b = carry
                ekv_t, ek_t = x
                a = a * decay + ekv_t
                b = b * decay + ek_t
                return ((a, b), (a, b))
            ekv_t = jnp.swapaxes(ekv, 0, 1)
            ek_t = jnp.swapaxes(ek, 0, 1)
            init = (jnp.zeros_like(decay), jnp.zeros_like(decay))
            _, (nf, df) = lax.scan(step, init, (ekv_t, ek_t))
            _, (nb, db) = lax.scan(step, init, (ekv_t, ek_t), reverse=True)
            nf = jnp.swapaxes(nf, 0, 1)
            df = jnp.swapaxes(df, 0, 1)
            nb = jnp.swapaxes(nb, 0, 1)
            db = jnp.swapaxes(db, 0, 1)
            euk = jnp.exp(jnp.minimum(u.astype(jnp.float32)[None, None, :] + kf, 30.0))
            num = nf + nb - ekv + euk * vf
            den = df + db - ek + euk
            base = jax.nn.sigmoid(r.astype(jnp.float32)) * (num / jnp.maximum(den, 1e-08))
            out = base * (0.8 + 0.2 * tf)
            return out.astype(r.dtype)
        return _bi_wkv(r, k, v, w, u, time_emb)

    def _L1_ffn_ref(hidden_states, gate_w, Wg, Wu, Wd, cWg, cWu, cWd):
        import jax, jax.numpy as jnp
        import numpy as np
        HIDDEN = 512
        NUM_EXPERTS = 32
        TOP_K = 4
        MOE_INTER = 192
        GROUP = 2
        NUM_CHUNK = NUM_EXPERTS // GROUP
        CHUNK_INTER = 128
        SMALL_SCALE = 0.05

        def _routing(x2d, gate_w):
            logits = x2d @ gate_w.T
            rw = jax.nn.softmax(logits.astype(jnp.float32), axis=-1)
            scores = jax.nn.sigmoid(logits.astype(jnp.float32))
            _, sel = jax.lax.top_k(scores, TOP_K)
            w = jnp.take_along_axis(rw, sel, axis=-1)
            w = w / w.sum(axis=-1, keepdims=True)
            return (w.astype(x2d.dtype), sel)

        def _moe(x2d, Wg, Wu, Wd, cw):
            g = jnp.einsum('th,ehi->eti', x2d, Wg)
            u = jnp.einsum('th,ehi->eti', x2d, Wu)
            a = jax.nn.silu(g) * u * cw.T[:, :, None]
            return jnp.einsum('eti,eih->th', a, Wd)
        B, S, H = hidden_states.shape
        T = B * S
        x = hidden_states.reshape(T, H)
        w, sel = _routing(x, gate_w)
        rows = jnp.arange(T)[:, None]
        cw_large = jnp.zeros((T, NUM_EXPERTS), x.dtype).at[rows, sel].add(w)
        cw_small = jnp.zeros((T, NUM_CHUNK), x.dtype).at[rows, sel // GROUP].add(w)
        large = _moe(x, Wg, Wu, Wd, cw_large)
        small = _moe(x, cWg, cWu, cWd, cw_small)
        return (large + SMALL_SCALE * small).reshape(B, S, H)
    x = x + _L0_ffn_ref(_L0_cond_ref(x, fside_BxSxS_0, fside_BxSxS_0, L0_cond_w, L0_cond_u, cond_512), L0_ffn_w_gate, L0_ffn_w_up, L0_ffn_w_down, L0_ffn_ln_weight)
    x = x + _L1_ffn_ref(_L1_cond_ref(x, fside_BxSxS_0, fside_BxSxS_0, L1_cond_w, L1_cond_u, cond_512), L1_ffn_gate_w, L1_ffn_Wg, L1_ffn_Wu, L1_ffn_Wd, L1_ffn_cWg, L1_ffn_cWu, L1_ffn_cWd)
    return x

_drawn_inputs = setup_inputs


def setup_inputs(seed=0):
    import zlib

    import numpy as np

    out = dict(_drawn_inputs(seed))
    spreads = {'L0_ffn_ln_weight': (1.0, 0.2)}
    factors = {'L1_cond_w': 8.0,
     'L1_cond_u': 8.0,
     'L1_ffn_gate_w': 8.0,
     'L1_ffn_Wg': 8.0,
     'L1_ffn_Wu': 8.0,
     'L1_ffn_Wd': 8.0,
     'L1_ffn_cWg': 8.0,
     'L1_ffn_cWu': 8.0,
     'L1_ffn_cWd': 8.0}
    for name, (base, spread) in spreads.items():
        noise = np.random.default_rng([zlib.crc32(name.encode()), seed]).standard_normal(out[name].shape)
        drawn = base * np.exp(spread * noise) if base else spread * noise
        out[name] = jnp.asarray(drawn.astype(out[name].dtype))
    for name, factor in factors.items():
        out[name] = (out[name] * factor).astype(out[name].dtype)
    return out
```

```python
from contextlib import ExitStack

import numpy as np

import concourse.bass as bass
from concourse import mybir

F32 = mybir.dt.float32
BF16 = mybir.dt.bfloat16
I32 = mybir.dt.int32
U32 = mybir.dt.uint32
ALU = mybir.AluOpType
ACT = mybir.ActivationFunctionType
AX = mybir.AxisListType

P = 128
B, T, C = 4, 512, 512
TOKENS = B * T
TILES = TOKENS // P
TT = T // P
CT = C // P
LAYERS = 2
UNITS = CT * LAYERS
INNER = 2048
IT = INNER // P
NCH = INNER // 512
EPS = 1e-5
RMS_EPS = 1e-6
QP = 127.0
ROUND = 12582912.0
E = 32
K = 4
LARGE, SMALL = 192, 128
WIDE = LARGE + SMALL
SMALL_SCALE = 0.05
LISTED = TOKENS * K // P + E
JT = TOKENS // P
LEAD = 4


def done(n):
    return n + LEAD


def setup(nc, A, S):
    with ExitStack() as ctx:
        def sb(name, shape, dt):
            return ctx.enter_context(nc.sbuf_tensor(name, shape, dt))

        def sem(name):
            return ctx.enter_context(nc.semaphore(name))

        condT = sb("cond_T", [P, B], F32)
        wdec = sb("decay_w", [P, LAYERS, CT], F32)
        time = sb("time_gate", [P, B], F32)
        half = sb("time_half", [P, B], F32)
        gate_rows = sb("gate_rows", [E, C], F32)
        ps_t = ctx.enter_context(nc.psum_tensor("ps_time", [P, B], F32))
        ps_g = ctx.enter_context(nc.psum_tensor("ps_gate_w", [P, CT * E], F32))

        small_in = sem("p_small_in")
        u_in = sem("p_u_in")
        zeroed = sem("p_zeroed")
        consts = sem("p_consts")
        exp_w = sem("p_exp_w")
        decay0 = sem("p_decay0")
        tsum = sem("p_time_sum")
        ttanh = sem("p_time_tanh")
        gturned = sem("p_gate_turned")
        dve_seq = sem("p_dve_seq")
        block = ctx.enter_context(nc.Block())

        @block.sync
        def _(sp):
            with nc.allow_non_contiguous_dma("a few hundred small vectors' elements"):
                sp.dma_start(condT[:], A["cond_512"].rearrange("b k -> k b")).then_inc(small_in, 16)
                for l in range(LAYERS):
                    sp.dma_start(wdec[:, l, :], A[f"L{l}_cond_w"].rearrange("(c p) -> p c", p=P)).then_inc(small_in, 16)
                    sp.dma_start(S["u"][:, l, :], A[f"L{l}_cond_u"].rearrange("(c p) -> p c", p=P)).then_inc(u_in, 16)
            sp.dma_start(gate_rows[:], A["L1_ffn_gate_w"]).then_inc(small_in, 16)
            sp.wait_ge(u_in, 32)

        @block.gpsimd
        def _(pool):
            nc.gpsimd.memset(S["ident"][:], 0.0)
            nc.gpsimd.memset(S["identb"][:], 0.0)
            nc.gpsimd.memset(S["tri"][:], 1.0)
            nc.gpsimd.memset(S["ones"][:], 1.0)
            nc.gpsimd.memset(S["round"][:], ROUND)
            nc.gpsimd.memset(S["zrow"][:], 0)
            nc.gpsimd.memset(S["mhalf"][:], -0.5).then_inc(zeroed, 1)
            pool.wait_ge(zeroed, 1)
            for m in (S["ident"], S["identb"]):
                nc.gpsimd.affine_select(out=m[:], in_=m[:], compare_op=ALU.not_equal, fill=1.0, base=0,
                                        pattern=[[-1, P]], channel_multiplier=1)
            nc.gpsimd.affine_select(out=S["tri"][:], in_=S["tri"][:], compare_op=ALU.is_gt, fill=0.0, base=0,
                                    pattern=[[1, P]], channel_multiplier=-1)
            nc.gpsimd.iota(S["token"][:], pattern=[[P, TILES]], base=0, channel_multiplier=1)
            nc.gpsimd.iota(S["iota_e"][:], pattern=[[1, E]], base=0, channel_multiplier=0, allow_small_or_imprecise_dtypes=True)
            nc.gpsimd.iota(S["iota_t"][:], pattern=[[1, LISTED]], base=0, channel_multiplier=0,
                           allow_small_or_imprecise_dtypes=True).then_inc(consts, 1)

        @block.scalar
        def _(act):
            act.wait_ge(small_in, 16 * 4)
            nc.scalar.activation(wdec[:], wdec[:], ACT.Exp).then_inc(exp_w, 1)
            act.wait_ge(exp_w, 1)
            nc.scalar.activation(wdec[:], wdec[:], ACT.Exp, scale=-1.0).then_inc(decay0, 1)
            act.wait_ge(tsum, 1)
            nc.scalar.activation(time[:], ps_t[:], ACT.Tanh, scale=0.5).then_inc(ttanh, 1)

        @block.vector
        def _(dve):
            seq = [0]

            def link(ins):
                seq[0] += 1
                ins.then_inc(dve_seq, 1)
                dve.wait_ge(dve_seq, seq[0])

            dve.wait_ge(ttanh, 1)
            link(nc.vector.tensor_scalar(time[:], time[:], 0.5, 0.5, ALU.mult, ALU.add))
            link(nc.vector.tensor_scalar(half[:], time[:], 0.5, 0.5, ALU.mult, ALU.add))
            for b in range(B):
                nc.vector.tensor_scalar(S["tfs"][:, b * TT:(b + 1) * TT], time[:, b:b + 1].to_broadcast([P, TT]), 0.1, 0.4,
                                        ALU.mult, ALU.add)
            dve.wait_ge(decay0, 1)
            for b in range(B):
                nc.vector.tensor_scalar(S["decay"][:, b * UNITS:(b + 1) * UNITS].rearrange("p (c l) -> p l c", l=LAYERS),
                                        wdec[:], half[:, b:b + 1], None, ALU.mult)
            dve.wait_ge(gturned, 1)
            nc.vector.tensor_copy(S["gate_wT"][:].rearrange("p k e -> p (k e)"), ps_g[:])

        @block.tensor
        def _(pe):
            pe.wait_ge(consts, 1)
            pe.wait_ge(small_in, 16 * 4)
            nc.tensor.matmul(ps_t[:], S["ones"][:], condT[:], start=True, stop=True).then_inc(tsum, 1)
            for k in range(CT):
                last = nc.tensor.transpose(ps_g[:, k * E:(k + 1) * E], gate_rows[:, k * P:(k + 1) * P], S["ident"][0:E, 0:E])
            last.then_inc(gturned, 1)


def ternary(nc, A, S):
    with ExitStack() as ctx:
        def sb(name, shape, dt):
            return ctx.enter_context(nc.sbuf_tensor(name, shape, dt))

        def sem(name):
            return ctx.enter_context(nc.semaphore(name))

        NW = 4
        QW = INNER * C // P // NW
        ws = sb("weight_stage", [P, NW * QW], F32)
        wq = sb("weight_half", [P, 2 * QW], BF16)
        absum = sb("abs_sums", [P, 3, NW], F32)
        part = sb("abs_part", [P, 3], F32)
        rscale = sb("weight_rscale", [P, 3], F32)
        junk = sb("abs_junk", [P, QW], BF16)
        ps_sum = ctx.enter_context(nc.psum_tensor("ps_sum", [P, 4], F32))
        ps_t = [ctx.enter_context(nc.psum_tensor(f"ps_wt{i}", [P, 1024], BF16)) for i in range(2)]

        x_in = sem("w_x_in")
        ln_in = sem("w_ln_in")
        w_in = sem("w_in")
        abs_done = sem("w_abs_done")
        part_done = sem("w_part_done")
        sum_done = sem("w_sum_done")
        scale_done = sem("w_scale_done")
        dve_seq = sem("w_dve_seq")
        rounded = sem("w_rounded")
        ternary_done = sem("w_ternary")
        turned = sem("w_turned")
        copied = sem("w_copied")

        weights = [A["L0_ffn_w_gate"].rearrange("(n p) h -> p n h", p=P),
                   A["L0_ffn_w_up"].rearrange("(n p) h -> p n h", p=P),
                   A["L0_ffn_w_down"].rearrange("(n p) i -> p n i", p=P)]
        block = ctx.enter_context(nc.Block())

        @block.sync
        def _(sp):
            for m in range(3):
                if m:
                    sp.wait_ge(ternary_done, NW * m)
                sp.dma_start(ws[:].rearrange("p (n h) -> p n h", h=weights[m].shape[2]), weights[m]).then_inc(w_in, 16)
                if m == 0:
                    sp.dma_start(S["x"][:], A["x"].rearrange("b (n p) c -> p (b n) c", p=P)).then_inc(x_in, 16)
                    sp.dma_start(S["ln"][:], A["L0_ffn_ln_weight"].rearrange("(a i) -> a i", a=1).to_broadcast([P, INNER])).then_inc(ln_in, 16)
            for s in (x_in, ln_in):
                sp.wait_ge(s, 16)

        @block.scalar
        def _(act):
            for m in range(3):
                act.wait_ge(w_in, 16 * (m + 1))
                for c in range(NW):
                    if m + c:
                        act.wait_ge(abs_done, m * NW + c)
                    nc.scalar.activation(junk[:], ws[:, c * QW:(c + 1) * QW], ACT.Abs,
                                         accum_out=absum[:, m, c:c + 1]).then_inc(abs_done, 1)
                act.wait_ge(scale_done, m + 1)
                for c in range(NW):
                    v = ws[:, c * QW:(c + 1) * QW]
                    nc.scalar.activation(v, v, ACT.Identity, scale=rscale[:, m:m + 1], bias=S["round"][:, 0:1]).then_inc(rounded, 1)

        @block.vector
        def _(dve):
            seq = [0]

            def link(ins):
                seq[0] += 1
                ins.then_inc(dve_seq, 1)
                dve.wait_ge(dve_seq, seq[0])

            for m in range(3):
                dve.wait_ge(abs_done, (m + 1) * NW)
                nc.vector.tensor_reduce(part[:, m:m + 1], absum[:, m, :], AX.X, ALU.add).then_inc(part_done, 1)
                dve.wait_ge(sum_done, m + 1)
                link(nc.vector.tensor_scalar(S["wscale"][:, m:m + 1], ps_sum[:, m:m + 1], 1.0 / (INNER * C), EPS,
                                             ALU.mult, ALU.max))
                nc.vector.reciprocal(rscale[:, m:m + 1], S["wscale"][:, m:m + 1]).then_inc(scale_done, 1)
                for c in range(NW):
                    dve.wait_ge(rounded, m * NW + c + 1)
                    if c % 2 == 0 and m + c:
                        dve.wait_ge(turned, 8 * m + 2 * c)
                    q = wq[:, (c % 2) * QW:(c % 2 + 1) * QW]
                    link(nc.vector.tensor_scalar(q, ws[:, c * QW:(c + 1) * QW], -ROUND, 1.0, ALU.add, ALU.min))
                    nc.vector.tensor_scalar(q, q, -1.0, None, ALU.max).then_inc(ternary_done, 1)
                    if c % 2:
                        for g in range(c // 2 * 4, c // 2 * 4 + 4):
                            dve.wait_ge(turned, 8 * m + g + 1)
                            if m < 2:
                                out = S["wT"][m][:, g % 4, (g // 4) * 1024:(g // 4 + 1) * 1024]
                                src = ps_t[g % 2][:]
                            else:
                                out = S["wT"][m][:, (g % 2) * 8:(g % 2 + 1) * 8, (g // 2) * P:(g // 2 + 1) * P]
                                src = ps_t[g % 2][:].rearrange("p (k o) -> p k o", o=P)
                            nc.vector.tensor_copy(out, src).then_inc(copied, 1)

        @block.tensor
        def _(pe):
            for m in range(3):
                pe.wait_ge(part_done, m + 1)
                nc.tensor.matmul(ps_sum[:, m:m + 1], S["ones"][:], part[:, m:m + 1], start=True, stop=True).then_inc(sum_done, 1)
                for g in range(8):
                    if g % 4 == 0:
                        pe.wait_ge(ternary_done, NW * m + g // 2 + 2)
                    if 8 * m + g >= 2:
                        pe.wait_ge(copied, 8 * m + g - 1)
                    for a in range(8):
                        if m < 2:
                            src = wq[:, a * C + (g % 4) * P:a * C + (g % 4 + 1) * P]
                        else:
                            k = (g % 2) * 8 + a
                            src = wq[:, (g // 2 % 2) * INNER + k * P:(g // 2 % 2) * INNER + (k + 1) * P]
                        last = nc.tensor.transpose(ps_t[g % 2][:, a * P:(a + 1) * P], src, S["identb"][:])
                    last.then_inc(turned, 1)


def mix(nc, A, S):
    with ExitStack() as ctx:
        def sb(name, shape, dt):
            return ctx.enter_context(nc.sbuf_tensor(name, shape, dt))

        def sem(name):
            return ctx.enter_context(nc.semaphore(name))

        side = sb("side", [P, TT, C], F32)
        kt = sb("key", [P, 2, T], F32)
        km = sb("key_min", [P, 2, T], F32)
        ek = sb("exp_key", [P, 2, T], F32)
        ekv = sb("exp_key_value", [P, 2, T], F32)
        ua = sb("bonus_arg", [P, 2, T], F32)
        eu = sb("exp_bonus", [P, 2, T], F32)
        euv = sb("exp_bonus_value", [P, 2, T], F32)
        fwd = [[sb(f"forward{q}{l}", [P, T], F32) for l in range(2)] for q in range(2)]
        bwd = [[sb(f"backward{q}{l}", [P, T + 1], F32) for l in range(2)] for q in range(2)]
        dmax = sb("den_max", [P, T], F32)
        rden = sb("den_reciprocal", [P, T], F32)
        diag = sb("decay_diagonals", [P, B * UNITS, P], F32)
        ps_k = [ctx.enter_context(nc.psum_tensor(f"ps_key{i}", [P, T], F32)) for i in range(2)]
        ps_q = [[ctx.enter_context(nc.psum_tensor(f"ps_sum{q}{l}", [P, T], F32)) for l in range(2)] for q in range(2)]

        side_in = sem("m_side_in")
        turned = sem("m_turned")
        key = sem("m_key")
        keymin = sem("m_keymin")
        expk = sem("m_expk")
        expkv = sem("m_expkv")
        arg = sem("m_arg")
        expu = sem("m_expu")
        expuv = sem("m_expuv")
        scanned = sem("m_scanned")
        summed = sem("m_summed")
        ratio = sem("m_ratio")
        chain = sem("m_chain")
        tails = sem("m_tails")
        diag_done = sem("m_diag")

        block = ctx.enter_context(nc.Block())

        @block.sync
        def _(sp):
            with sp.Fori(0, B) as b:
                sp.wait_ge(turned, done(b * CT))
                sp.dma_start(side[:], A["fside_BxSxS_0"][bass.ds(b, 1), :, :].rearrange("b (n p) c -> p (b n) c", p=P)).then_inc(side_in, 16)

        @block.tensor
        def _(pe):
            pe.sem_inc(turned, LEAD)
            pe.sem_inc(summed, LEAD)
            pe.wait_ge(tails, 1)
            pe.wait_ge(diag_done, 1)
            with pe.Fori(0, B) as b:
                pe.wait_ge(side_in, b * 16 + 16)

                def turn(ct):
                    pe.wait_ge(key, done(b * CT + ct - 1))
                    for tt in range(TT):
                        last = nc.tensor.transpose(ps_k[ct % 2][:, tt * P:(tt + 1) * P], side[:, tt, ct * P:(ct + 1) * P], S["ident"][:])
                    last.then_inc(turned, 1)

                turn(0)
                for ct in range(CT):
                    if ct + 1 < CT:
                        turn(ct + 1)
                    for l in range(LAYERS):
                        u = b * UNITS + ct * LAYERS + l
                        pe.wait_ge(scanned, done(u + 1))
                        pe.wait_ge(expuv, done(u + 1))
                        pe.wait_ge(ratio, done(u - 1))
                        for q, extra in ((0, euv), (1, eu)):
                            for tt in range(TT):
                                out = ps_q[q][l][:, tt * P:(tt + 1) * P]
                                at = slice(tt * P, (tt + 1) * P)
                                nc.tensor.matmul(out, fwd[q][l][:, at], S["ident"][:], start=True, stop=False)
                                nc.tensor.matmul(out, bwd[q][l][:, tt * P + 1:(tt + 1) * P + 1], diag[:, bass.ds(u, 1), :].rearrange("p a c -> p (a c)"),
                                                 start=False, stop=False)
                                last = nc.tensor.matmul(out, extra[:, l, at], S["ident"][:], start=False, stop=True)
                        last.then_inc(summed, 1)

        @block.scalar
        def _(act):
            act.sem_inc(key, LEAD)
            act.sem_inc(expk, LEAD)
            act.sem_inc(expu, LEAD)
            with act.Fori(0, B) as b:
                for ct in range(CT):
                    c = b * CT + ct
                    act.wait_ge(turned, done(c + 1))
                    act.wait_ge(expuv, done(2 * c - 2))
                    nc.scalar.activation(kt[:, ct % 2, :], ps_k[ct % 2][:], ACT.Copy).then_inc(key, 1)
                    act.wait_ge(keymin, done(c + 1))
                    act.wait_ge(scanned, done(2 * c - 2))
                    nc.scalar.activation(ek[:, ct % 2, :], km[:, ct % 2, :], ACT.Exp).then_inc(expk, 1)
                    for l in range(LAYERS):
                        u = b * UNITS + ct * LAYERS + l
                        act.wait_ge(arg, done(u + 1))
                        act.wait_ge(summed, done(u - 1))
                        nc.scalar.activation(eu[:, l, :], ua[:, l, :], ACT.Exp).then_inc(expu, 1)

        @block.gpsimd
        def _(pool):
            pool.sem_inc(expkv, LEAD)
            pool.sem_inc(expuv, LEAD)
            for n in range(B * UNITS):
                last = nc.gpsimd.tensor_scalar(diag[:, n, :], S["ident"][:], S["decay"][:, n:n + 1], None, ALU.mult)
            last.then_inc(diag_done, 1)
            with pool.Fori(0, B) as b:
                for ct in range(CT):
                    c = b * CT + ct
                    pool.wait_ge(scanned, done(2 * c - 2))
                    pool.wait_ge(expk, done(c + 1))
                    nc.gpsimd.tensor_tensor(ekv[:, ct % 2, :], ek[:, ct % 2, :], kt[:, ct % 2, :], ALU.mult).then_inc(expkv, 1)
                    for l in range(LAYERS):
                        u = b * UNITS + ct * LAYERS + l
                        pool.wait_ge(summed, done(u - 1))
                        pool.wait_ge(expu, done(u + 1))
                        nc.gpsimd.tensor_tensor(euv[:, l, :], eu[:, l, :], kt[:, ct % 2, :], ALU.mult).then_inc(expuv, 1)

        @block.vector
        def _(dve):
            for q in range(2):
                for l in range(2):
                    last = nc.vector.memset(bwd[q][l][:, T:T + 1], 0.0)
            last.then_inc(tails, 1)
            dve.sem_inc(keymin, LEAD)
            dve.sem_inc(arg, LEAD)
            dve.sem_inc(scanned, LEAD)
            dve.sem_inc(ratio, LEAD)
            with dve.Fori(0, B) as b:
                def ratios(n):
                    ct, l = n // LAYERS, n % LAYERS
                    u = b * UNITS + n
                    dve.wait_ge(summed, done(u + 1))
                    nc.vector.tensor_scalar(dmax[:], ps_q[1][l][:], 1e-8, None, ALU.max).then_inc(chain, 1)
                    dve.wait_ge(chain, u * 2 + 1)
                    nc.vector.reciprocal(rden[:], dmax[:]).then_inc(chain, 1)
                    dve.wait_ge(chain, u * 2 + 2)
                    nc.vector.tensor_tensor(S["ratio"][l][:, bass.ds(b * TT, TT), ct * P:(ct + 1) * P],
                                            ps_q[0][l][:].rearrange("p (n c) -> p n c", n=TT),
                                            rden[:].rearrange("p (n c) -> p n c", n=TT), ALU.mult).then_inc(ratio, 1)

                for ct in range(CT):
                    c = b * CT + ct
                    dve.wait_ge(key, done(c + 1))
                    dve.wait_ge(expk, done(c - 1))
                    nc.vector.tensor_scalar(km[:, ct % 2, :], kt[:, ct % 2, :], 30.0, None, ALU.min).then_inc(keymin, 1)
                    for l in range(LAYERS):
                        u = b * UNITS + ct * LAYERS + l
                        dve.wait_ge(expu, done(u - 1))
                        nc.vector.tensor_scalar(ua[:, l, :], kt[:, ct % 2, :], S["u"][:, l, ct:ct + 1], 30.0, ALU.add, ALU.min).then_inc(arg, 1)
                    for l in range(LAYERS):
                        n = ct * LAYERS + l
                        u = b * UNITS + n
                        dve.wait_ge(expkv, done(c + 1))
                        dve.wait_ge(summed, done(u - 1))
                        decay = S["decay"][:, bass.ds(u, 1)].to_broadcast([P, T])
                        for q, src in ((0, ekv), (1, ek)):
                            v = src[:, ct % 2, :]
                            nc.vector.tensor_tensor_scan(fwd[q][l][:], decay, v, 0.0, ALU.mult, ALU.add)
                            last = nc.vector.tensor_tensor_scan(bwd[q][l][:, 0:T][:, ::-1], decay, v[:, ::-1], 0.0, ALU.mult, ALU.add)
                        last.then_inc(scanned, 1)
                        if n:
                            ratios(n - 1)
                ratios(UNITS - 1)


def bitnet(nc, A, S):
    with ExitStack() as ctx:
        def sb(name, shape, dt):
            return ctx.enter_context(nc.sbuf_tensor(name, shape, dt))

        def sem(name):
            return ctx.enter_context(nc.semaphore(name))

        th = sb("f_tanh", [P, C], F32)
        o = sb("f_mixed", [P, 2, C], F32)
        q = sb("f_quant", [P, 2, C], BF16)
        qT = sb("f_quant_T", [P, 2, CT, P], BF16)
        fs = sb("f_scalars", [P, 2, 8], F32)
        sg = sb("silu", [P, 2, 512], F32)
        h = sb("hidden", [P, 2, 512], F32)
        sqj = sb("square_junk", [P, 512], BF16)
        hp = sb("hidden_ln", [P, 2, INNER], F32)
        ss = sb("square_sums", [P, 2, NCH], F32)
        mx = sb("chunk_max", [P, 2, NCH], F32)
        bs = sb("b_scalars", [P, 2, 8], F32)
        q2 = sb("b_quant", [P, INNER], BF16)
        q2T = sb("b_quant_T", [P, IT, P], BF16)

        def ps(name, shape, dt):
            return ctx.enter_context(nc.psum_tensor(name, shape, dt))

        ps_gate = [ps(f"ps_gate{i}", [P, 512], F32) for i in range(2)]
        ps_up = [ps(f"ps_up{i}", [P, 512], F32) for i in range(2)]
        ps_f = ps("ps_front_T", [P, 1024], BF16)
        ps_b = [ps(f"ps_back_T{i}", [P, 1024], BF16) for i in range(2)]
        ps_y = ps("ps_down", [P, 512], F32)

        tanh = sem("b_tanh")
        scaled = sem("b_scaled")
        to_done = sem("b_front_rounded")
        q_done = sem("b_front_quant")
        q_turned = sem("b_front_turned")
        qT_done = sem("b_front_T")
        gate_done = sem("b_gate")
        up_done = sem("b_up")
        silu_done = sem("b_silu")
        h_done = sem("b_hidden")
        sq_done = sem("b_squares")
        hp_done = sem("b_hidden_ln")
        var_done = sem("b_var")
        r_done = sem("b_rsqrt")
        bs_done = sem("b_back_scalars")
        t2_done = sem("b_back_rounded")
        q2_done = sem("b_back_quant")
        q2_turned = sem("b_back_turned")
        q2T_done = sem("b_back_T")
        down_done = sem("b_down")
        x_done = sem("b_x")
        chain = sem("b_chain")

        def steps(eng, step):
            step(0, 0, front=True, back=False)
            step(1, 1, front=True, back=True)
            with eng.Fori(1, TILES // 2 - 1) as ii:
                step(ii * 2, 0, front=True, back=True)
                step(ii * 2 + 1, 1, front=True, back=True)
            step(TILES - 2, 0, front=True, back=True)
            step(TILES - 1, 1, front=False, back=True)
            step(TILES, 0, front=False, back=True, mid=False)

        def col(ap, i):
            return ap[:, bass.ds(i, 1), :].rearrange("p a c -> p (a c)")

        block = ctx.enter_context(nc.Block())

        @block.tensor
        def _(pe):
            for s in (q_turned, gate_done, up_done, q2_turned, down_done):
                pe.sem_inc(s, LEAD)

            def turn_front(i, par):
                pe.wait_ge(q_done, done(i + 1))
                pe.wait_ge(qT_done, done(i))
                for k in range(CT):
                    last = nc.tensor.transpose(ps_f[:, k * P:(k + 1) * P], q[:, par, k * P:(k + 1) * P], S["identb"][:])
                last.then_inc(q_turned, 1)

            def step(i, par, front, back, mid=True):
                if mid:
                    pe.wait_ge(qT_done, done(i + 1))
                    for n in range(NCH):
                        g = i * NCH + n
                        pe.wait_ge(silu_done, done(g - 1))
                        for k in range(CT):
                            last = nc.tensor.matmul(ps_gate[n % 2][:], qT[:, par, k, :], S["wT"][0][:, k, n * 512:(n + 1) * 512],
                                                    start=(k == 0), stop=(k == CT - 1))
                        last.then_inc(gate_done, 1)
                        pe.wait_ge(h_done, done(g - 1))
                        for k in range(CT):
                            last = nc.tensor.matmul(ps_up[n % 2][:], qT[:, par, k, :], S["wT"][1][:, k, n * 512:(n + 1) * 512],
                                                    start=(k == 0), stop=(k == CT - 1))
                        last.then_inc(up_done, 1)
                if front:
                    turn_front(i + 1, 1 - par)
                if back:
                    j = i - 1
                    pe.wait_ge(q2_done, done(j + 1))
                    for hf in range(2):
                        pe.wait_ge(q2T_done, done(j * 2 + hf - 1))
                        for a in range(8):
                            k = hf * 8 + a
                            last = nc.tensor.transpose(ps_b[hf][:, a * P:(a + 1) * P], q2[:, k * P:(k + 1) * P], S["identb"][:])
                        last.then_inc(q2_turned, 1)
                    pe.wait_ge(x_done, done(j))
                    for k in range(IT):
                        if k % 8 == 0:
                            pe.wait_ge(q2T_done, done(j * 2 + k // 8 + 1))
                        last = nc.tensor.matmul(ps_y[:], q2T[:, k, :], S["wT"][2][:, k, :], start=(k == 0), stop=(k == IT - 1))
                    last.then_inc(down_done, 1)

            turn_front(0, 0)
            steps(pe, step)

        @block.scalar
        def _(act):
            for s in (tanh, to_done, qT_done, silu_done, sq_done, t2_done, q2T_done):
                act.sem_inc(s, LEAD)

            def front_tanh(i, par):
                act.wait_ge(scaled, done(i))
                nc.scalar.activation(th[:], col(S["x"], i), ACT.Tanh, scale=0.5).then_inc(tanh, 1)

            def front_round(i, par):
                act.wait_ge(scaled, done(i + 1))
                act.wait_ge(q_done, done(i - 1))
                nc.scalar.activation(o[:, par, :], o[:, par, :], ACT.Identity, scale=fs[:, par, 3:4],
                                     bias=S["round"][:, 0:1]).then_inc(to_done, 1)

            def front_copy(i, par):
                act.wait_ge(q_turned, done(i + 1))
                act.wait_ge(up_done, done(i * NCH - NCH))
                nc.scalar.activation(qT[:, par, :, :].rearrange("p k t -> p (k t)"), ps_f[:, 0:512], ACT.Copy).then_inc(qT_done, 1)

            def step(i, par, front, back, mid=True):
                def chunk(n):
                    g = i * NCH + n
                    act.wait_ge(gate_done, done(g + 1))
                    act.wait_ge(h_done, done(g - 1))
                    nc.scalar.activation(sg[:, n % 2, :], ps_gate[n % 2][:], ACT.Silu, scale=fs[:, par, 4:5]).then_inc(silu_done, 1)

                def square(n):
                    g = i * NCH + n
                    act.wait_ge(h_done, done(g + 1))
                    act.wait_ge(sq_done, done(g))
                    nc.scalar.activation(sqj[:], h[:, n % 2, :], ACT.Square, accum_out=ss[:, par, n:n + 1]).then_inc(sq_done, 1)

                if front:
                    front_tanh(i + 1, 1 - par)
                if mid:
                    chunk(0)
                    chunk(1)
                    square(0)
                if front:
                    front_round(i + 1, 1 - par)
                if back:
                    j = i - 1
                    act.wait_ge(bs_done, done(j + 1))
                    nc.scalar.activation(hp[:, 1 - par, :], hp[:, 1 - par, :], ACT.Identity, scale=bs[:, 1 - par, 6:7],
                                         bias=S["round"][:, 0:1]).then_inc(t2_done, 1)
                if mid:
                    chunk(2)
                    square(1)
                    chunk(3)
                    square(2)
                    square(3)
                if front:
                    front_copy(i + 1, 1 - par)
                if back:
                    for hf in range(2):
                        act.wait_ge(q2_turned, done(j * 2 + hf + 1))
                        act.wait_ge(down_done, done(j))
                        nc.scalar.activation(q2T[:, hf * 8:hf * 8 + 8, :].rearrange("p k t -> p (k t)"), ps_b[hf][:], ACT.Copy).then_inc(q2T_done, 1)

            front_tanh(0, 0)
            front_round(0, 0)
            front_copy(0, 0)
            steps(act, step)

        @block.gpsimd
        def _(pool):
            pool.sem_inc(hp_done, LEAD)
            pool.sem_inc(r_done, LEAD)

            def step(i, par, front, back, mid=True):
                if not mid:
                    return
                for n in range(NCH):
                    g = i * NCH + n
                    pool.wait_ge(q2_done, done(i - 1))
                    pool.wait_ge(h_done, done(g + 1))
                    nc.gpsimd.tensor_tensor(hp[:, par, n * 512:(n + 1) * 512], h[:, n % 2, :],
                                            S["ln"][:, n * 512:(n + 1) * 512], ALU.mult).then_inc(hp_done, 1)
                pool.wait_ge(var_done, i + 1)
                nc.gpsimd.tensor_tensor(bs[:, par, 3:4], bs[:, par, 2:3], S["mhalf"][:, 0:1], ALU.pow).then_inc(r_done, 1)

            steps(pool, step)

        @block.vector
        def _(dve):
            for s in (scaled, q_done, h_done, bs_done, q2_done, x_done):
                dve.sem_inc(s, LEAD)
            FRONT, MID = 5, 4
            used = [0]

            def link(base, n, ins):
                ins.then_inc(chain, 1)
                dve.wait_ge(chain, base + n)

            def front_scale(i, par):
                base = i * FRONT + (i - 1) * MID if not isinstance(i, int) or i else 0
                dve.wait_ge(tanh, done(i + 1))
                dve.wait_ge(q_done, done(i - 1))
                link(base, 1, nc.vector.scalar_tensor_tensor(out=th[:], in0=th[:], scalar=1.0, in1=col(S["ratio"][0], i),
                                                             op0=ALU.add, op1=ALU.mult))
                link(base, 2, nc.vector.tensor_scalar(o[:, par, :], th[:], S["tfs"][:, bass.ds(i, 1)], None, ALU.mult))
                link(base, 3, nc.vector.tensor_reduce(fs[:, par, 0:1], o[:, par, :], AX.X, ALU.max, apply_absolute_value=True))
                link(base, 4, nc.vector.tensor_scalar(fs[:, par, 1:2], fs[:, par, 0:1], EPS, None, ALU.max))
                nc.vector.tensor_scalar(fs[:, par, 4:5], fs[:, par, 1:2], S["wscale"][:, 0:1], 1.0 / QP, ALU.mult, ALU.mult)
                nc.vector.tensor_scalar(fs[:, par, 5:6], fs[:, par, 1:2], S["wscale"][:, 1:2], 1.0 / QP, ALU.mult, ALU.mult)
                link(base, 5, nc.vector.reciprocal(fs[:, par, 2:3], fs[:, par, 1:2]))
                nc.vector.tensor_scalar(fs[:, par, 3:4], fs[:, par, 2:3], QP, None, ALU.mult).then_inc(scaled, 1)

            def front_quant(i, par):
                dve.wait_ge(to_done, done(i + 1))
                dve.wait_ge(q_turned, done(i - 1))
                nc.vector.tensor_scalar(q[:, par, :], o[:, par, :], -ROUND, QP, ALU.add, ALU.min).then_inc(q_done, 1)

            def step(i, par, front, back, mid=True):
                def chunk(n):
                    g = i * NCH + n
                    dve.wait_ge(silu_done, done(g + 1))
                    dve.wait_ge(up_done, done(g + 1))
                    dve.wait_ge(sq_done, done(g - 1))
                    dve.wait_ge(hp_done, done(g - 1))
                    nc.vector.scalar_tensor_tensor(out=h[:, n % 2, :], in0=ps_up[n % 2][:], scalar=fs[:, par, 5:6],
                                                   in1=sg[:, n % 2, :], op0=ALU.mult, op1=ALU.mult).then_inc(h_done, 1)

                def chunk_max(n):
                    dve.wait_ge(hp_done, done(i * NCH + n + 1))
                    return nc.vector.tensor_reduce(mx[:, par, n:n + 1], hp[:, par, n * 512:(n + 1) * 512], AX.X, ALU.max,
                                                   apply_absolute_value=True)

                if mid:
                    chunk(0)
                if front:
                    front_scale(i + 1, 1 - par)
                if mid:
                    chunk(1)
                    chunk_max(0)
                if back:
                    j = i - 1
                    dve.wait_ge(t2_done, done(j + 1))
                    dve.wait_ge(q2_turned, done(j * 2))
                    nc.vector.tensor_scalar(q2[:], hp[:, 1 - par, :], -ROUND, QP, ALU.add, ALU.min).then_inc(q2_done, 1)
                if front:
                    front_quant(i + 1, 1 - par)
                if mid:
                    chunk(2)
                    chunk_max(1)
                    chunk(3)
                    chunk_max(2)
                    base = (i + (2 if front else 1)) * FRONT + i * MID
                    link(base, 1, chunk_max(3))
                    nc.vector.tensor_reduce(bs[:, par, 1:2], mx[:, par, :], AX.X, ALU.max)
                    dve.wait_ge(sq_done, done(i * NCH + NCH))
                    link(base, 2, nc.vector.tensor_reduce(bs[:, par, 0:1], ss[:, par, :], AX.X, ALU.add))
                    nc.vector.tensor_scalar(bs[:, par, 2:3], bs[:, par, 0:1], 1.0 / INNER, RMS_EPS, ALU.mult, ALU.add).then_inc(var_done, 1)
                    dve.wait_ge(r_done, done(i + 1))
                    link(base, 3, nc.vector.tensor_scalar(bs[:, par, 4:5], bs[:, par, 1:2], bs[:, par, 3:4], EPS, ALU.mult, ALU.max))
                    nc.vector.tensor_scalar(bs[:, par, 7:8], bs[:, par, 4:5], S["wscale"][:, 2:3], 1.0 / QP, ALU.mult, ALU.mult)
                    link(base, 4, nc.vector.reciprocal(bs[:, par, 5:6], bs[:, par, 4:5]))
                    nc.vector.tensor_scalar(bs[:, par, 6:7], bs[:, par, 5:6], bs[:, par, 3:4], QP, ALU.mult, ALU.mult).then_inc(bs_done, 1)
                if back:
                    dve.wait_ge(down_done, done(j + 1))
                    nc.vector.scalar_tensor_tensor(out=col(S["x"], j), in0=ps_y[:], scalar=bs[:, 1 - par, 7:8],
                                                   in1=col(S["x"], j), op0=ALU.mult, op1=ALU.add).then_inc(x_done, 1)

            front_scale(0, 0)
            front_quant(0, 0)
            steps(dve, step)


def project(nc, A, S):
    with ExitStack() as ctx:
        def sb(name, shape, dt):
            return ctx.enter_context(nc.sbuf_tensor(name, shape, dt))

        def sem(name):
            return ctx.enter_context(nc.semaphore(name))

        th = sb("r_tanh", [P, 2, C], F32)
        t1 = sb("r_gated", [P, 2, C], F32)
        o = sb("r_mixed", [P, 2, C], F32)
        oT = sb("r_mixed_T", [P, 2, CT, P], F32)
        ps_o = [ctx.enter_context(nc.psum_tensor(f"ps_mixed_T{i}", [P, 512], F32)) for i in range(2)]
        ps_l = [ctx.enter_context(nc.psum_tensor(f"ps_logits{i}", [P, E], F32)) for i in range(2)]
        tanh = sem("r_tanh_done")
        gated = sem("r_gated_done")
        mixed = sem("r_mixed_done")
        turned = sem("r_turned")
        oT_done = sem("r_T_done")
        logits = sem("r_logits")
        lcopied = sem("r_logits_copied")
        stored = [sem(f"r_stored{i}") for i in range(2)]
        zeroed = sem("r_lists_zeroed")

        def pairs(eng, step):
            with eng.Fori(0, TILES // 2) as ii:
                step(ii * 2, 0, ii)
                step(ii * 2 + 1, 1, ii)

        def col(ap, i):
            return ap[:, bass.ds(i, 1), :].rearrange("p a c -> p (a c)")

        block = ctx.enter_context(nc.Block())

        @block.sync
        def _(sp):
            for s in stored:
                sp.sem_inc(s, 16)
            sp.dma_start(S["lists"].rearrange("(p a) b -> p (a b)", p=P), S["zrow"][:]).then_inc(zeroed, 16)

            def step(i, par, ii):
                sp.wait_ge(mixed, done(i + 1))
                sp.dma_start(S["rows"][bass.ds(i * P, P), :], o[:, par, :]).then_inc(stored[par], 16)

            pairs(sp, step)
            for s in stored:
                sp.wait_ge(s, 16 + 16 * (TILES // 2))
            sp.wait_ge(zeroed, 16)

        @block.scalar
        def _(act):
            act.sem_inc(tanh, LEAD)
            act.sem_inc(oT_done, LEAD)

            def step(i, par, ii):
                act.wait_ge(gated, done(i - 1))
                nc.scalar.activation(th[:, par, :], col(S["x"], i), ACT.Tanh, scale=0.5).then_inc(tanh, 1)
                act.wait_ge(turned, done(i + 1))
                act.wait_ge(logits, done(i - 1))
                nc.scalar.activation(oT[:, par, :, :].rearrange("p k t -> p (k t)"), ps_o[par][:], ACT.Copy).then_inc(oT_done, 1)

            pairs(act, step)

        @block.vector
        def _(dve):
            dve.sem_inc(gated, LEAD)
            dve.sem_inc(mixed, LEAD)
            dve.sem_inc(lcopied, LEAD)

            def step(i, par, ii):
                dve.wait_ge(tanh, done(i + 1))
                nc.vector.scalar_tensor_tensor(out=t1[:, par, :], in0=th[:, par, :], scalar=1.0, in1=col(S["ratio"][1], i),
                                               op0=ALU.add, op1=ALU.mult).then_inc(gated, 1)
                dve.wait_ge(gated, done(i + 1))
                dve.wait_ge(turned, done(i - 1))
                dve.wait_ge(stored[par], ii * 16 + 16)
                nc.vector.tensor_scalar(o[:, par, :], t1[:, par, :], S["tfs"][:, bass.ds(i, 1)], None, ALU.mult).then_inc(mixed, 1)
                dve.wait_ge(logits, done(i + 1))
                nc.vector.tensor_copy(col(S["logits"], i), ps_l[par][:]).then_inc(lcopied, 1)

            pairs(dve, step)

        @block.tensor
        def _(pe):
            pe.sem_inc(turned, LEAD)
            pe.sem_inc(logits, LEAD)

            def step(i, par, ii):
                pe.wait_ge(mixed, done(i + 1))
                pe.wait_ge(oT_done, done(i - 1))
                for k in range(CT):
                    last = nc.tensor.transpose(ps_o[par][:, k * P:(k + 1) * P], o[:, par, k * P:(k + 1) * P], S["ident"][:])
                last.then_inc(turned, 1)
                pe.wait_ge(oT_done, done(i + 1))
                pe.wait_ge(lcopied, done(i - 1))
                for k in range(CT):
                    last = nc.tensor.matmul(ps_l[par][:], oT[:, par, k, :], S["gate_wT"][:, k, :], start=(k == 0), stop=(k == CT - 1))
                last.then_inc(logits, 1)

            pairs(pe, step)


def route(nc, A, S):
    with ExitStack() as ctx:
        def sb(name, shape, dt):
            return ctx.enter_context(nc.sbuf_tensor(name, shape, dt))

        def sem(name):
            return ctx.enter_context(nc.semaphore(name))

        score = sb("score", [P, TILES, E], F32)
        top = sb("top", [P, TILES, 8], F32)
        topi = sb("top_index", [P, TILES, 8], U32)
        expert = sb("expert", [P, TILES, K], F32)
        hot = sb("one_hot", [P, TILES, K, E], F32)
        hot2 = sb("one_hot_times", [P, TILES, K, E], F32)
        chosen = sb("chosen", [P, TILES, E], F32)
        before = [sb(f"before{i}", [P, TILES, E], F32) for i in range(2)]
        rank = sb("rank", [P, TILES, E], F32)
        rank4 = sb("rank4", [P, TILES, K], F32)
        ranki = sb("rank_int", [P, TILES, K], I32)
        lowi = sb("rank_low", [P, TILES, K], I32)
        highi = sb("rank_high", [P, TILES, K], I32)
        lowf = sb("rank_low_f", [P, TILES, K], F32)
        highf = sb("rank_high_f", [P, TILES, K], F32)
        place = sb("place_f", [P, TILES, K], F32)
        placei = sb("place", [P, TILES, K], U32)
        slotf = sb("slot_f", [P, TILES, K], F32)
        lmax = sb("logit_max", [P, TILES], F32)
        shifted = sb("logit_shifted", [P, TILES, E], F32)
        ex = sb("logit_exp", [P, TILES, E], F32)
        z = sb("softmax_sum", [P, TILES], F32)
        rz = sb("softmax_rsum", [P, TILES], F32)
        prob = sb("prob", [P, TILES, E], F32)
        wsum = sb("chosen_sum", [P, TILES], F32)
        rwsum = sb("chosen_rsum", [P, TILES], F32)
        cnt = sb("count", [P, E], F32)
        cnti = sb("count_int", [P, E], I32)
        ntf = sb("tiles_f", [P, E], F32)
        onesr = sb("ones_row", [P, E], F32)
        cum = sb("tiles_until_f", [P, E], F32)
        base = sb("first_row", [P, E], F32)
        cmp_ = sb("tile_cmp", [1, LISTED, E], F32)
        cmp2 = sb("tile_cmp_n", [1, LISTED, E], F32)
        te = sb("tile_expert_f", [1, LISTED], F32)
        tstart = sb("tile_start_f", [1, LISTED], F32)
        tj = sb("tile_j_f", [1, LISTED], F32)
        tcol = sb("tile_col_f", [1, LISTED], F32)
        ps_r = ctx.enter_context(nc.psum_tensor("ps_rank", [P, TILES * E], F32))
        ps_c = ctx.enter_context(nc.psum_tensor("ps_count", [P, E], F32))

        tanh = sem("t_tanh")
        seq = sem("t_seq")
        prefix = sem("t_prefix")
        ranked = sem("t_ranked")
        shift = sem("t_shift")
        exped = sem("t_exp")
        placed = sem("t_placed")
        scattered = sem("t_scattered")
        listed = sem("t_listed")

        block = ctx.enter_context(nc.Block())

        @block.scalar
        def _(act):
            nc.scalar.activation(score[:], S["logits"][:], ACT.Tanh, scale=0.5).then_inc(tanh, 1)
            act.wait_ge(shift, 1)
            nc.scalar.activation(ex[:], shifted[:], ACT.Exp).then_inc(exped, 1)

        @block.tensor
        def _(pe):
            pe.wait_ge(prefix, 1)
            nc.tensor.matmul(ps_r[:], S["tri"][:], chosen[:].rearrange("p n e -> p (n e)"), start=True, stop=False)
            nc.tensor.matmul(ps_r[:], S["ones"][:], before[1][:].rearrange("p n e -> p (n e)"), start=False, stop=True)
            nc.tensor.matmul(ps_c[:], S["ones"][:], chosen[:, TILES - 1, :], start=True, stop=False)
            nc.tensor.matmul(ps_c[:], S["ones"][:], before[1][:, TILES - 1, :], start=False, stop=True).then_inc(ranked, 1)

        @block.vector
        def _(dve):
            count = [0]

            def link(ins):
                count[0] += 1
                ins.then_inc(seq, 1)
                dve.wait_ge(seq, count[0])

            v = nc.vector
            dve.wait_ge(tanh, 1)
            link(v.tensor_scalar(score[:], score[:], 0.5, 0.5, ALU.mult, ALU.add))
            for i in range(TILES):
                last = v.max(top[:, i, :], score[:, i, :])
            link(last)
            for i in range(TILES):
                last = v.max_index(topi[:, i, :], top[:, i, :], score[:, i, :])
            link(last)
            link(v.tensor_copy(expert[:], topi[:, :, 0:K]))
            for i in range(TILES):
                last = v.tensor_tensor(hot[:, i, :, :], S["iota_e"][:].unsqueeze(1).to_broadcast([P, K, E]),
                                       expert[:, i, :].unsqueeze(2).to_broadcast([P, K, E]), ALU.is_equal)
            link(last)
            link(v.tensor_reduce(chosen[:], hot[:].rearrange("p n k e -> p n e k"), AX.X, ALU.add))
            v.memset(before[0][:, 0, :], 0.0)
            link(v.tensor_copy(before[0][:, 1:TILES, :], chosen[:, 0:TILES - 1, :]))
            a = 0
            for d in (1, 2, 4, 8):
                v.tensor_copy(before[1 - a][:, 0:d, :], before[a][:, 0:d, :])
                link(v.tensor_tensor(before[1 - a][:, d:TILES, :], before[a][:, d:TILES, :], before[a][:, 0:TILES - d, :], ALU.add))
                a = 1 - a
            link(v.tensor_copy(before[1][:], before[0][:]))
            dve.sem_inc(prefix, 1)

            dve.wait_ge(ranked, 1)
            link(v.tensor_copy(rank[:].rearrange("p n e -> p (n e)"), ps_r[:]))
            link(v.tensor_copy(cnt[:], ps_c[:]))

            def pick(out, values):
                for i in range(TILES):
                    last = v.tensor_tensor(hot2[:, i, :, :], hot[:, i, :, :], values[:, i, :].unsqueeze(1).to_broadcast([P, K, E]), ALU.mult)
                link(last)
                link(v.tensor_reduce(out, hot2[:], AX.X, ALU.add))

            pick(rank4[:], rank)
            link(v.tensor_copy(ranki[:], rank4[:]))
            link(v.tensor_scalar(lowi[:], ranki[:], P - 1, 9, ALU.bitwise_and, ALU.logical_shift_left))
            link(v.tensor_scalar(highi[:], ranki[:], 7, None, ALU.logical_shift_right))
            link(v.tensor_copy(lowf[:], lowi[:]))
            link(v.tensor_copy(highf[:], highi[:]))
            link(v.scalar_tensor_tensor(out=place[:], in0=expert[:], scalar=float(JT), in1=lowf[:], op0=ALU.mult, op1=ALU.add))
            link(v.tensor_tensor(place[:], place[:], highf[:], ALU.add))
            v.tensor_copy(placei[:], place[:]).then_inc(placed, 1)
            link(v.tensor_reduce(lmax[:], S["logits"][:], AX.X, ALU.max))
            v.tensor_tensor(shifted[:], S["logits"][:], lmax[:].unsqueeze(2).to_broadcast([P, TILES, E]), ALU.subtract).then_inc(shift, 1)
            dve.wait_ge(exped, 1)
            link(v.tensor_reduce(z[:], ex[:], AX.X, ALU.add))
            link(v.reciprocal(rz[:], z[:]))
            link(v.tensor_tensor(prob[:], ex[:], rz[:].unsqueeze(2).to_broadcast([P, TILES, E]), ALU.mult))
            pick(S["weight"][:], prob)
            link(v.tensor_reduce(wsum[:], S["weight"][:], AX.X, ALU.add))
            link(v.reciprocal(rwsum[:], wsum[:]))
            link(v.tensor_tensor(S["weight"][:], S["weight"][:], rwsum[:].unsqueeze(2).to_broadcast([P, TILES, K]), ALU.mult))

            link(v.tensor_scalar(cnt[:], cnt[:], float(P - 1), None, ALU.add))
            link(v.tensor_copy(cnti[:], cnt[:]))
            link(v.tensor_scalar(cnti[:], cnti[:], 7, None, ALU.logical_shift_right))
            link(v.tensor_copy(ntf[:], cnti[:]))
            link(v.tensor_scalar(ntf[:], ntf[:], 1.0, None, ALU.max))
            link(v.memset(onesr[:], 1.0))
            link(v.tensor_tensor_scan(cum[:], onesr[:], ntf[:], 0.0, ALU.mult, ALU.add))
            link(v.tensor_copy(S["tiles_until"][:], cum[0:1, :]))
            link(v.tensor_tensor(base[:], cum[:], ntf[:], ALU.subtract))
            link(v.tensor_scalar(base[:], base[:], float(P), None, ALU.mult))
            link(v.tensor_tensor(rank[:], rank[:], base[:].unsqueeze(1).to_broadcast([P, TILES, E]), ALU.add))
            pick(slotf[:], rank)
            link(v.tensor_copy(S["slot"][:], slotf[:]))
            tb = S["iota_t"][0:1, :].unsqueeze(2).to_broadcast([1, LISTED, E])
            link(v.tensor_tensor(cmp_[:], cum[0:1, :].unsqueeze(1).to_broadcast([1, LISTED, E]), tb, ALU.is_le))
            link(v.tensor_tensor(cmp2[:], cmp_[:], ntf[0:1, :].unsqueeze(1).to_broadcast([1, LISTED, E]), ALU.mult))
            link(v.tensor_reduce(te[:], cmp_[:], AX.X, ALU.add))
            link(v.tensor_reduce(tstart[:], cmp2[:], AX.X, ALU.add))
            link(v.tensor_scalar(te[:], te[:], float(E - 1), None, ALU.min))
            link(v.tensor_tensor(tj[:], S["iota_t"][0:1, :], tstart[:], ALU.subtract))
            link(v.tensor_scalar(tj[:], tj[:], float(JT - 1), None, ALU.min))
            link(v.scalar_tensor_tensor(out=tcol[:], in0=te[:], scalar=float(JT), in1=tj[:], op0=ALU.mult, op1=ALU.add))
            link(v.tensor_copy(S["tile_expert"][:], te[:]))
            link(v.tensor_copy(S["tile_col"][:], tcol[:]))

        @block.gpsimd
        def _(pool):
            pool.wait_ge(placed, 1)
            for i in range(TILES):
                for k in range(K):
                    nc.gpsimd.indirect_dma_start(S["lists"], bass.IndirectOffsetOnAxis(placei[:, i, k:k + 1], 0),
                                                 S["token"][:, i:i + 1], None, bounds_check=P * 512 - 1).then_inc(scattered, 16)

        @block.sync
        def _(sp):
            sp.wait_ge(scattered, 16 * TILES * K)
            sp.dma_start(S["list"][:], S["lists"].rearrange("(p a) b -> p (a b)", p=P)).then_inc(listed, 16)
            sp.wait_ge(listed, 16)


def experts(nc, A, S):
    with ExitStack() as ctx:
        def sb(name, shape, dt):
            return ctx.enter_context(nc.sbuf_tensor(name, shape, dt))

        def ps(name, shape, dt):
            return ctx.enter_context(nc.psum_tensor(name, shape, dt))

        def sem(name):
            return ctx.enter_context(nc.semaphore(name))

        wg = sb("e_gate", [P, 2, CT, WIDE], F32)
        wu = sb("e_up", [P, 2, CT, WIDE], F32)
        wd = sb("e_down", [P, 2, 3, C], F32)
        idx = sb("e_index", [P, 2], U32)
        x = sb("e_rows", [P, 2, C], F32)
        xT = sb("e_rows_T", [P, 2, CT, P], F32)
        sg = sb("e_silu", [P, 2, WIDE], F32)
        a = sb("e_hidden", [P, 2, WIDE], F32)
        aT = sb("e_hidden_T", [P, 2, 3, P], F32)
        y = sb("e_out", [P, 2, C], F32)
        ps_x = ps("ps_rows_T", [P, 512], F32)
        ps_g = [ps(f"ps_e_gate{i}", [P, WIDE], F32) for i in range(2)]
        ps_u = [ps(f"ps_e_up{i}", [P, WIDE], F32) for i in range(2)]
        ps_a = ps("ps_hidden_T", [P, 3 * P], F32)
        ps_y = [ps(f"ps_e_out{i}", [P, C], F32) for i in range(2)]

        w_in = [sem(f"e_w_in{i}") for i in range(2)]
        weights = sem("e_weights")
        indexed = sem("e_indexed")
        gathered = [sem(f"e_gathered{i}") for i in range(2)]
        turned = sem("e_turned")
        xT_done = sem("e_rows_T_done")
        gate_done = sem("e_gate_done")
        up_done = sem("e_up_done")
        silu_done = sem("e_silu_done")
        a_done = sem("e_hidden_done")
        a_turned = sem("e_hidden_turned")
        aT_done = sem("e_hidden_T_done")
        down_done = sem("e_down_done")
        y_done = sem("e_out_done")
        stored = [sem(f"e_stored{i}") for i in range(2)]

        def steps(eng, step):
            step(0, 0, 0, nxt=True, prev=False)
            step(1, 1, 0, nxt=True, prev=True)
            with eng.Fori(1, LISTED // 2 - 1) as tt:
                step(tt * 2, 0, tt, nxt=True, prev=True)
                step(tt * 2 + 1, 1, tt, nxt=True, prev=True)
            step(LISTED - 2, 0, LISTED // 2 - 1, nxt=True, prev=True)
            step(LISTED - 1, 1, LISTED // 2 - 1, nxt=False, prev=True)
            step(LISTED, 0, LISTED // 2, nxt=False, prev=True, mid=False)

        def look(eng, table, t, top):
            return eng.value_load(table[0:1, bass.ds(t, 1)], min_val=0, max_val=top)

        block = ctx.enter_context(nc.Block())

        @block.sync
        def _(sp):
            LOADS = 7

            def load(e, pair, slot):
                def w(dst, src):
                    sp.dma_start(dst, src).then_inc(w_in[slot], 16)

                def rows(ap, i):
                    return ap[bass.ds(i, 1), :, :].rearrange("a (k p) n -> p (a k) n", p=P)

                w(wg[:, slot, :, 0:LARGE], rows(A["L1_ffn_Wg"], e))
                w(wg[:, slot, :, LARGE:WIDE], rows(A["L1_ffn_cWg"], pair))
                w(wu[:, slot, :, 0:LARGE], rows(A["L1_ffn_Wu"], e))
                w(wu[:, slot, :, LARGE:WIDE], rows(A["L1_ffn_cWu"], pair))
                down = A["L1_ffn_Wd"][bass.ds(e, 1), :, :].rearrange("a i n -> (a i) n")
                w(wd[:, slot, 0, :], down[0:P, :])
                w(wd[0:LARGE - P, slot, 2, :], down[P:LARGE, :])
                w(wd[:, slot, 1, :], A["L1_ffn_cWd"][bass.ds(pair, 1), :, :].rearrange("a i n -> (a i) n"))
                sp.wait_ge(w_in[slot], pair * (16 * LOADS) + 16 * LOADS)
                sp.sem_inc(weights, 1)

            load(0, 0, 0)
            load(1, 0, 1)
            with sp.Fori(1, E // 2) as pair:
                for slot in range(2):
                    e = pair * 2 + slot
                    sp.wait_ge(down_done, done(look(sp, S["tiles_until"], e - 2, LISTED)))
                    load(e, pair, slot)

        @block.gpsimd
        def _(pool):
            pool.sem_inc(indexed, LEAD)

            def gather(t, par, tt):
                c = look(pool, S["tile_col"], t, E * JT - 1)
                if not isinstance(t, int) or t >= 2:
                    pool.wait_ge(turned, done(t - 1))
                nc.gpsimd.tensor_copy(idx[:, par:par + 1], S["list"][:, bass.ds(c, 1)]).then_inc(indexed, 1)
                pool.wait_ge(indexed, done(t + 1))
                pool.sem_inc(copied, 1)
                nc.gpsimd.indirect_dma_start(x[:, par, :], None, S["rows"], bass.IndirectOffsetOnAxis(idx[:, par:par + 1], 0),
                                             bounds_check=TOKENS - 1).then_inc(gathered[par], 16)

            copied = sem("e_index_ready")
            gather(0, 0, 0)
            gather(1, 1, 0)
            with pool.Fori(1, LISTED // 2) as tt:
                gather(tt * 2, 0, tt)
                gather(tt * 2 + 1, 1, tt)

        @block.tensor
        def _(pe):
            for s in (turned, gate_done, up_done, a_turned, down_done):
                pe.sem_inc(s, LEAD)

            def turn(t, par, tt):
                pe.wait_ge(gathered[par], tt * 16 + 16)
                pe.wait_ge(xT_done, done(t))
                for k in range(CT):
                    last = nc.tensor.transpose(ps_x[:, k * P:(k + 1) * P], x[:, par, k * P:(k + 1) * P], S["ident"][:])
                last.then_inc(turned, 1)

            def slot_of(e):
                return e % 2

            def step(t, par, tt, nxt, prev, mid=True):
                if nxt:
                    turn(t + 1, 1 - par, tt + par)
                if mid:
                    e = look(pe, S["tile_expert"], t, E - 1)
                    slot = slot_of(e)
                    pe.wait_ge(weights, e + 1)
                    pe.wait_ge(xT_done, done(t + 1))
                    pe.wait_ge(silu_done, done(t - 1))
                    for k in range(CT):
                        last = nc.tensor.matmul(ps_g[par][:], xT[:, par, k, :],
                                                wg[:, bass.ds(slot, 1), k, :].rearrange("p a n -> p (a n)"),
                                                start=(k == 0), stop=(k == CT - 1))
                    last.then_inc(gate_done, 1)
                if prev:
                    pe.wait_ge(a_done, done(t))
                    pe.wait_ge(aT_done, done(t - 1))
                    nc.tensor.transpose(ps_a[:, 0:P], a[:, 1 - par, 0:P], S["ident"][:])
                    nc.tensor.transpose(ps_a[:, P:2 * P], a[:, 1 - par, LARGE:WIDE], S["ident"][:])
                    nc.tensor.transpose(ps_a[0:LARGE - P, 2 * P:3 * P], a[:, 1 - par, P:LARGE], S["ident"][:]).then_inc(a_turned, 1)
                if mid:
                    pe.wait_ge(a_done, done(t - 1))
                    for k in range(CT):
                        last = nc.tensor.matmul(ps_u[par][:], xT[:, par, k, :],
                                                wu[:, bass.ds(slot, 1), k, :].rearrange("p a n -> p (a n)"),
                                                start=(k == 0), stop=(k == CT - 1))
                    last.then_inc(up_done, 1)
                if prev:
                    slot = slot_of(look(pe, S["tile_expert"], t - 1, E - 1))
                    pe.wait_ge(aT_done, done(t))
                    pe.wait_ge(y_done, done(t - 2))
                    for k in range(3):
                        n = P if k < 2 else LARGE - P
                        last = nc.tensor.matmul(ps_y[1 - par][:], aT[0:n, 1 - par, k, :],
                                                wd[0:n, bass.ds(slot, 1), k, :].rearrange("p a n -> p (a n)"),
                                                start=(k == 0), stop=(k == 2))
                    last.then_inc(down_done, 1)

            turn(0, 0, 0)
            steps(pe, step)

        @block.scalar
        def _(act):
            for s in (xT_done, silu_done, y_done):
                act.sem_inc(s, LEAD)
            for s in stored:
                act.sem_inc(s, 16)

            def rows_T(t, par):
                act.wait_ge(turned, done(t + 1))
                act.wait_ge(up_done, done(t - 1))
                nc.scalar.activation(xT[:, par, :, :].rearrange("p k t -> p (k t)"), ps_x[:], ACT.Copy).then_inc(xT_done, 1)

            def step(t, par, tt, nxt, prev, mid=True):
                if nxt:
                    rows_T(t + 1, 1 - par)
                if mid:
                    act.wait_ge(gate_done, done(t + 1))
                    act.wait_ge(a_done, done(t - 1))
                    nc.scalar.activation(sg[:, par, :], ps_g[par][:], ACT.Silu).then_inc(silu_done, 1)
                if prev:
                    act.wait_ge(down_done, done(t))
                    act.wait_ge(stored[1 - par], (tt + par - 1) * 16 + 16)
                    nc.scalar.activation(y[:, 1 - par, :], ps_y[1 - par][:], ACT.Copy).then_inc(y_done, 1)
                    act.wait_ge(y_done, done(t))
                    act.dma_start(S["results"][bass.ds((t - 1) * P, P), :], y[:, 1 - par, :]).then_inc(stored[1 - par], 16)

            rows_T(0, 0)
            steps(act, step)
            for s in stored:
                act.wait_ge(s, 16 + 16 * (LISTED // 2))

        @block.vector
        def _(dve):
            dve.sem_inc(a_done, LEAD)
            dve.sem_inc(aT_done, LEAD)

            def step(t, par, tt, nxt, prev, mid=True):
                if prev:
                    dve.wait_ge(a_turned, done(t))
                    dve.wait_ge(down_done, done(t - 2))
                    nc.vector.tensor_copy(aT[:, 1 - par, 0:2, :].rearrange("p k t -> p (k t)"), ps_a[:, 0:2 * P])
                    nc.vector.tensor_copy(aT[0:LARGE - P, 1 - par, 2, :], ps_a[0:LARGE - P, 2 * P:3 * P]).then_inc(aT_done, 1)
                if mid:
                    dve.wait_ge(silu_done, done(t + 1))
                    dve.wait_ge(up_done, done(t + 1))
                    dve.wait_ge(a_turned, done(t - 1))
                    nc.vector.tensor_tensor(a[:, par, 0:LARGE], ps_u[par][:, 0:LARGE], sg[:, par, 0:LARGE], ALU.mult)
                    nc.vector.scalar_tensor_tensor(out=a[:, par, LARGE:WIDE], in0=ps_u[par][:, LARGE:WIDE], scalar=SMALL_SCALE,
                                                   in1=sg[:, par, LARGE:WIDE], op0=ALU.mult, op1=ALU.mult).then_inc(a_done, 1)

            steps(dve, step)


def combine(nc, A, S, out):
    with ExitStack() as ctx:
        def sb(name, shape, dt):
            return ctx.enter_context(nc.sbuf_tensor(name, shape, dt))

        def sem(name):
            return ctx.enter_context(nc.semaphore(name))

        DEPTH = 2
        row = [[sb(f"c_row{d}{k}", [P, C], F32) for k in range(K)] for d in range(DEPTH)]
        fetched = [[sem(f"c_fetched{d}{k}") for k in range(K)] for d in range(DEPTH)]
        added = sem("c_added")
        stored = sem("c_stored")
        flat = out.rearrange("b t c -> (b t) c")
        block = ctx.enter_context(nc.Block())

        @block.gpsimd
        def _(pool):
            for i in range(TILES):
                if i >= DEPTH:
                    pool.wait_ge(added, K * (i - DEPTH + 1))
                for k in range(K):
                    nc.gpsimd.indirect_dma_start(row[i % DEPTH][k][:], None, S["results"],
                                                 bass.IndirectOffsetOnAxis(S["slot"][:, i, k:k + 1], 0),
                                                 bounds_check=LISTED * P - 1).then_inc(fetched[i % DEPTH][k], 16)

        @block.vector
        def _(dve):
            for i in range(TILES):
                for k in range(K):
                    dve.wait_ge(fetched[i % DEPTH][k], 16 * (i // DEPTH + 1))
                    if k:
                        dve.wait_ge(added, K * i + k)
                    nc.vector.scalar_tensor_tensor(out=S["x"][:, i, :], in0=row[i % DEPTH][k][:], scalar=S["weight"][:, i, k:k + 1],
                                                   in1=S["x"][:, i, :], op0=ALU.mult, op1=ALU.add).then_inc(added, 1)

        @block.sync
        def _(sp):
            for i in range(TILES):
                sp.wait_ge(added, K * (i + 1))
                sp.dma_start(flat[i * P:(i + 1) * P, :], S["x"][:, i, :]).then_inc(stored, 16)
            sp.wait_ge(stored, 16 * TILES)


def program(nc, A, out):
    with ExitStack() as ctx:
        S = {}

        def keep(stack, name, shape, dt):
            S[name] = stack.enter_context(nc.sbuf_tensor("s_" + name, shape, dt))

        S["lists"] = nc.dram_tensor("lists", [P * 512, 1], U32, kind="Internal").ap()
        S["rows"] = nc.dram_tensor("rows", [TOKENS, C], F32, kind="Internal").ap()
        S["results"] = nc.dram_tensor("results", [LISTED * P, C], F32, kind="Internal").ap()
        keep(ctx, "x", [P, TILES, C], F32)
        keep(ctx, "ident", [P, P], F32)
        keep(ctx, "identb", [P, P], BF16)
        keep(ctx, "tri", [P, P], F32)
        keep(ctx, "ones", [P, P], F32)
        keep(ctx, "round", [P, 1], F32)
        keep(ctx, "mhalf", [P, 1], F32)
        keep(ctx, "token", [P, TILES], U32)
        keep(ctx, "slot", [P, TILES, K], U32)
        keep(ctx, "weight", [P, TILES, K], F32)
        keep(ctx, "logits", [P, TILES, E], F32)
        keep(ctx, "list", [P, 512], U32)
        keep(ctx, "zrow", [P, 512], U32)
        keep(ctx, "tiles_until", [1, E], I32)
        keep(ctx, "tile_expert", [1, LISTED], I32)
        keep(ctx, "tile_col", [1, LISTED], I32)
        keep(ctx, "iota_e", [P, E], F32)
        keep(ctx, "iota_t", [P, LISTED], F32)
        keep(ctx, "gate_wT", [P, CT, E], F32)
        keep(ctx, "tfs", [P, TILES], F32)
        with ExitStack() as front:
            keep(front, "ratio1", [P, TILES, C], F32)
            with ExitStack() as layer0:
                keep(layer0, "ratio0", [P, TILES, C], F32)
                S["ratio"] = [S["ratio0"], S["ratio1"]]
                keep(layer0, "u", [P, LAYERS, CT], F32)
                keep(layer0, "decay", [P, B * UNITS], F32)
                setup(nc, A, S)
                mix(nc, A, S)
                keep(layer0, "wscale", [P, 3], F32)
                keep(layer0, "ln", [P, INNER], F32)
                S["wT"] = [layer0.enter_context(nc.sbuf_tensor(f"s_wT{m}", shape, BF16))
                           for m, shape in enumerate(([P, CT, INNER], [P, CT, INNER], [P, IT, C]))]
                ternary(nc, A, S)
                bitnet(nc, A, S)
            project(nc, A, S)
        route(nc, A, S)
        experts(nc, A, S)
        combine(nc, A, S, out)


_INS = ["x", "fside_BxSxS_0", "cond_512", "L0_cond_w", "L0_cond_u", "L0_ffn_w_gate", "L0_ffn_w_up", "L0_ffn_w_down",
        "L0_ffn_ln_weight", "L1_cond_w", "L1_cond_u", "L1_ffn_gate_w", "L1_ffn_Wg", "L1_ffn_Wu", "L1_ffn_Wd",
        "L1_ffn_cWg", "L1_ffn_cWu", "L1_ffn_cWd"]


def kernel(**inputs):
    import concourse.bacc as _bacc
    from concourse.bass_utils import run_bass_kernel_spmd as _run

    nc = _bacc.Bacc("TRN2", target_bir_lowering=False, num_devices=1)
    arrays, A = {}, {}
    for name in _INS:
        v = np.ascontiguousarray(inputs[name])
        arrays[f"in_{name}"] = v
        A[name] = nc.dram_tensor(f"in_{name}", v.shape, mybir.dt.from_np(v.dtype), kind="ExternalInput").ap()
    out = nc.dram_tensor("out_0", (B, T, C), F32, kind="ExternalOutput").ap()
    program(nc, A, out)
    r = _run(nc, [arrays], core_ids=[0])
    return r.results[0]["out_0"]
```

```python
from contextlib import ExitStack

import numpy as np

import concourse.bass as bass
from concourse import mybir

F32 = mybir.dt.float32
F32R = mybir.dt.float32r
BF16 = mybir.dt.bfloat16
I32 = mybir.dt.int32
U32 = mybir.dt.uint32
ALU = mybir.AluOpType
ACT = mybir.ActivationFunctionType
AX = mybir.AxisListType

P = 128
B, T, C = 4, 512, 512
TOKENS = B * T
TILES = TOKENS // P
TT = T // P
CT = C // P
LAYERS = 2
UNITS = CT * LAYERS
INNER = 2048
IT = INNER // P
NCH = INNER // 512
EPS = 1e-5
RMS_EPS = 1e-6
QP = 127.0
ROUND = 12582912.0
E = 32
K = 4
LARGE, SMALL = 192, 128
WIDE = LARGE + SMALL
SMALL_SCALE = 0.05
LISTED = TOKENS * K // P + E
TABLE = LISTED + 2
JT = TOKENS // P
LEAD = 4


def done(n):
    return n + LEAD


def setup(nc, A, S):
    with ExitStack() as ctx:
        def sb(name, shape, dt):
            return ctx.enter_context(nc.sbuf_tensor(name, shape, dt))

        def sem(name):
            return ctx.enter_context(nc.semaphore(name))

        condT = sb("cond_T", [P, B], F32)
        wdec = sb("decay_w", [P, LAYERS, CT], F32)
        time = sb("time_gate", [P, B], F32)
        half = sb("time_half", [P, B], F32)
        gate_rows = sb("gate_rows", [E, C], F32)
        ps_t = ctx.enter_context(nc.psum_tensor("ps_time", [P, B], F32))
        ps_g = ctx.enter_context(nc.psum_tensor("ps_gate_w", [P, CT * E], F32))

        small_in = sem("p_small_in")
        u_in = sem("p_u_in")
        zeroed = sem("p_zeroed")
        consts = sem("p_consts")
        exp_w = sem("p_exp_w")
        decay0 = sem("p_decay0")
        tsum = sem("p_time_sum")
        ttanh = sem("p_time_tanh")
        gturned = sem("p_gate_turned")
        dve_seq = sem("p_dve_seq")
        block = ctx.enter_context(nc.Block())

        @block.sync
        def _(sp):
            with nc.allow_non_contiguous_dma("a few hundred small vectors' elements"):
                sp.dma_start(condT[:], A["cond_512"].rearrange("b k -> k b")).then_inc(small_in, 16)
                for l in range(LAYERS):
                    sp.dma_start(wdec[:, l, :], A[f"L{l}_cond_w"].rearrange("(c p) -> p c", p=P)).then_inc(small_in, 16)
                    sp.dma_start(S["u"][:, l, :], A[f"L{l}_cond_u"].rearrange("(c p) -> p c", p=P)).then_inc(u_in, 16)
            sp.dma_start(gate_rows[:], A["L1_ffn_gate_w"]).then_inc(small_in, 16)
            sp.wait_ge(u_in, 32)

        @block.gpsimd
        def _(pool):
            nc.gpsimd.memset(S["ident"][:], 0.0)
            nc.gpsimd.memset(S["identb"][:], 0.0)
            nc.gpsimd.memset(S["tri"][:], 1.0)
            nc.gpsimd.memset(S["ones"][:], 1.0)
            nc.gpsimd.memset(S["round"][:], ROUND)
            nc.gpsimd.memset(S["two"][:], 2.0)
            nc.gpsimd.memset(S["zrow"][:], 0)
            nc.gpsimd.memset(S["mhalf"][:], -0.5).then_inc(zeroed, 1)
            pool.wait_ge(zeroed, 1)
            for m in (S["ident"], S["identb"]):
                nc.gpsimd.affine_select(out=m[:], in_=m[:], compare_op=ALU.not_equal, fill=1.0, base=0,
                                        pattern=[[-1, P]], channel_multiplier=1)
            nc.gpsimd.affine_select(out=S["tri"][:], in_=S["tri"][:], compare_op=ALU.is_gt, fill=0.0, base=0,
                                    pattern=[[1, P]], channel_multiplier=-1)
            nc.gpsimd.iota(S["token"][:], pattern=[[P, TILES]], base=0, channel_multiplier=1)
            nc.gpsimd.iota(S["iota_e"][:], pattern=[[1, E]], base=0, channel_multiplier=0, allow_small_or_imprecise_dtypes=True)
            nc.gpsimd.iota(S["iota_t"][:], pattern=[[1, TABLE]], base=0, channel_multiplier=0,
                           allow_small_or_imprecise_dtypes=True).then_inc(consts, 1)

        @block.scalar
        def _(act):
            act.wait_ge(small_in, 16 * 4)
            nc.scalar.activation(wdec[:], wdec[:], ACT.Exp).then_inc(exp_w, 1)
            act.wait_ge(exp_w, 1)
            nc.scalar.activation(wdec[:], wdec[:], ACT.Exp, scale=-1.0).then_inc(decay0, 1)
            act.wait_ge(tsum, 1)
            nc.scalar.activation(time[:], ps_t[:], ACT.Tanh, scale=0.5).then_inc(ttanh, 1)

        @block.vector
        def _(dve):
            seq = [0]

            def link(ins):
                seq[0] += 1
                ins.then_inc(dve_seq, 1)
                dve.wait_ge(dve_seq, seq[0])

            dve.wait_ge(ttanh, 1)
            link(nc.vector.tensor_scalar(time[:], time[:], 0.5, 0.5, ALU.mult, ALU.add))
            link(nc.vector.tensor_scalar(half[:], time[:], 0.5, 0.5, ALU.mult, ALU.add))
            for b in range(B):
                nc.vector.tensor_scalar(S["tfs"][:, b * TT:(b + 1) * TT], time[:, b:b + 1].to_broadcast([P, TT]), 0.1, 0.4,
                                        ALU.mult, ALU.add)
            dve.wait_ge(decay0, 1)
            for b in range(B):
                nc.vector.tensor_scalar(S["decay"][:, b * UNITS:(b + 1) * UNITS].rearrange("p (c l) -> p l c", l=LAYERS),
                                        wdec[:], half[:, b:b + 1], None, ALU.mult)
            dve.wait_ge(gturned, 1)
            nc.vector.tensor_copy(S["gate_wT"][:].rearrange("p k e -> p (k e)"), ps_g[:])

        @block.tensor
        def _(pe):
            pe.wait_ge(consts, 1)
            pe.wait_ge(small_in, 16 * 4)
            nc.tensor.matmul(ps_t[:], S["ones"][:], condT[:], start=True, stop=True).then_inc(tsum, 1)
            for k in range(CT):
                last = nc.tensor.transpose(ps_g[:, k * E:(k + 1) * E], gate_rows[:, k * P:(k + 1) * P], S["ident"][0:E, 0:E])
            last.then_inc(gturned, 1)


def ternary(nc, A, S):
    with ExitStack() as ctx:
        def sb(name, shape, dt):
            return ctx.enter_context(nc.sbuf_tensor(name, shape, dt))

        def sem(name):
            return ctx.enter_context(nc.semaphore(name))

        NW = 4
        QW = INNER * C // P // NW
        stage = sb("weight_stage", [P, NW * QW], F32)
        ws = [S["x"][:].rearrange("p a c -> p (a c)"), stage[:], S["x"][:].rearrange("p a c -> p (a c)")]
        wq = sb("weight_half", [P, 2 * QW], BF16)
        absum = sb("abs_sums", [P, 3, NW], F32)
        part = sb("abs_part", [P, 3], F32)
        rscale = sb("weight_rscale", [P, 3], F32)
        junk = sb("abs_junk", [P, QW], BF16)
        ps_sum = ctx.enter_context(nc.psum_tensor("ps_sum", [P, 4], F32))
        ps_t = [ctx.enter_context(nc.psum_tensor(f"ps_wt{i}", [P, 1024], BF16)) for i in range(2)]

        ln_in = sem("w_ln_in")
        up_in = sem("w_up_in")
        down_in = sem("w_down_in")
        abs_done = sem("w_abs_done")
        part_done = sem("w_part_done")
        sum_done = sem("w_sum_done")
        scale_done = sem("w_scale_done")
        dve_seq = sem("w_dve_seq")
        rounded = sem("w_rounded")
        ternary_done = sem("w_ternary")
        turned = sem("w_turned")
        copied = sem("w_copied")

        weights = [None,
                   A["L0_ffn_w_up"].rearrange("(n p) h -> p n h", p=P),
                   A["L0_ffn_w_down"].rearrange("(n p) i -> p n i", p=P)]
        block = ctx.enter_context(nc.Block())

        @block.sync
        def _(sp):
            sp.dma_start(ws[1].rearrange("p (n h) -> p n h", h=C), weights[1]).then_inc(up_in, 16)
            sp.dma_start(S["ln"][:], A["L0_ffn_ln_weight"].rearrange("(a i) -> a i", a=1).to_broadcast([P, INNER])).then_inc(ln_in, 16)
            sp.wait_ge(ternary_done, NW)
            sp.dma_start(ws[2].rearrange("p (n h) -> p n h", h=INNER), weights[2]).then_inc(down_in, 16)
            sp.wait_ge(ln_in, 16)

        def wait_weights(eng, m):
            if m:
                eng.wait_ge((up_in, down_in)[m - 1], 16)

        @block.scalar
        def _(act):
            for m in range(3):
                wait_weights(act, m)
                for c in range(NW - 1):
                    if m + c:
                        act.wait_ge(abs_done, m * (NW - 1) + c)
                    nc.scalar.activation(junk[:], ws[m][:, c * QW:(c + 1) * QW], ACT.Abs,
                                         accum_out=absum[:, m, c:c + 1]).then_inc(abs_done, 1)
                act.wait_ge(scale_done, m + 1)
                for c in range(NW):
                    v = ws[m][:, c * QW:(c + 1) * QW]
                    nc.scalar.activation(v, v, ACT.Identity, scale=rscale[:, m:m + 1], bias=S["round"][:, 0:1]).then_inc(rounded, 1)

        @block.vector
        def _(dve):
            seq = [0]

            def link(ins):
                seq[0] += 1
                ins.then_inc(dve_seq, 1)
                dve.wait_ge(dve_seq, seq[0])

            for m in range(3):
                wait_weights(dve, m)
                link(nc.vector.tensor_reduce(absum[:, m, NW - 1:NW], ws[m][:, (NW - 1) * QW:NW * QW], AX.X, ALU.add,
                                             apply_absolute_value=True))
                dve.wait_ge(abs_done, (m + 1) * (NW - 1))
                nc.vector.tensor_reduce(part[:, m:m + 1], absum[:, m, :], AX.X, ALU.add).then_inc(part_done, 1)
                dve.wait_ge(sum_done, m + 1)
                link(nc.vector.tensor_scalar(S["wscale"][:, m:m + 1], ps_sum[:, m:m + 1], 1.0 / (INNER * C), EPS,
                                             ALU.mult, ALU.max))
                nc.vector.reciprocal(rscale[:, m:m + 1], S["wscale"][:, m:m + 1]).then_inc(scale_done, 1)
                for c in range(NW):
                    dve.wait_ge(rounded, m * NW + c + 1)
                    if c % 2 == 0 and m + c:
                        dve.wait_ge(turned, 8 * m + 2 * c)
                    q = wq[:, (c % 2) * QW:(c % 2 + 1) * QW]
                    link(nc.vector.tensor_scalar(q, ws[m][:, c * QW:(c + 1) * QW], -ROUND, 1.0, ALU.add, ALU.min))
                    nc.vector.tensor_scalar(q, q, -1.0, None, ALU.max).then_inc(ternary_done, 1)
                    if c % 2:
                        for g in range(c // 2 * 4, c // 2 * 4 + 4):
                            dve.wait_ge(turned, 8 * m + g + 1)
                            if m < 2:
                                out = S["wT"][m][:, g % 4, (g // 4) * 1024:(g // 4 + 1) * 1024]
                                src = ps_t[g % 2][:]
                            else:
                                out = S["wT"][m][:, (g % 2) * 8:(g % 2 + 1) * 8, (g // 2) * P:(g // 2 + 1) * P]
                                src = ps_t[g % 2][:].rearrange("p (k o) -> p k o", o=P)
                            nc.vector.tensor_copy(out, src).then_inc(copied, 1)

        @block.tensor
        def _(pe):
            for m in range(3):
                pe.wait_ge(part_done, m + 1)
                nc.tensor.matmul(ps_sum[:, m:m + 1], S["ones"][:], part[:, m:m + 1], start=True, stop=True).then_inc(sum_done, 1)
                for g in range(8):
                    if g % 4 == 0:
                        pe.wait_ge(ternary_done, NW * m + g // 2 + 2)
                    if 8 * m + g >= 2:
                        pe.wait_ge(copied, 8 * m + g - 1)
                    for a in range(8):
                        if m < 2:
                            src = wq[:, a * C + (g % 4) * P:a * C + (g % 4 + 1) * P]
                        else:
                            k = (g % 2) * 8 + a
                            src = wq[:, (g // 2 % 2) * INNER + k * P:(g // 2 % 2) * INNER + (k + 1) * P]
                        last = nc.tensor.transpose(ps_t[g % 2][:, a * P:(a + 1) * P], src, S["identb"][:])
                    last.then_inc(turned, 1)


def mix(nc, A, S):
    with ExitStack() as ctx:
        def sb(name, shape, dt):
            return ctx.enter_context(nc.sbuf_tensor(name, shape, dt))

        def sem(name):
            return ctx.enter_context(nc.semaphore(name))

        side = sb("side", [P, TT, C], F32)
        kt = sb("key", [P, 2, T], F32)
        km = sb("key_min", [P, 2, T], F32)
        ek = sb("exp_key", [P, 2, T], F32)
        ekv = sb("exp_key_value", [P, 2, T], F32)
        ua = sb("bonus_arg", [P, 2, T], F32)
        eu = sb("exp_bonus", [P, 2, T], F32)
        euv = sb("exp_bonus_value", [P, 2, T], F32)
        fwd = [[sb(f"forward{q}{l}", [P, T], F32) for l in range(2)] for q in range(2)]
        bwd = [[sb(f"backward{q}{l}", [P, T + 1], F32) for l in range(2)] for q in range(2)]
        dmax = sb("den_max", [P, 2, T], F32)
        guess = sb("den_reciprocal_guess", [P, 2, T], F32)
        rem = sb("den_times_guess", [P, T], F32)
        corr = sb("guess_correction", [P, T], F32)
        num = sb("numerator", [P, 2, T], F32)
        rden = sb("den_reciprocal", [P, 2, T], F32)
        diag = sb("decay_diagonals", [P, 2, P], F32)
        ps_k = [ctx.enter_context(nc.psum_tensor(f"ps_key{i}", [P, T], F32)) for i in range(2)]
        ps_q = [[ctx.enter_context(nc.psum_tensor(f"ps_sum{q}{l}", [P, T], F32)) for l in range(2)] for q in range(2)]

        side_in = sem("m_side_in")
        turned = sem("m_turned")
        key = sem("m_key")
        keymin = sem("m_keymin")
        expk = sem("m_expk")
        expkv = sem("m_expkv")
        arg = sem("m_arg")
        expu = sem("m_expu")
        expuv = sem("m_expuv")
        scanned = sem("m_scanned")
        summed = sem("m_summed")
        ratio = sem("m_ratio")
        tails = sem("m_tails")
        maxed = sem("m_den_max")
        logged = sem("m_den_log")
        guessed = sem("m_guess")
        timed = sem("m_den_times_guess")
        corrected = sem("m_corrected")
        num_out = sem("m_num_out")
        weights_in = sem("m_weights_in")
        refined = sem("m_refined")

        def batches(eng, unit_pair):
            for ct in range(CT):
                unit_pair(0, ct, first=(ct == 0))
            with eng.Fori(1, B - 1) as b:
                for ct in range(CT):
                    unit_pair(b, ct)
            for ct in range(CT):
                unit_pair(B - 1, ct, last=ct)

        block = ctx.enter_context(nc.Block())

        @block.sync
        def _(sp):
            with sp.Fori(0, B) as b:
                sp.wait_ge(turned, done(b * CT))
                sp.dma_start(side[:], A["fside_BxSxS_0"][bass.ds(b, 1), :, :].rearrange("b (n p) c -> p (b n) c", p=P)).then_inc(side_in, 16)
            sp.dma_start(S["x"][:].rearrange("p a c -> p (a c)").rearrange("p (n h) -> p n h", h=C),
                         A["L0_ffn_w_gate"].rearrange("(n p) h -> p n h", p=P)).then_inc(weights_in, 16)
            sp.wait_ge(weights_in, 16)

        @block.tensor
        def _(pe):
            pe.sem_inc(turned, LEAD)
            pe.sem_inc(summed, LEAD)
            pe.wait_ge(tails, 1)

            def turn(b, ct):
                if ct == 0:
                    pe.wait_ge(side_in, b * 16 + 16)
                pe.wait_ge(key, done(b * CT + ct - 1))
                for tt in range(TT):
                    last = nc.tensor.transpose(ps_k[ct % 2][:, tt * P:(tt + 1) * P], side[:, tt, ct * P:(ct + 1) * P], S["ident"][:])
                last.then_inc(turned, 1)

            def unit_pair(b, ct, first=False, last=None):
                for l in range(LAYERS):
                    u = b * UNITS + ct * LAYERS + l
                    pe.wait_ge(scanned, done(u + 1))
                    pe.wait_ge(expuv, done(u + 1))
                    pe.wait_ge(maxed, done(u - 1))
                    pe.wait_ge(num_out, done(u - 1))
                    for q, extra in ((1, eu), (0, euv)):
                        for tt in range(TT):
                            out = ps_q[q][l][:, tt * P:(tt + 1) * P]
                            at = slice(tt * P, (tt + 1) * P)
                            nc.tensor.matmul(out, fwd[q][l][:, at], S["ident"][:], start=True, stop=False)
                            nc.tensor.matmul(out, bwd[q][l][:, tt * P + 1:(tt + 1) * P + 1], diag[:, l, :], start=False, stop=False)
                            done_ = nc.tensor.matmul(out, extra[:, l, at], S["ident"][:], start=False, stop=True)
                    done_.then_inc(summed, 1)
                    if l == 0 and (last is None or last < CT - 2):
                        turn(b + (ct + 2) // CT, (ct + 2) % CT)

            turn(0, 0)
            turn(0, 1)
            batches(pe, unit_pair)

        @block.scalar
        def _(act):
            nc.scalar.preload_act_table_set("natural_log_exp_and_others")
            for s in (key, expk, expu, guessed, logged, corrected, num_out):
                act.sem_inc(s, LEAD)

            def key_out(c, par):
                act.wait_ge(turned, done(c + 1))
                act.wait_ge(expuv, done(2 * c - 2))
                nc.scalar.activation(kt[:, par, :], ps_k[par][:], ACT.Copy).then_inc(key, 1)

            def exp_key(c, par):
                act.wait_ge(keymin, done(c + 1))
                act.wait_ge(scanned, done(2 * c - 2))
                nc.scalar.activation(ek[:, par, :], km[:, par, :], ACT.Exp).then_inc(expk, 1)

            def guess_of(u, l):
                act.wait_ge(maxed, done(u + 1))
                act.wait_ge(refined, done(u - 1))
                nc.scalar.activation(guess[:, l, :], dmax[:, l, :], ACT.Ln).then_inc(logged, 1)
                act.wait_ge(logged, done(u + 1))
                nc.scalar.activation(guess[:, l, :], guess[:, l, :], ACT.Exp, scale=-1.0).then_inc(guessed, 1)
                act.wait_ge(summed, done(u + 1))
                act.wait_ge(ratio, done(u - 1))
                nc.scalar.activation(num[:, l, :], ps_q[0][l][:], ACT.Copy).then_inc(num_out, 1)
                act.wait_ge(timed, done(u + 1))
                act.wait_ge(refined, done(u))
                nc.scalar.activation(corr[:], rem[:], ACT.Identity, scale=-1.0, bias=S["two"][:, 0:1]).then_inc(corrected, 1)

            def unit_pair(b, ct, first=False, last=None):
                c = b * CT + ct
                for l in range(LAYERS):
                    u = c * LAYERS + l
                    if last != CT - 1:
                        if l == 0:
                            key_out(c + 1, (ct + 1) % 2)
                        else:
                            exp_key(c + 1, (ct + 1) % 2)
                    act.wait_ge(arg, done(u + 1))
                    act.wait_ge(summed, done(u - 1))
                    nc.scalar.activation(eu[:, l, :], ua[:, l, :], ACT.Exp).then_inc(expu, 1)
                    if not first:
                        guess_of(u - 2, l)

            key_out(0, 0)
            exp_key(0, 0)
            batches(act, unit_pair)
            guess_of(B * UNITS - 2, 0)
            guess_of(B * UNITS - 1, 1)

        @block.gpsimd
        def _(pool):
            for s in (expkv, expuv, refined, timed):
                pool.sem_inc(s, LEAD)

            def exp_key_value(c, par):
                pool.wait_ge(scanned, done(2 * c - 2))
                pool.wait_ge(expk, done(c + 1))
                nc.gpsimd.tensor_tensor(ekv[:, par, :], ek[:, par, :], kt[:, par, :], ALU.mult).then_inc(expkv, 1)

            def refine(u, l):
                pool.wait_ge(corrected, done(u))
                pool.wait_ge(guessed, done(u + 1))
                nc.gpsimd.tensor_tensor(rem[:], dmax[:, l, :], guess[:, l, :], ALU.mult).then_inc(timed, 1)
                pool.wait_ge(corrected, done(u + 1))
                pool.wait_ge(ratio, done(u - 1))
                nc.gpsimd.tensor_tensor(rden[:, l, :], corr[:], guess[:, l, :], ALU.mult).then_inc(refined, 1)

            def unit_pair(b, ct, first=False, last=None):
                c = b * CT + ct
                for l in range(LAYERS):
                    u = c * LAYERS + l
                    if l == 1 and last != CT - 1:
                        exp_key_value(c + 1, (ct + 1) % 2)
                    pool.wait_ge(summed, done(u - 1))
                    nc.gpsimd.tensor_tensor(diag[:, l, :], S["ident"][:], S["decay"][:, bass.ds(u, 1)].to_broadcast([P, P]), ALU.mult)
                    pool.wait_ge(expu, done(u + 1))
                    nc.gpsimd.tensor_tensor(euv[:, l, :], eu[:, l, :], kt[:, ct % 2, :], ALU.mult).then_inc(expuv, 1)
                    if not first:
                        refine(u - 2, l)

            exp_key_value(0, 0)
            batches(pool, unit_pair)
            refine(B * UNITS - 2, 0)
            refine(B * UNITS - 1, 1)

        @block.vector
        def _(dve):
            for q in range(2):
                for l in range(2):
                    done_ = nc.vector.memset(bwd[q][l][:, T:T + 1], 0.0)
            done_.then_inc(tails, 1)
            for s in (keymin, arg, scanned, maxed, ratio):
                dve.sem_inc(s, LEAD)

            def key_min(c, par):
                dve.wait_ge(key, done(c + 1))
                dve.wait_ge(expk, done(c - 1))
                nc.vector.tensor_scalar(km[:, par, :], kt[:, par, :], 30.0, None, ALU.min).then_inc(keymin, 1)

            def bonus_args(c, ct):
                for l in range(LAYERS):
                    dve.wait_ge(expu, done(c * LAYERS + l - 1))
                    nc.vector.tensor_scalar(ua[:, l, :], kt[:, ct % 2, :], S["u"][:, l, ct:ct + 1], 30.0, ALU.add, ALU.min).then_inc(arg, 1)

            def den_max(u, l):
                dve.wait_ge(summed, done(u + 1))
                nc.vector.tensor_scalar(dmax[:, l, :], ps_q[1][l][:], 1e-8, None, ALU.max).then_inc(maxed, 1)

            def ratio_of(u, b, n):
                l, ct = n % LAYERS, n // LAYERS
                dve.wait_ge(refined, done(u + 1))
                dve.wait_ge(num_out, done(u + 1))
                nc.vector.tensor_tensor(S["ratio"][l][:, bass.ds(b * TT, TT), ct * P:(ct + 1) * P],
                                        rden[:, l, :].rearrange("p (n c) -> p n c", n=TT),
                                        num[:, l, :].rearrange("p (n c) -> p n c", n=TT), ALU.mult).then_inc(ratio, 1)

            def unit_pair(b, ct, first=False, last=None):
                c = b * CT + ct
                for l in range(LAYERS):
                    n = ct * LAYERS + l
                    u = b * UNITS + n
                    dve.wait_ge(expkv, done(c + 1))
                    dve.wait_ge(summed, done(u - 1))
                    decay = S["decay"][:, bass.ds(u, 1)].to_broadcast([P, T])
                    for q, src in ((0, ekv), (1, ek)):
                        v = src[:, ct % 2, :]
                        nc.vector.tensor_tensor_scan(fwd[q][l][:], decay, v, 0.0, ALU.mult, ALU.add)
                        done_ = nc.vector.tensor_tensor_scan(bwd[q][l][:, 0:T][:, ::-1], decay, v[:, ::-1], 0.0, ALU.mult, ALU.add)
                    done_.then_inc(scanned, 1)
                    if not isinstance(u, int) or u >= 3:
                        ratio_of(u - 3, b if n >= 3 else b - 1, (n - 3) % UNITS)
                    if not first or l:
                        den_max(u - 1, 1 - l)
                    if last != CT - 1:
                        if l == 0:
                            key_min(c + 1, (ct + 1) % 2)
                        else:
                            bonus_args(c + 1, (ct + 1) % CT)

            key_min(0, 0)
            bonus_args(0, 0)
            batches(dve, unit_pair)
            ratio_of(B * UNITS - 3, B - 1, UNITS - 3)
            den_max(B * UNITS - 1, 1)
            ratio_of(B * UNITS - 2, B - 1, UNITS - 2)
            ratio_of(B * UNITS - 1, B - 1, UNITS - 1)


def bitnet(nc, A, S):
    with ExitStack() as ctx:
        def sb(name, shape, dt):
            return ctx.enter_context(nc.sbuf_tensor(name, shape, dt))

        def sem(name):
            return ctx.enter_context(nc.semaphore(name))

        th = sb("f_tanh", [P, C], F32)
        o = sb("f_mixed", [P, 2, C], F32)
        q = sb("f_quant", [P, 2, C], BF16)
        qT = sb("f_quant_T", [P, 2, CT, P], BF16)
        fs = sb("f_scalars", [P, 2, 8], F32)
        sg = sb("silu", [P, 2, 512], F32)
        h = sb("hidden", [P, 2, 512], F32)
        sqj = sb("square_junk", [P, 512], BF16)
        hp = sb("hidden_ln", [P, 2, INNER], F32)
        ss = sb("square_sums", [P, 2, NCH], F32)
        mx = sb("chunk_max", [P, 2, NCH], F32)
        bs = sb("b_scalars", [P, 2, 8], F32)
        q2 = sb("b_quant", [P, INNER], BF16)
        q2T = sb("b_quant_T", [P, IT, P], BF16)

        def ps(name, shape, dt):
            return ctx.enter_context(nc.psum_tensor(name, shape, dt))

        ps_gate = [ps(f"ps_gate{i}", [P, 512], F32) for i in range(2)]
        ps_up = [ps(f"ps_up{i}", [P, 512], F32) for i in range(2)]
        ps_f = ps("ps_front_T", [P, 1024], BF16)
        ps_b = [ps(f"ps_back_T{i}", [P, 1024], BF16) for i in range(2)]
        ps_y = ps("ps_down", [P, 512], F32)

        x_first = sem("b_x_first")
        x_rest = sem("b_x_rest")
        tanh = sem("b_tanh")
        scaled = sem("b_scaled")
        to_done = sem("b_front_rounded")
        q_done = sem("b_front_quant")
        q_turned = sem("b_front_turned")
        qT_done = sem("b_front_T")
        gate_done = sem("b_gate")
        up_done = sem("b_up")
        silu_done = sem("b_silu")
        h_done = sem("b_hidden")
        sq_done = sem("b_squares")
        hp_done = sem("b_hidden_ln")
        var_done = sem("b_var")
        r_done = sem("b_rsqrt")
        bs_done = sem("b_back_scalars")
        t2_done = sem("b_back_rounded")
        q2_done = sem("b_back_quant")
        q2_turned = sem("b_back_turned")
        q2T_done = sem("b_back_T")
        down_done = sem("b_down")
        x_done = sem("b_x")
        chain = sem("b_chain")

        def steps(eng, step):
            step(0, 0, front=True, back=False)
            step(1, 1, front=True, back=True)
            with eng.Fori(1, TILES // 2 - 1) as ii:
                step(ii * 2, 0, front=True, back=True)
                step(ii * 2 + 1, 1, front=True, back=True)
            step(TILES - 2, 0, front=True, back=True)
            step(TILES - 1, 1, front=False, back=True)
            step(TILES, 0, front=False, back=True, mid=False)

        def col(ap, i):
            return ap[:, bass.ds(i, 1), :].rearrange("p a c -> p (a c)")

        block = ctx.enter_context(nc.Block())

        @block.sync
        def _(sp):
            rows = A["x"].rearrange("b (n p) c -> p (b n) c", p=P)
            sp.dma_start(S["x"][:, 0:2, :], rows[:, 0:2, :]).then_inc(x_first, 16)
            sp.dma_start(S["x"][:, 2:TILES, :], rows[:, 2:TILES, :]).then_inc(x_rest, 16)

        @block.tensor
        def _(pe):
            for s in (q_turned, gate_done, up_done, q2_turned, down_done):
                pe.sem_inc(s, LEAD)

            def turn_front(i, par):
                pe.wait_ge(q_done, done(i + 1))
                pe.wait_ge(qT_done, done(i))
                for k in range(CT):
                    last = nc.tensor.transpose(ps_f[:, k * P:(k + 1) * P], q[:, par, k * P:(k + 1) * P], S["identb"][:])
                last.then_inc(q_turned, 1)

            def step(i, par, front, back, mid=True):
                def chunk(n):
                    g = i * NCH + n
                    pe.wait_ge(silu_done, done(g - 1))
                    for k in range(CT):
                        last = nc.tensor.matmul(ps_gate[n % 2][:], qT[:, par, k, :], S["wT"][0][:, k, n * 512:(n + 1) * 512],
                                                start=(k == 0), stop=(k == CT - 1))
                    last.then_inc(gate_done, 1)
                    pe.wait_ge(h_done, done(g - 1))
                    for k in range(CT):
                        last = nc.tensor.matmul(ps_up[n % 2][:], qT[:, par, k, :], S["wT"][1][:, k, n * 512:(n + 1) * 512],
                                                start=(k == 0), stop=(k == CT - 1))
                    last.then_inc(up_done, 1)

                j = i - 1
                if mid:
                    pe.wait_ge(qT_done, done(i + 1))
                    chunk(0)
                    chunk(1)
                if back:
                    pe.wait_ge(q2_done, done(j + 1))
                    for hf in range(2):
                        pe.wait_ge(q2T_done, done(j * 2 + hf - 1))
                        for a in range(8):
                            k = hf * 8 + a
                            last = nc.tensor.transpose(ps_b[hf][:, a * P:(a + 1) * P], q2[:, k * P:(k + 1) * P], S["identb"][:])
                        last.then_inc(q2_turned, 1)
                if mid:
                    chunk(2)
                    chunk(3)
                if front:
                    turn_front(i + 1, 1 - par)
                if back:
                    pe.wait_ge(x_done, done(j))
                    for k in range(IT):
                        if k % 8 == 0:
                            pe.wait_ge(q2T_done, done(j * 2 + k // 8 + 1))
                        last = nc.tensor.matmul(ps_y[:], q2T[:, k, :], S["wT"][2][:, k, :], start=(k == 0), stop=(k == IT - 1))
                    last.then_inc(down_done, 1)

            turn_front(0, 0)
            steps(pe, step)

        @block.scalar
        def _(act):
            for s in (tanh, to_done, qT_done, silu_done, sq_done, t2_done, q2T_done):
                act.sem_inc(s, LEAD)

            def front_tanh(i, par):
                act.wait_ge(x_first if isinstance(i, int) and i < 2 else x_rest, 16)
                act.wait_ge(scaled, done(i))
                nc.scalar.activation(th[:], col(S["x"], i), ACT.Tanh, scale=0.5).then_inc(tanh, 1)

            def front_round(i, par):
                act.wait_ge(scaled, done(i + 1))
                act.wait_ge(q_done, done(i - 1))
                nc.scalar.activation(o[:, par, :], o[:, par, :], ACT.Identity, scale=fs[:, par, 3:4],
                                     bias=S["round"][:, 0:1]).then_inc(to_done, 1)

            def front_copy(i, par):
                act.wait_ge(q_turned, done(i + 1))
                act.wait_ge(up_done, done(i * NCH - NCH))
                nc.scalar.activation(qT[:, par, :, :].rearrange("p k t -> p (k t)"), ps_f[:, 0:512], ACT.Copy).then_inc(qT_done, 1)

            def step(i, par, front, back, mid=True):
                def chunk(n):
                    g = i * NCH + n
                    act.wait_ge(gate_done, done(g + 1))
                    act.wait_ge(h_done, done(g - 1))
                    nc.scalar.activation(sg[:, n % 2, :], ps_gate[n % 2][:], ACT.Silu, scale=fs[:, par, 4:5]).then_inc(silu_done, 1)

                def square(n):
                    g = i * NCH + n
                    act.wait_ge(h_done, done(g + 1))
                    act.wait_ge(sq_done, done(g))
                    nc.scalar.activation(sqj[:], h[:, n % 2, :], ACT.Square, accum_out=ss[:, par, n:n + 1]).then_inc(sq_done, 1)

                if front:
                    front_tanh(i + 1, 1 - par)
                if mid:
                    chunk(0)
                    chunk(1)
                    square(0)
                if front:
                    front_round(i + 1, 1 - par)
                if back:
                    j = i - 1
                    for hf in range(2):
                        act.wait_ge(q2_turned, done(j * 2 + hf + 1))
                        act.wait_ge(down_done, done(j))
                        nc.scalar.activation(q2T[:, hf * 8:hf * 8 + 8, :].rearrange("p k t -> p (k t)"), ps_b[hf][:], ACT.Copy).then_inc(q2T_done, 1)
                if mid:
                    chunk(2)
                    square(1)
                    chunk(3)
                    square(2)
                    square(3)
                if front:
                    front_copy(i + 1, 1 - par)
                if mid:
                    act.wait_ge(bs_done, done(i + 1))
                    nc.scalar.activation(hp[:, par, :], hp[:, par, :], ACT.Identity, scale=bs[:, par, 6:7],
                                         bias=S["round"][:, 0:1]).then_inc(t2_done, 1)

            front_tanh(0, 0)
            front_round(0, 0)
            front_copy(0, 0)
            steps(act, step)

        @block.gpsimd
        def _(pool):
            pool.sem_inc(hp_done, LEAD)
            pool.sem_inc(r_done, LEAD)

            def step(i, par, front, back, mid=True):
                if not mid:
                    return
                for n in range(NCH):
                    g = i * NCH + n
                    pool.wait_ge(q2_done, done(i - 1))
                    pool.wait_ge(h_done, done(g + 1))
                    nc.gpsimd.tensor_tensor(hp[:, par, n * 512:(n + 1) * 512], h[:, n % 2, :],
                                            S["ln"][:, n * 512:(n + 1) * 512], ALU.mult).then_inc(hp_done, 1)
                pool.wait_ge(var_done, i + 1)
                nc.gpsimd.tensor_tensor(bs[:, par, 3:4], bs[:, par, 2:3], S["mhalf"][:, 0:1], ALU.pow).then_inc(r_done, 1)

            steps(pool, step)

        @block.vector
        def _(dve):
            for s in (scaled, q_done, h_done, bs_done, q2_done, x_done):
                dve.sem_inc(s, LEAD)
            FRONT, MID = 5, 5
            used = [0]

            def link(base, n, ins):
                ins.then_inc(chain, 1)
                dve.wait_ge(chain, base + n)

            def front_scale(i, par):
                base = i * FRONT + (i - 1) * MID if not isinstance(i, int) or i else 0
                dve.wait_ge(tanh, done(i + 1))
                dve.wait_ge(q_done, done(i - 1))
                link(base, 1, nc.vector.scalar_tensor_tensor(out=th[:], in0=th[:], scalar=1.0, in1=col(S["ratio"][0], i),
                                                             op0=ALU.add, op1=ALU.mult))
                link(base, 2, nc.vector.tensor_scalar(o[:, par, :], th[:], S["tfs"][:, bass.ds(i, 1)], None, ALU.mult))
                link(base, 3, nc.vector.tensor_reduce(fs[:, par, 0:1], o[:, par, :], AX.X, ALU.max, apply_absolute_value=True))
                link(base, 4, nc.vector.tensor_scalar(fs[:, par, 1:2], fs[:, par, 0:1], EPS, None, ALU.max))
                nc.vector.tensor_scalar(fs[:, par, 4:5], fs[:, par, 1:2], S["wscale"][:, 0:1], 1.0 / QP, ALU.mult, ALU.mult)
                nc.vector.tensor_scalar(fs[:, par, 5:6], fs[:, par, 1:2], S["wscale"][:, 1:2], 1.0 / QP, ALU.mult, ALU.mult)
                link(base, 5, nc.vector.reciprocal(fs[:, par, 2:3], fs[:, par, 1:2]))
                nc.vector.tensor_scalar(fs[:, par, 3:4], fs[:, par, 2:3], QP, None, ALU.mult).then_inc(scaled, 1)

            def front_quant(i, par):
                dve.wait_ge(to_done, done(i + 1))
                dve.wait_ge(q_turned, done(i - 1))
                nc.vector.tensor_scalar(q[:, par, :], o[:, par, :], -ROUND, QP, ALU.add, ALU.min).then_inc(q_done, 1)

            def step(i, par, front, back, mid=True):
                def chunk(n):
                    g = i * NCH + n
                    dve.wait_ge(silu_done, done(g + 1))
                    dve.wait_ge(up_done, done(g + 1))
                    dve.wait_ge(sq_done, done(g - 1))
                    dve.wait_ge(hp_done, done(g - 1))
                    nc.vector.scalar_tensor_tensor(out=h[:, n % 2, :], in0=ps_up[n % 2][:], scalar=fs[:, par, 5:6],
                                                   in1=sg[:, n % 2, :], op0=ALU.mult, op1=ALU.mult).then_inc(h_done, 1)

                def chunk_max(n):
                    dve.wait_ge(hp_done, done(i * NCH + n + 1))
                    return nc.vector.tensor_reduce(mx[:, par, n:n + 1], hp[:, par, n * 512:(n + 1) * 512], AX.X, ALU.max,
                                                   apply_absolute_value=True)

                j = i - 1
                if mid:
                    chunk(0)
                if back:
                    dve.wait_ge(t2_done, done(j + 1))
                    dve.wait_ge(q2_turned, done(j * 2))
                    nc.vector.tensor_scalar(q2[:], hp[:, 1 - par, :], -ROUND, QP, ALU.add, ALU.min).then_inc(q2_done, 1)
                if front:
                    front_scale(i + 1, 1 - par)
                if mid:
                    chunk(1)
                    chunk_max(0)
                if front:
                    front_quant(i + 1, 1 - par)
                if mid:
                    chunk(2)
                    chunk_max(1)
                    chunk(3)
                    chunk_max(2)
                    base = (i + (2 if front else 1)) * FRONT + i * MID
                    dve.wait_ge(sq_done, done(i * NCH + NCH))
                    link(base, 1, nc.vector.tensor_reduce(bs[:, par, 0:1], ss[:, par, :], AX.X, ALU.add))
                    nc.vector.tensor_scalar(bs[:, par, 2:3], bs[:, par, 0:1], 1.0 / INNER, RMS_EPS, ALU.mult, ALU.add).then_inc(var_done, 1)
                    link(base, 2, chunk_max(3))
                    link(base, 3, nc.vector.tensor_reduce(bs[:, par, 1:2], mx[:, par, :], AX.X, ALU.max))
                    dve.wait_ge(r_done, done(i + 1))
                    link(base, 4, nc.vector.tensor_scalar(bs[:, par, 4:5], bs[:, par, 1:2], bs[:, par, 3:4], EPS, ALU.mult, ALU.max))
                    nc.vector.tensor_scalar(bs[:, par, 7:8], bs[:, par, 4:5], S["wscale"][:, 2:3], 1.0 / QP, ALU.mult, ALU.mult)
                    link(base, 5, nc.vector.reciprocal(bs[:, par, 5:6], bs[:, par, 4:5]))
                    nc.vector.tensor_scalar(bs[:, par, 6:7], bs[:, par, 5:6], bs[:, par, 3:4], QP, ALU.mult, ALU.mult).then_inc(bs_done, 1)
                if back:
                    dve.wait_ge(down_done, done(j + 1))
                    nc.vector.scalar_tensor_tensor(out=col(S["x"], j), in0=ps_y[:], scalar=bs[:, 1 - par, 7:8],
                                                   in1=col(S["x"], j), op0=ALU.mult, op1=ALU.add).then_inc(x_done, 1)

            front_scale(0, 0)
            front_quant(0, 0)
            steps(dve, step)


def project(nc, A, S):
    with ExitStack() as ctx:
        def sb(name, shape, dt):
            return ctx.enter_context(nc.sbuf_tensor(name, shape, dt))

        def sem(name):
            return ctx.enter_context(nc.semaphore(name))

        th = sb("r_tanh", [P, 2, C], F32)
        t1 = sb("r_gated", [P, 2, C], F32)
        o = sb("r_mixed", [P, 2, C], F32)
        oT = sb("r_mixed_T", [P, 2, CT, P], F32)
        ps_o = [ctx.enter_context(nc.psum_tensor(f"ps_mixed_T{i}", [P, 512], F32)) for i in range(2)]
        ps_l = [ctx.enter_context(nc.psum_tensor(f"ps_logits{i}", [P, E], F32)) for i in range(2)]
        tanh = sem("r_tanh_done")
        gated = sem("r_gated_done")
        mixed = sem("r_mixed_done")
        turned = sem("r_turned")
        oT_done = sem("r_T_done")
        logits = sem("r_logits")
        lcopied = sem("r_logits_copied")
        stored = [sem(f"r_stored{i}") for i in range(2)]
        zeroed = sem("r_lists_zeroed")

        def pairs(eng, step):
            with eng.Fori(0, TILES // 2) as ii:
                step(ii * 2, 0, ii)
                step(ii * 2 + 1, 1, ii)

        def col(ap, i):
            return ap[:, bass.ds(i, 1), :].rearrange("p a c -> p (a c)")

        block = ctx.enter_context(nc.Block())

        @block.sync
        def _(sp):
            for s in stored:
                sp.sem_inc(s, 16)
            sp.dma_start(S["lists"].rearrange("(p a) b -> p (a b)", p=P), S["zrow"][:]).then_inc(zeroed, 16)

            def step(i, par, ii):
                sp.wait_ge(mixed, done(i + 1))
                sp.dma_start(S["rows"][bass.ds(i * P, P), :], o[:, par, :]).then_inc(stored[par], 16)

            pairs(sp, step)
            for s in stored:
                sp.wait_ge(s, 16 + 16 * (TILES // 2))
            sp.wait_ge(zeroed, 16)

        @block.scalar
        def _(act):
            act.sem_inc(tanh, LEAD)
            act.sem_inc(oT_done, LEAD)

            def step(i, par, ii):
                act.wait_ge(gated, done(i - 1))
                nc.scalar.activation(th[:, par, :], col(S["x"], i), ACT.Tanh, scale=0.5).then_inc(tanh, 1)
                act.wait_ge(turned, done(i + 1))
                act.wait_ge(logits, done(i - 1))
                nc.scalar.activation(oT[:, par, :, :].rearrange("p k t -> p (k t)"), ps_o[par][:], ACT.Copy).then_inc(oT_done, 1)

            pairs(act, step)

        @block.vector
        def _(dve):
            dve.sem_inc(gated, LEAD)
            dve.sem_inc(mixed, LEAD)
            dve.sem_inc(lcopied, LEAD)

            def step(i, par, ii):
                dve.wait_ge(tanh, done(i + 1))
                nc.vector.scalar_tensor_tensor(out=t1[:, par, :], in0=th[:, par, :], scalar=1.0, in1=col(S["ratio"][1], i),
                                               op0=ALU.add, op1=ALU.mult).then_inc(gated, 1)
                dve.wait_ge(gated, done(i + 1))
                dve.wait_ge(turned, done(i - 1))
                dve.wait_ge(stored[par], ii * 16 + 16)
                nc.vector.tensor_scalar(o[:, par, :], t1[:, par, :], S["tfs"][:, bass.ds(i, 1)], None, ALU.mult).then_inc(mixed, 1)
                dve.wait_ge(logits, done(i + 1))
                nc.vector.tensor_copy(col(S["logits"], i), ps_l[par][:]).then_inc(lcopied, 1)

            pairs(dve, step)

        @block.tensor
        def _(pe):
            pe.sem_inc(turned, LEAD)
            pe.sem_inc(logits, LEAD)

            def step(i, par, ii):
                pe.wait_ge(mixed, done(i + 1))
                pe.wait_ge(oT_done, done(i - 1))
                for k in range(CT):
                    last = nc.tensor.transpose(ps_o[par][:, k * P:(k + 1) * P], o[:, par, k * P:(k + 1) * P], S["ident"][:])
                last.then_inc(turned, 1)
                pe.wait_ge(oT_done, done(i + 1))
                pe.wait_ge(lcopied, done(i - 1))
                for k in range(CT):
                    last = nc.tensor.matmul(ps_l[par][:], oT[:, par, k, :], S["gate_wT"][:, k, :], start=(k == 0), stop=(k == CT - 1))
                last.then_inc(logits, 1)

            pairs(pe, step)


def route(nc, A, S):
    with ExitStack() as ctx:
        def sb(name, shape, dt):
            return ctx.enter_context(nc.sbuf_tensor(name, shape, dt))

        def sem(name):
            return ctx.enter_context(nc.semaphore(name))

        score = sb("score", [P, TILES, E], F32)
        top = sb("top", [P, TILES, 8], F32)
        topi = sb("top_index", [P, TILES, 8], U32)
        expert = sb("expert", [P, TILES, K], F32)
        hot = sb("one_hot", [P, TILES, K, E], F32)
        hot2 = sb("one_hot_times", [P, TILES, K, E], F32)
        chosen = sb("chosen", [P, TILES, E], F32)
        before = [sb(f"before{i}", [P, TILES, E], F32) for i in range(2)]
        rank = sb("rank", [P, TILES, E], F32)
        rank4 = sb("rank4", [P, TILES, K], F32)
        ranki = sb("rank_int", [P, TILES, K], I32)
        lowi = sb("rank_low", [P, TILES, K], I32)
        highi = sb("rank_high", [P, TILES, K], I32)
        lowf = sb("rank_low_f", [P, TILES, K], F32)
        highf = sb("rank_high_f", [P, TILES, K], F32)
        place = sb("place_f", [P, TILES, K], F32)
        placei = sb("place", [P, TILES, K], U32)
        slotf = sb("slot_f", [P, TILES, K], F32)
        lmax = sb("logit_max", [P, TILES], F32)
        shifted = sb("logit_shifted", [P, TILES, E], F32)
        ex = sb("logit_exp", [P, TILES, E], F32)
        z = sb("softmax_sum", [P, TILES], F32)
        rz = sb("softmax_rsum", [P, TILES], F32)
        prob = sb("prob", [P, TILES, E], F32)
        wsum = sb("chosen_sum", [P, TILES], F32)
        rwsum = sb("chosen_rsum", [P, TILES], F32)
        cnt = sb("count", [P, E], F32)
        cnti = sb("count_int", [P, E], I32)
        ntf = sb("tiles_f", [P, E], F32)
        onesr = sb("ones_row", [P, E], F32)
        cum = sb("tiles_until_f", [P, E], F32)
        base = sb("first_row", [P, E], F32)
        cmp_ = sb("tile_cmp", [1, TABLE, E], F32)
        cmp2 = sb("tile_cmp_n", [1, TABLE, E], F32)
        te = sb("tile_expert_f", [1, TABLE], F32)
        tstart = sb("tile_start_f", [1, TABLE], F32)
        tj = sb("tile_j_f", [1, TABLE], F32)
        tcol = sb("tile_col_f", [1, TABLE], F32)
        first = sb("tile_first_f", [1, TABLE], F32)
        after = sb("tile_after_f", [1, TABLE], F32)
        valid = sb("tile_after_valid", [1, TABLE], F32)
        endf = sb("tile_end_f", [1, 1], F32)
        endi = sb("tile_end_int", [1, 1], I32)
        ps_r = ctx.enter_context(nc.psum_tensor("ps_rank", [P, TILES * E], F32))
        ps_c = ctx.enter_context(nc.psum_tensor("ps_count", [P, E], F32))

        tanh = sem("t_tanh")
        seq = sem("t_seq")
        prefix = sem("t_prefix")
        ranked = sem("t_ranked")
        shift = sem("t_shift")
        exped = sem("t_exp")
        placed = sem("t_placed")
        scattered = sem("t_scattered")
        listed = sem("t_listed")

        block = ctx.enter_context(nc.Block())

        @block.scalar
        def _(act):
            nc.scalar.activation(score[:], S["logits"][:], ACT.Tanh, scale=0.5).then_inc(tanh, 1)
            act.wait_ge(shift, 1)
            nc.scalar.activation(ex[:], shifted[:], ACT.Exp).then_inc(exped, 1)

        @block.tensor
        def _(pe):
            pe.wait_ge(prefix, 1)
            nc.tensor.matmul(ps_r[:], S["tri"][:], chosen[:].rearrange("p n e -> p (n e)"), start=True, stop=False)
            nc.tensor.matmul(ps_r[:], S["ones"][:], before[1][:].rearrange("p n e -> p (n e)"), start=False, stop=True)
            nc.tensor.matmul(ps_c[:], S["ones"][:], chosen[:, TILES - 1, :], start=True, stop=False)
            nc.tensor.matmul(ps_c[:], S["ones"][:], before[1][:, TILES - 1, :], start=False, stop=True).then_inc(ranked, 1)

        @block.vector
        def _(dve):
            count = [0]

            def link(ins):
                count[0] += 1
                ins.then_inc(seq, 1)
                dve.wait_ge(seq, count[0])

            v = nc.vector
            dve.wait_ge(tanh, 1)
            link(v.tensor_scalar(score[:], score[:], 0.5, 0.5, ALU.mult, ALU.add))
            for i in range(TILES):
                last = v.max(top[:, i, :], score[:, i, :])
            link(last)
            for i in range(TILES):
                last = v.max_index(topi[:, i, :], top[:, i, :], score[:, i, :])
            link(last)
            link(v.tensor_copy(expert[:], topi[:, :, 0:K]))
            for i in range(TILES):
                last = v.tensor_tensor(hot[:, i, :, :], S["iota_e"][:].unsqueeze(1).to_broadcast([P, K, E]),
                                       expert[:, i, :].unsqueeze(2).to_broadcast([P, K, E]), ALU.is_equal)
            link(last)
            link(v.tensor_reduce(chosen[:], hot[:].rearrange("p n k e -> p n e k"), AX.X, ALU.add))
            v.memset(before[0][:, 0, :], 0.0)
            link(v.tensor_copy(before[0][:, 1:TILES, :], chosen[:, 0:TILES - 1, :]))
            a = 0
            for d in (1, 2, 4, 8):
                v.tensor_copy(before[1 - a][:, 0:d, :], before[a][:, 0:d, :])
                link(v.tensor_tensor(before[1 - a][:, d:TILES, :], before[a][:, d:TILES, :], before[a][:, 0:TILES - d, :], ALU.add))
                a = 1 - a
            link(v.tensor_copy(before[1][:], before[0][:]))
            dve.sem_inc(prefix, 1)

            dve.wait_ge(ranked, 1)
            link(v.tensor_copy(rank[:].rearrange("p n e -> p (n e)"), ps_r[:]))
            link(v.tensor_copy(cnt[:], ps_c[:]))

            def pick(out, values):
                for i in range(TILES):
                    last = v.tensor_tensor(hot2[:, i, :, :], hot[:, i, :, :], values[:, i, :].unsqueeze(1).to_broadcast([P, K, E]), ALU.mult)
                link(last)
                link(v.tensor_reduce(out, hot2[:], AX.X, ALU.add))

            pick(rank4[:], rank)
            link(v.tensor_copy(ranki[:], rank4[:]))
            link(v.tensor_scalar(lowi[:], ranki[:], P - 1, 9, ALU.bitwise_and, ALU.logical_shift_left))
            link(v.tensor_scalar(highi[:], ranki[:], 7, None, ALU.logical_shift_right))
            link(v.tensor_copy(lowf[:], lowi[:]))
            link(v.tensor_copy(highf[:], highi[:]))
            link(v.scalar_tensor_tensor(out=place[:], in0=expert[:], scalar=float(JT), in1=lowf[:], op0=ALU.mult, op1=ALU.add))
            link(v.tensor_tensor(place[:], place[:], highf[:], ALU.add))
            v.tensor_copy(placei[:], place[:]).then_inc(placed, 1)
            link(v.tensor_reduce(lmax[:], S["logits"][:], AX.X, ALU.max))
            v.tensor_tensor(shifted[:], S["logits"][:], lmax[:].unsqueeze(2).to_broadcast([P, TILES, E]), ALU.subtract).then_inc(shift, 1)
            dve.wait_ge(exped, 1)
            link(v.tensor_reduce(z[:], ex[:], AX.X, ALU.add))
            link(v.reciprocal(rz[:], z[:]))
            link(v.tensor_tensor(prob[:], ex[:], rz[:].unsqueeze(2).to_broadcast([P, TILES, E]), ALU.mult))
            pick(S["weight"][:], prob)
            link(v.tensor_reduce(wsum[:], S["weight"][:], AX.X, ALU.add))
            link(v.reciprocal(rwsum[:], wsum[:]))
            link(v.tensor_tensor(S["weight"][:], S["weight"][:], rwsum[:].unsqueeze(2).to_broadcast([P, TILES, K]), ALU.mult))

            link(v.tensor_scalar(cnt[:], cnt[:], float(P - 1), None, ALU.add))
            link(v.tensor_copy(cnti[:], cnt[:]))
            link(v.tensor_scalar(cnti[:], cnti[:], 7, None, ALU.logical_shift_right))
            link(v.tensor_copy(ntf[:], cnti[:]))
            link(v.tensor_scalar(ntf[:], ntf[:], 1.0, None, ALU.max))
            link(v.memset(onesr[:], 1.0))
            link(v.tensor_tensor_scan(cum[:], onesr[:], ntf[:], 0.0, ALU.mult, ALU.add))
            link(v.tensor_tensor(base[:], cum[:], ntf[:], ALU.subtract))
            link(v.tensor_scalar(base[:], base[:], float(P), None, ALU.mult))
            link(v.tensor_tensor(rank[:], rank[:], base[:].unsqueeze(1).to_broadcast([P, TILES, E]), ALU.add))
            pick(slotf[:], rank)
            link(v.tensor_copy(S["slot"][:], slotf[:]))
            tb = S["iota_t"][0:1, :].unsqueeze(2).to_broadcast([1, TABLE, E])
            link(v.tensor_tensor(cmp_[:], cum[0:1, :].unsqueeze(1).to_broadcast([1, TABLE, E]), tb, ALU.is_le))
            link(v.tensor_tensor(cmp2[:], cmp_[:], ntf[0:1, :].unsqueeze(1).to_broadcast([1, TABLE, E]), ALU.mult))
            link(v.tensor_reduce(te[:], cmp_[:], AX.X, ALU.add))
            link(v.tensor_reduce(tstart[:], cmp2[:], AX.X, ALU.add))
            link(v.tensor_scalar(te[:], te[:], float(E - 1), None, ALU.min))
            link(v.tensor_tensor(tj[:], S["iota_t"][0:1, :], tstart[:], ALU.subtract))
            link(v.tensor_scalar(first[:], tj[:], 0.0, None, ALU.is_equal))
            link(v.tensor_scalar(after[:], te[:], 2.0, None, ALU.add))
            link(v.tensor_scalar(valid[:], after[:], float(E - 1), None, ALU.is_le))
            link(v.tensor_tensor(after[:], after[:], valid[:], ALU.mult))
            link(v.tensor_tensor(after[:], after[:], first[:], ALU.mult))
            link(v.tensor_copy(S["tile_next"][:], after[:]))
            link(v.tensor_scalar(endf[:], cum[0:1, E - 1:E], 1.0, None, ALU.add))
            link(v.tensor_copy(endi[:], endf[:]))
            link(v.tensor_scalar(S["tile_end"][:], endi[:], 1, 1, ALU.logical_shift_right, ALU.logical_shift_left))
            link(v.tensor_scalar(tj[:], tj[:], float(JT - 1), None, ALU.min))
            link(v.scalar_tensor_tensor(out=tcol[:], in0=te[:], scalar=float(JT), in1=tj[:], op0=ALU.mult, op1=ALU.add))
            link(v.tensor_copy(S["tile_expert"][:], te[:]))
            link(v.tensor_copy(S["tile_col"][:], tcol[:]))

        @block.gpsimd
        def _(pool):
            pool.wait_ge(placed, 1)
            for i in range(TILES):
                for k in range(K):
                    nc.gpsimd.indirect_dma_start(S["lists"], bass.IndirectOffsetOnAxis(placei[:, i, k:k + 1], 0),
                                                 S["token"][:, i:i + 1], None, bounds_check=P * 512 - 1).then_inc(scattered, 16)

        @block.sync
        def _(sp):
            sp.wait_ge(scattered, 16 * TILES * K)
            sp.dma_start(S["list"][:], S["lists"].rearrange("(p a) b -> p (a b)", p=P)).then_inc(listed, 16)
            sp.wait_ge(listed, 16)


def experts(nc, A, S):
    with ExitStack() as ctx:
        def sb(name, shape, dt):
            return ctx.enter_context(nc.sbuf_tensor(name, shape, dt))

        def ps(name, shape, dt):
            return ctx.enter_context(nc.psum_tensor(name, shape, dt))

        def sem(name):
            return ctx.enter_context(nc.semaphore(name))

        SLOTS = 3
        REST = LARGE - P
        gu_hi = sb("e_gate_up_high", [P, SLOTS, 2, CT, WIDE], F32R)
        gu_lo = sb("e_gate_up_low", [P, SLOTS, 2, CT, WIDE], F32R)
        d_hi = sb("e_down_high", [P, SLOTS, 3, C], F32R)
        d_lo = sb("e_down_low", [P, SLOTS, 3, C], F32R)
        st_gu = sb("e_stage_gate_up", [P, 2, 2, CT, LARGE], F32)
        st_d = sb("e_stage_down", [P, 2, 2, C], F32)
        st_sgu = sb("e_stage_small_gate_up", [P, 2, 2, CT, SMALL], F32)
        st_sd = sb("e_stage_small_down", [P, 2, C], F32)
        idx = sb("e_index", [P, 2], U32)
        x = sb("e_rows", [P, 2, C], F32)
        xh = sb("e_rows_T_high", [P, 2, CT * P], F32R)
        xl = sb("e_rows_T_low", [P, 2, CT * P], F32R)
        sg = sb("e_silu", [P, 2, WIDE], F32)
        a = sb("e_hidden", [P, 2, WIDE], F32)
        ah = sb("e_hidden_T_high", [P, 2, 3 * P], F32R)
        al = sb("e_hidden_T_low", [P, 2, 3 * P], F32R)
        y = sb("e_out", [P, 2, C], F32)
        ps_x = ps("ps_rows_T", [P, 512], F32)
        ps_g = [ps(f"ps_e_gate{i}", [P, WIDE], F32) for i in range(2)]
        ps_u = [ps(f"ps_e_up{i}", [P, WIDE], F32) for i in range(2)]
        ps_a = ps("ps_hidden_T", [P, 3 * P], F32)
        ps_y = [ps(f"ps_e_out{i}", [P, C], F32) for i in range(2)]

        large_in = [sem(f"e_large_in{i}") for i in range(2)]
        small_in = [sem(f"e_small_in{i}") for i in range(2)]
        staged = sem("e_staged")
        high = [sem(f"e_{n}_high_done") for n in ("gate", "up", "down")]
        low = [sem(f"e_{n}_low_done") for n in ("gate", "up", "down")]
        gate_low, up_low, d_low = low
        indexed = sem("e_indexed")
        index_ready = sem("e_index_ready")
        gathered = [sem(f"e_gathered{i}") for i in range(2)]
        turned = sem("e_turned")
        xh_done = sem("e_rows_T_high_done")
        xl_done = sem("e_rows_T_low_done")
        gate_done = sem("e_gate_done")
        up_done = sem("e_up_done")
        silu_done = sem("e_silu_done")
        a_done = sem("e_hidden_done")
        a_turned = sem("e_hidden_turned")
        ah_done = sem("e_hidden_T_high_done")
        al_done = sem("e_hidden_T_low_done")
        down_done = sem("e_down_done")
        y_done = sem("e_out_done")
        stored = [sem(f"e_stored{i}") for i in range(2)]
        filled = sem("e_filled")
        all_stored = sem("e_all_stored")

        def look(eng, table, t, low, top):
            return eng.value_load(table[0:1, bass.ds(t, 1)], min_val=low, max_val=top)

        def steps(eng, step):
            end = look(eng, S["tile_end"], 0, E, LISTED)
            step(0, 0, 0, prev=False)
            step(1, 1, 0)
            with eng.Fori(1, LISTED // 2) as tt:
                with eng.If(end > tt * 2):
                    step(tt * 2, 0, tt)
                    step(tt * 2 + 1, 1, tt)
            step(end, 0, end // 2, nxt=False, mid=False)
            return end

        GATE, UP, DOWN = range(3)

        def called_for(eng, t, prepare, part):
            n = look(eng, S["tile_next"], t, 0, E - 1)
            with eng.If(n > 0):
                prepare(n, part, t)

        def pieces(e, part):
            st, slot, sst = e % 2, e % SLOTS, (e // 2) % 2
            if part < DOWN:
                for stage, i, lo, hi in ((st_gu, st, 0, LARGE), (st_sgu, sst, LARGE, WIDE)):
                    yield (stage[:, bass.ds(i, 1), part, :, :].rearrange("p a k n -> p (a k) n"),
                           gu_hi[:, bass.ds(slot, 1), part, :, lo:hi].rearrange("p a k n -> p (a k) n"),
                           gu_lo[:, bass.ds(slot, 1), part, :, lo:hi].rearrange("p a k n -> p (a k) n"))
            else:
                for n, stage, k in ((P, st_d[:, bass.ds(st, 1), 0, :], 0), (P, st_sd[:, bass.ds(sst, 1), :], 1),
                                    (REST, st_d[0:REST, bass.ds(st, 1), 1, :], 2)):
                    yield stage, d_hi[0:n, bass.ds(slot, 1), k, :], d_lo[0:n, bass.ds(slot, 1), k, :]

        block = ctx.enter_context(nc.Block())

        @block.sync
        def _(sp):
            def rows(ap, i):
                return ap[bass.ds(i, 1), :, :].rearrange("a (k p) n -> p (a k) n", p=P)

            def load(e, st, pair, sst, before):
                sp.wait_ge(up_low, done(e - 1))
                if st == 0:
                    for n, name in enumerate(("L1_ffn_cWg", "L1_ffn_cWu")):
                        sp.dma_start(st_sgu[:, sst, n, :, :], rows(A[name], pair)).then_inc(small_in[sst], 16)
                for n, name in enumerate(("L1_ffn_Wg", "L1_ffn_Wu")):
                    sp.dma_start(st_gu[:, st, n, :, :], rows(A[name], e)).then_inc(large_in[st], 16)
                if before:
                    landed(*before)
                sp.wait_ge(d_low, done(e - 1))
                if st == 0:
                    sp.dma_start(st_sd[:, sst, :], A["L1_ffn_cWd"][bass.ds(pair, 1), :, :].rearrange("a i n -> (a i) n")).then_inc(small_in[sst], 16)
                down = A["L1_ffn_Wd"][bass.ds(e, 1), :, :].rearrange("a i n -> (a i) n")
                sp.dma_start(st_d[:, st, 0, :], down[0:P, :]).then_inc(large_in[st], 16)
                sp.dma_start(st_d[0:REST, st, 1, :], down[P:LARGE, :]).then_inc(large_in[st], 16)

            def landed(four, n):
                sp.wait_ge(large_in[n % 2], four * 128 + (n // 2 + 1) * 64)
                sp.wait_ge(small_in[n // 2], four * 48 + 48)
                sp.sem_inc(staged, 1)

            load(0, 0, 0, 0, None)
            for n in range(1, 4):
                load(n, n % 2, n // 2, n // 2, (0, n - 1))
            with sp.Fori(1, E // 4) as four:
                for n in range(4):
                    load(four * 4 + n, n % 2, four * 2 + n // 2, n // 2, (four, n - 1) if n else (four - 1, 3))
            landed(E // 4 - 1, 3)
            end = look(sp, S["tile_end"], 0, E, LISTED)
            with sp.Fori(E // 2, LISTED // 2) as tt:
                with sp.If(end <= tt * 2):
                    for i in range(2):
                        sp.dma_start(S["results"][bass.ds(tt * (2 * P) + i * P, P), :], S["zrow"][:].bitcast(F32)).then_inc(filled, 16)
                with sp.If(end > tt * 2):
                    sp.sem_inc(filled, 32)
            sp.wait_ge(filled, (LISTED - E) * 16)

        @block.gpsimd
        def _(pool):
            pool.sem_inc(indexed, LEAD)

            def gather(t, par):
                c = look(pool, S["tile_col"], t, 0, E * JT - 1)
                pool.wait_ge(turned, done(t - 1))
                nc.gpsimd.tensor_copy(idx[:, par:par + 1], S["list"][:, bass.ds(c, 1)]).then_inc(indexed, 1)
                pool.wait_ge(indexed, done(t + 1))
                pool.sem_inc(index_ready, 1)
                nc.gpsimd.indirect_dma_start(x[:, par, :], None, S["rows"], bass.IndirectOffsetOnAxis(idx[:, par:par + 1], 0),
                                             bounds_check=TOKENS - 1).then_inc(gathered[par], 16)

            end = look(pool, S["tile_end"], 0, E, LISTED)
            gather(0, 0)
            gather(1, 1)
            gather(2, 0)
            with pool.Fori(1, LISTED // 2) as tt:
                with pool.If(end > tt * 2):
                    gather(tt * 2 + 1, 1)
                    gather(tt * 2 + 2, 0)

        @block.tensor
        def _(pe):
            for s in (turned, gate_done, up_done, a_turned, down_done):
                pe.sem_inc(s, LEAD)

            def turn(t, par, tt):
                pe.wait_ge(gathered[par], tt * 16 + 16)
                pe.wait_ge(xl_done, done(t))
                for k in range(CT):
                    last = nc.tensor.transpose(ps_x[:, k * P:(k + 1) * P], x[:, par, k * P:(k + 1) * P], S["ident"][:])
                last.then_inc(turned, 1)

            def products(out, lhs_hi, lhs_lo, rhs_hi, rhs_lo, parts):
                for k, n in enumerate(parts):
                    at = slice(k * P, (k + 1) * P)
                    nc.tensor.matmul(out, lhs_hi[0:n, at], rhs_hi(k, n), start=(k == 0), stop=False)
                    nc.tensor.matmul(out, lhs_hi[0:n, at], rhs_lo(k, n), start=False, stop=False)
                    last = nc.tensor.matmul(out, lhs_lo[0:n, at], rhs_hi(k, n), start=False, stop=(k == len(parts) - 1))
                return last

            def gate_up(w, slot, which):
                return lambda k, n: w[:, bass.ds(slot, 1), which, k, :].rearrange("p a n -> p (a n)")

            def down(w, slot):
                return lambda k, n: w[0:n, bass.ds(slot, 1), k, :].rearrange("p a n -> p (a n)")

            def step(t, par, tt, nxt=True, prev=True, mid=True):
                if mid:
                    e = look(pe, S["tile_expert"], t, 0, E - 1)
                    slot = e % SLOTS
                if prev:
                    e_prev = look(pe, S["tile_expert"], t - 1, 0, E - 1)
                    slot_prev = e_prev % SLOTS
                if nxt:
                    turn(t + 1, 1 - par, tt + par)
                if prev:
                    pe.wait_ge(a_done, done(t))
                    pe.wait_ge(al_done, done(t - 1))
                    nc.tensor.transpose(ps_a[:, 0:P], a[:, 1 - par, 0:P], S["ident"][:])
                    nc.tensor.transpose(ps_a[:, P:2 * P], a[:, 1 - par, LARGE:WIDE], S["ident"][:])
                    nc.tensor.transpose(ps_a[0:REST, 2 * P:3 * P], a[:, 1 - par, P:LARGE], S["ident"][:]).then_inc(a_turned, 1)
                if mid:
                    pe.wait_ge(gate_low, done(e + 1))
                    pe.wait_ge(xl_done, done(t + 1))
                    pe.wait_ge(silu_done, done(t - 1))
                    products(ps_g[par][:], xh[:, par, :], xl[:, par, :], gate_up(gu_hi, slot, 0), gate_up(gu_lo, slot, 0),
                             [P] * CT).then_inc(gate_done, 1)
                    pe.wait_ge(up_low, done(e + 1))
                    pe.wait_ge(a_done, done(t - 1))
                    products(ps_u[par][:], xh[:, par, :], xl[:, par, :], gate_up(gu_hi, slot, 1), gate_up(gu_lo, slot, 1),
                             [P] * CT).then_inc(up_done, 1)
                if prev:
                    pe.wait_ge(d_low, done(e_prev + 1))
                    pe.wait_ge(al_done, done(t))
                    pe.wait_ge(y_done, done(t - 2))
                    products(ps_y[1 - par][:], ah[:, 1 - par, :], al[:, 1 - par, :], down(d_hi, slot_prev), down(d_lo, slot_prev),
                             [P, P, REST]).then_inc(down_done, 1)

            turn(0, 0, 0)
            steps(pe, step)

        @block.scalar
        def _(act):
            for s in (*high, xh_done, silu_done, ah_done, y_done):
                act.sem_inc(s, LEAD)
            for s in stored:
                act.sem_inc(s, 16)

            def prepare_high(e, part, t):
                act.wait_ge(staged, e + 1)
                act.wait_ge(down_done if part == DOWN else up_done, done(t))
                for src, hi, lo in pieces(e, part):
                    last = nc.scalar.activation(hi, src, ACT.Copy)
                last.then_inc(high[part], 1)

            def rows_high(t, par):
                act.wait_ge(turned, done(t + 1))
                act.wait_ge(up_done, done(t - 1))
                nc.scalar.activation(xh[:, par, :], ps_x[:], ACT.Copy).then_inc(xh_done, 1)

            def step(t, par, tt, nxt=True, prev=True, mid=True):
                if nxt:
                    rows_high(t + 1, 1 - par)
                if prev:
                    act.wait_ge(a_turned, done(t))
                    act.wait_ge(down_done, done(t - 2))
                    nc.scalar.activation(ah[:, 1 - par, 0:2 * P], ps_a[:, 0:2 * P], ACT.Copy)
                    nc.scalar.activation(ah[0:REST, 1 - par, 2 * P:3 * P], ps_a[0:REST, 2 * P:3 * P], ACT.Copy).then_inc(ah_done, 1)
                if mid:
                    called_for(act, t, prepare_high, GATE)
                    act.wait_ge(gate_done, done(t + 1))
                    act.wait_ge(a_done, done(t - 1))
                    nc.scalar.activation(sg[:, par, :], ps_g[par][:], ACT.Silu).then_inc(silu_done, 1)
                if mid and prev:
                    called_for(act, t - 1, prepare_high, DOWN)
                if mid:
                    called_for(act, t, prepare_high, UP)
                if prev:
                    act.wait_ge(down_done, done(t))
                    act.wait_ge(stored[1 - par], tt * 16 + par * 16)
                    nc.scalar.activation(y[:, 1 - par, :], ps_y[1 - par][:], ACT.Copy).then_inc(y_done, 1)
                    act.wait_ge(y_done, done(t))
                    act.dma_start(S["results"][bass.ds((t - 1) * P, P), :], y[:, 1 - par, :]).then_inc(stored[1 - par], 16)

            for e in range(2):
                for part in (GATE, UP, DOWN):
                    prepare_high(e, part, 0)
            rows_high(0, 0)
            end = steps(act, step)
            for s in stored:
                act.wait_ge(s, 16 + end * 8)
            act.sem_inc(all_stored, 1)

        @block.vector
        def _(dve):
            for s in (*low, xl_done, a_done, al_done):
                dve.sem_inc(s, LEAD)

            def prepare_low(e, part, t):
                dve.wait_ge(high[part], done(e + 1))
                for src, hi, lo in pieces(e, part):
                    last = nc.vector.tensor_tensor(lo, src, hi.bitcast(F32), ALU.subtract)
                last.then_inc(low[part], 1)

            def rows_low(t, par):
                dve.wait_ge(xh_done, done(t + 1))
                nc.vector.tensor_tensor(xl[:, par, :], ps_x[:], xh[:, par, :].bitcast(F32), ALU.subtract).then_inc(xl_done, 1)

            def step(t, par, tt, nxt=True, prev=True, mid=True):
                if nxt:
                    rows_low(t + 1, 1 - par)
                if prev:
                    dve.wait_ge(ah_done, done(t))
                    nc.vector.tensor_tensor(al[:, 1 - par, 0:2 * P], ps_a[:, 0:2 * P], ah[:, 1 - par, 0:2 * P].bitcast(F32), ALU.subtract)
                    nc.vector.tensor_tensor(al[0:REST, 1 - par, 2 * P:3 * P], ps_a[0:REST, 2 * P:3 * P],
                                            ah[0:REST, 1 - par, 2 * P:3 * P].bitcast(F32), ALU.subtract).then_inc(al_done, 1)
                if mid:
                    called_for(dve, t, prepare_low, GATE)
                if mid:
                    dve.wait_ge(silu_done, done(t + 1))
                    dve.wait_ge(up_done, done(t + 1))
                    dve.wait_ge(a_turned, done(t - 1))
                    nc.vector.tensor_tensor(a[:, par, 0:LARGE], ps_u[par][:, 0:LARGE], sg[:, par, 0:LARGE], ALU.mult)
                    nc.vector.scalar_tensor_tensor(out=a[:, par, LARGE:WIDE], in0=ps_u[par][:, LARGE:WIDE], scalar=SMALL_SCALE,
                                                   in1=sg[:, par, LARGE:WIDE], op0=ALU.mult, op1=ALU.mult).then_inc(a_done, 1)
                if mid and prev:
                    called_for(dve, t - 1, prepare_low, DOWN)
                if mid:
                    called_for(dve, t, prepare_low, UP)

            for e in range(2):
                for part in (GATE, UP, DOWN):
                    prepare_low(e, part, 0)
            rows_low(0, 0)
            steps(dve, step)


def combine(nc, A, S, out):
    with ExitStack() as ctx:
        def sb(name, shape, dt):
            return ctx.enter_context(nc.sbuf_tensor(name, shape, dt))

        def sem(name):
            return ctx.enter_context(nc.semaphore(name))

        DEPTH = 2
        row = [[sb(f"c_row{d}{k}", [P, C], F32) for k in range(K)] for d in range(DEPTH)]
        fetched = [[sem(f"c_fetched{d}{k}") for k in range(K)] for d in range(DEPTH)]
        added = sem("c_added")
        stored = sem("c_stored")
        flat = out.rearrange("b t c -> (b t) c")
        block = ctx.enter_context(nc.Block())

        @block.gpsimd
        def _(pool):
            for i in range(TILES):
                if i >= DEPTH:
                    pool.wait_ge(added, K * (i - DEPTH + 1))
                for k in range(K):
                    nc.gpsimd.indirect_dma_start(row[i % DEPTH][k][:], None, S["results"],
                                                 bass.IndirectOffsetOnAxis(S["slot"][:, i, k:k + 1], 0),
                                                 bounds_check=LISTED * P - 1).then_inc(fetched[i % DEPTH][k], 16)

        @block.vector
        def _(dve):
            for i in range(TILES):
                for k in range(K):
                    dve.wait_ge(fetched[i % DEPTH][k], 16 * (i // DEPTH + 1))
                    if k:
                        dve.wait_ge(added, K * i + k)
                    nc.vector.scalar_tensor_tensor(out=S["x"][:, i, :], in0=row[i % DEPTH][k][:], scalar=S["weight"][:, i, k:k + 1],
                                                   in1=S["x"][:, i, :], op0=ALU.mult, op1=ALU.add).then_inc(added, 1)

        @block.sync
        def _(sp):
            for i in range(TILES):
                sp.wait_ge(added, K * (i + 1))
                sp.dma_start(flat[i * P:(i + 1) * P, :], S["x"][:, i, :]).then_inc(stored, 16)
            sp.wait_ge(stored, 16 * TILES)


def program(nc, A, out):
    with ExitStack() as ctx:
        S = {}

        def keep(stack, name, shape, dt):
            S[name] = stack.enter_context(nc.sbuf_tensor("s_" + name, shape, dt))

        S["lists"] = nc.dram_tensor("lists", [P * 512, 1], U32, kind="Internal").ap()
        S["rows"] = nc.dram_tensor("rows", [TOKENS, C], F32, kind="Internal").ap()
        S["results"] = nc.dram_tensor("results", [LISTED * P, C], F32, kind="Internal").ap()
        keep(ctx, "x", [P, TILES, C], F32)
        keep(ctx, "ident", [P, P], F32)
        keep(ctx, "identb", [P, P], BF16)
        keep(ctx, "tri", [P, P], F32)
        keep(ctx, "ones", [P, P], F32)
        keep(ctx, "round", [P, 1], F32)
        keep(ctx, "two", [P, 1], F32)
        keep(ctx, "mhalf", [P, 1], F32)
        keep(ctx, "token", [P, TILES], U32)
        keep(ctx, "slot", [P, TILES, K], U32)
        keep(ctx, "weight", [P, TILES, K], F32)
        keep(ctx, "logits", [P, TILES, E], F32)
        keep(ctx, "list", [P, 512], U32)
        keep(ctx, "zrow", [P, 512], U32)
        keep(ctx, "tile_expert", [1, TABLE], I32)
        keep(ctx, "tile_col", [1, TABLE], I32)
        keep(ctx, "tile_next", [1, TABLE], I32)
        keep(ctx, "tile_end", [1, 1], I32)
        keep(ctx, "iota_e", [P, E], F32)
        keep(ctx, "iota_t", [P, TABLE], F32)
        keep(ctx, "gate_wT", [P, CT, E], F32)
        keep(ctx, "tfs", [P, TILES], F32)
        with ExitStack() as front:
            keep(front, "ratio1", [P, TILES, C], F32)
            with ExitStack() as layer0:
                keep(layer0, "ratio0", [P, TILES, C], F32)
                S["ratio"] = [S["ratio0"], S["ratio1"]]
                keep(layer0, "u", [P, LAYERS, CT], F32)
                keep(layer0, "decay", [P, B * UNITS], F32)
                setup(nc, A, S)
                mix(nc, A, S)
                keep(layer0, "wscale", [P, 3], F32)
                keep(layer0, "ln", [P, INNER], F32)
                S["wT"] = [layer0.enter_context(nc.sbuf_tensor(f"s_wT{m}", shape, BF16))
                           for m, shape in enumerate(([P, CT, INNER], [P, CT, INNER], [P, IT, C]))]
                ternary(nc, A, S)
                bitnet(nc, A, S)
            project(nc, A, S)
        route(nc, A, S)
        experts(nc, A, S)
        combine(nc, A, S, out)


_INS = ["x", "fside_BxSxS_0", "cond_512", "L0_cond_w", "L0_cond_u", "L0_ffn_w_gate", "L0_ffn_w_up", "L0_ffn_w_down",
        "L0_ffn_ln_weight", "L1_cond_w", "L1_cond_u", "L1_ffn_gate_w", "L1_ffn_Wg", "L1_ffn_Wu", "L1_ffn_Wd",
        "L1_ffn_cWg", "L1_ffn_cWu", "L1_ffn_cWd"]


def kernel(**inputs):
    import concourse.bacc as _bacc
    from concourse.bass_utils import run_bass_kernel_spmd as _run

    nc = _bacc.Bacc("TRN2", target_bir_lowering=False, num_devices=1)
    arrays, A = {}, {}
    for name in _INS:
        v = np.ascontiguousarray(inputs[name])
        arrays[f"in_{name}"] = v
        A[name] = nc.dram_tensor(f"in_{name}", v.shape, mybir.dt.from_np(v.dtype), kind="ExternalInput").ap()
    out = nc.dram_tensor("out_0", (B, T, C), F32, kind="ExternalOutput").ap()
    program(nc, A, out)
    r = _run(nc, [arrays], core_ids=[0])
    return r.results[0]["out_0"]
```

```python
from contextlib import ExitStack

import numpy as np

import concourse.bass as bass
from concourse import mybir

F32 = mybir.dt.float32
F32R = mybir.dt.float32r
BF16 = mybir.dt.bfloat16
I32 = mybir.dt.int32
U32 = mybir.dt.uint32
ALU = mybir.AluOpType
ACT = mybir.ActivationFunctionType
AX = mybir.AxisListType

P = 128
B, T, C = 4, 512, 512
TOKENS = B * T
TILES = TOKENS // P
TT = T // P
CT = C // P
LAYERS = 2
UNITS = CT * LAYERS
INNER = 2048
IT = INNER // P
NCH = INNER // 512
EPS = 1e-5
RMS_EPS = 1e-6
QP = 127.0
ROUND = 12582912.0
E = 32
K = 4
LARGE, SMALL = 192, 128
WIDE = LARGE + SMALL
SMALL_SCALE = 0.05
LISTED = TOKENS * K // P + E
JT = TOKENS // P
LEAD = 4


def done(n):
    return n + LEAD


def setup(nc, A, S):
    with ExitStack() as ctx:
        def sb(name, shape, dt):
            return ctx.enter_context(nc.sbuf_tensor(name, shape, dt))

        def sem(name):
            return ctx.enter_context(nc.semaphore(name))

        condT = sb("cond_T", [P, B], F32)
        wdec = sb("decay_w", [P, LAYERS, CT], F32)
        time = sb("time_gate", [P, B], F32)
        half = sb("time_half", [P, B], F32)
        gate_rows = sb("gate_rows", [E, C], F32)
        ps_t = ctx.enter_context(nc.psum_tensor("ps_time", [P, B], F32))
        ps_g = ctx.enter_context(nc.psum_tensor("ps_gate_w", [P, CT * E], F32))

        small_in = sem("p_small_in")
        u_in = sem("p_u_in")
        zeroed = sem("p_zeroed")
        consts = sem("p_consts")
        exp_w = sem("p_exp_w")
        decay0 = sem("p_decay0")
        tsum = sem("p_time_sum")
        ttanh = sem("p_time_tanh")
        gturned = sem("p_gate_turned")
        dve_seq = sem("p_dve_seq")
        block = ctx.enter_context(nc.Block())

        @block.sync
        def _(sp):
            with nc.allow_non_contiguous_dma("a few hundred small vectors' elements"):
                sp.dma_start(condT[:], A["cond_512"].rearrange("b k -> k b")).then_inc(small_in, 16)
                for l in range(LAYERS):
                    sp.dma_start(wdec[:, l, :], A[f"L{l}_cond_w"].rearrange("(c p) -> p c", p=P)).then_inc(small_in, 16)
                    sp.dma_start(S["u"][:, l, :], A[f"L{l}_cond_u"].rearrange("(c p) -> p c", p=P)).then_inc(u_in, 16)
            sp.dma_start(gate_rows[:], A["L1_ffn_gate_w"]).then_inc(small_in, 16)
            sp.wait_ge(u_in, 32)

        @block.gpsimd
        def _(pool):
            nc.gpsimd.memset(S["ident"][:], 0.0)
            nc.gpsimd.memset(S["identb"][:], 0.0)
            nc.gpsimd.memset(S["tri"][:], float(E * JT))
            nc.gpsimd.memset(S["ones"][:], 1.0)
            nc.gpsimd.memset(S["round"][:], ROUND)
            nc.gpsimd.memset(S["two"][:], 2.0)
            nc.gpsimd.memset(S["zrow"][:], 0)
            nc.gpsimd.memset(S["mhalf"][:], -0.5).then_inc(zeroed, 1)
            pool.wait_ge(zeroed, 1)
            for m in (S["ident"], S["identb"]):
                nc.gpsimd.affine_select(out=m[:], in_=m[:], compare_op=ALU.not_equal, fill=1.0, base=0,
                                        pattern=[[-1, P]], channel_multiplier=1)
            nc.gpsimd.affine_select(out=S["tri"][:], in_=S["tri"][:], compare_op=ALU.is_gt, fill=0.0, base=0,
                                    pattern=[[1, P]], channel_multiplier=-1)
            nc.gpsimd.iota(S["token"][:], pattern=[[P, TILES]], base=0, channel_multiplier=1)
            nc.gpsimd.iota(S["iota_e"][:], pattern=[[1, E]], base=0, channel_multiplier=0, allow_small_or_imprecise_dtypes=True).then_inc(consts, 1)

        @block.scalar
        def _(act):
            act.wait_ge(small_in, 16 * 4)
            nc.scalar.activation(wdec[:], wdec[:], ACT.Exp).then_inc(exp_w, 1)
            act.wait_ge(exp_w, 1)
            nc.scalar.activation(wdec[:], wdec[:], ACT.Exp, scale=-1.0).then_inc(decay0, 1)
            act.wait_ge(tsum, 1)
            nc.scalar.activation(time[:], ps_t[:], ACT.Tanh, scale=0.5).then_inc(ttanh, 1)

        @block.vector
        def _(dve):
            seq = [0]

            def link(ins):
                seq[0] += 1
                ins.then_inc(dve_seq, 1)
                dve.wait_ge(dve_seq, seq[0])

            dve.wait_ge(ttanh, 1)
            link(nc.vector.tensor_scalar(time[:], time[:], 0.5, 0.5, ALU.mult, ALU.add))
            link(nc.vector.tensor_scalar(half[:], time[:], 0.5, 0.5, ALU.mult, ALU.add))
            for b in range(B):
                nc.vector.tensor_scalar(S["tfs"][:, b * TT:(b + 1) * TT], time[:, b:b + 1].to_broadcast([P, TT]), 0.1, 0.4,
                                        ALU.mult, ALU.add)
            dve.wait_ge(decay0, 1)
            for b in range(B):
                nc.vector.tensor_scalar(S["decay"][:, b * UNITS:(b + 1) * UNITS].rearrange("p (c l) -> p l c", l=LAYERS),
                                        wdec[:], half[:, b:b + 1], None, ALU.mult)
            dve.wait_ge(gturned, 1)
            nc.vector.tensor_copy(S["gate_wT"][:].rearrange("p k e -> p (k e)"), ps_g[:])

        @block.tensor
        def _(pe):
            pe.wait_ge(consts, 1)
            pe.wait_ge(small_in, 16 * 4)
            nc.tensor.matmul(ps_t[:], S["ones"][:], condT[:], start=True, stop=True).then_inc(tsum, 1)
            for k in range(CT):
                last = nc.tensor.transpose(ps_g[:, k * E:(k + 1) * E], gate_rows[:, k * P:(k + 1) * P], S["ident"][0:E, 0:E])
            last.then_inc(gturned, 1)


def ternary(nc, A, S):
    with ExitStack() as ctx:
        def sb(name, shape, dt):
            return ctx.enter_context(nc.sbuf_tensor(name, shape, dt))

        def sem(name):
            return ctx.enter_context(nc.semaphore(name))

        NW = 4
        QW = INNER * C // P // NW
        stage = sb("weight_stage", [P, NW * QW], F32)
        ws = [S["x"][:].rearrange("p a c -> p (a c)"), stage[:], S["x"][:].rearrange("p a c -> p (a c)")]
        wq = sb("weight_half", [P, 2 * QW], BF16)
        absum = sb("abs_sums", [P, 3, NW], F32)
        part = sb("abs_part", [P, 3], F32)
        rscale = sb("weight_rscale", [P, 3], F32)
        junk = sb("abs_junk", [P, QW], BF16)
        ps_sum = ctx.enter_context(nc.psum_tensor("ps_sum", [P, 4], F32))
        ps_t = [ctx.enter_context(nc.psum_tensor(f"ps_wt{i}", [P, 1024], BF16)) for i in range(2)]

        ln_in = sem("w_ln_in")
        up_in = sem("w_up_in")
        down_in = sem("w_down_in")
        abs_done = sem("w_abs_done")
        part_done = sem("w_part_done")
        sum_done = sem("w_sum_done")
        scale_done = sem("w_scale_done")
        dve_seq = sem("w_dve_seq")
        rounded = sem("w_rounded")
        rounded_last = sem("w_rounded_last")
        ternary_done = sem("w_ternary")
        turned = sem("w_turned")
        copied = sem("w_copied")

        weights = [None,
                   A["L0_ffn_w_up"].rearrange("(n p) h -> p n h", p=P),
                   A["L0_ffn_w_down"].rearrange("(n p) i -> p n i", p=P)]
        block = ctx.enter_context(nc.Block())

        @block.sync
        def _(sp):
            sp.dma_start(ws[1].rearrange("p (n h) -> p n h", h=C), weights[1]).then_inc(up_in, 16)
            sp.dma_start(S["ln"][:], A["L0_ffn_ln_weight"].rearrange("(a i) -> a i", a=1).to_broadcast([P, INNER])).then_inc(ln_in, 16)
            sp.wait_ge(ternary_done, NW)
            sp.dma_start(ws[2].rearrange("p (n h) -> p n h", h=INNER), weights[2]).then_inc(down_in, 16)
            sp.wait_ge(ln_in, 16)

        def wait_weights(eng, m):
            if m:
                eng.wait_ge((up_in, down_in)[m - 1], 16)

        @block.scalar
        def _(act):
            for m in range(3):
                wait_weights(act, m)
                for c in range(NW):
                    if m + c:
                        act.wait_ge(abs_done, m * NW + c)
                    nc.scalar.activation(junk[:], ws[m][:, c * QW:(c + 1) * QW], ACT.Abs,
                                         accum_out=absum[:, m, c:c + 1]).then_inc(abs_done, 1)
                act.wait_ge(scale_done, m + 1)
                for c in range(NW - 1):
                    v = ws[m][:, c * QW:(c + 1) * QW]
                    nc.scalar.activation(v, v, ACT.Identity, scale=rscale[:, m:m + 1], bias=S["round"][:, 0:1]).then_inc(rounded, 1)

        @block.gpsimd
        def _(pool):
            for m in range(3):
                pool.wait_ge(scale_done, m + 1)
                v = ws[m][:, (NW - 1) * QW:NW * QW]
                nc.gpsimd.tensor_scalar(v, v, rscale[:, m:m + 1], ROUND, ALU.mult, ALU.add).then_inc(rounded_last, 1)

        @block.vector
        def _(dve):
            seq = [0]

            def link(ins):
                seq[0] += 1
                ins.then_inc(dve_seq, 1)
                dve.wait_ge(dve_seq, seq[0])

            def scale(m):
                dve.wait_ge(abs_done, (m + 1) * NW)
                nc.vector.tensor_reduce(part[:, m:m + 1], absum[:, m, :], AX.X, ALU.add).then_inc(part_done, 1)
                dve.wait_ge(sum_done, m + 1)
                link(nc.vector.tensor_scalar(S["wscale"][:, m:m + 1], ps_sum[:, m:m + 1], 1.0 / (INNER * C), EPS,
                                             ALU.mult, ALU.max))
                nc.vector.reciprocal(rscale[:, m:m + 1], S["wscale"][:, m:m + 1]).then_inc(scale_done, 1)

            scale(0)
            for m in range(3):
                for c in range(NW):
                    if c < NW - 1:
                        dve.wait_ge(rounded, m * (NW - 1) + c + 1)
                    else:
                        dve.wait_ge(rounded_last, m + 1)
                    if c % 2 == 0 and m + c:
                        dve.wait_ge(turned, 8 * m + 2 * c)
                    q = wq[:, (c % 2) * QW:(c % 2 + 1) * QW]
                    link(nc.vector.tensor_scalar(q, ws[m][:, c * QW:(c + 1) * QW], -ROUND, 1.0, ALU.add, ALU.min))
                    nc.vector.tensor_scalar(q, q, -1.0, None, ALU.max).then_inc(ternary_done, 1)
                    if c % 2:
                        for g in range(c // 2 * 4, c // 2 * 4 + 4):
                            dve.wait_ge(turned, 8 * m + g + 1)
                            if m < 2:
                                out = S["wT"][m][:, g % 4, (g // 4) * 1024:(g // 4 + 1) * 1024]
                                src = ps_t[g % 2][:]
                            else:
                                out = S["wT"][m][:, (g % 2) * 8:(g % 2 + 1) * 8, (g // 2) * P:(g // 2 + 1) * P]
                                src = ps_t[g % 2][:].rearrange("p (k o) -> p k o", o=P)
                            nc.vector.tensor_copy(out, src).then_inc(copied, 1)
                            if g == 5 and m < 2:
                                scale(m + 1)

        @block.tensor
        def _(pe):
            def total(m):
                pe.wait_ge(part_done, m + 1)
                nc.tensor.matmul(ps_sum[:, m:m + 1], S["ones"][:], part[:, m:m + 1], start=True, stop=True).then_inc(sum_done, 1)

            total(0)
            for m in range(3):
                for g in range(8):
                    if g % 4 == 0:
                        pe.wait_ge(ternary_done, NW * m + g // 2 + 2)
                    if 8 * m + g >= 2:
                        pe.wait_ge(copied, 8 * m + g - 1)
                    for a in range(8):
                        if m < 2:
                            src = wq[:, a * C + (g % 4) * P:a * C + (g % 4 + 1) * P]
                        else:
                            k = (g % 2) * 8 + a
                            src = wq[:, (g // 2 % 2) * INNER + k * P:(g // 2 % 2) * INNER + (k + 1) * P]
                        last = nc.tensor.transpose(ps_t[g % 2][:, a * P:(a + 1) * P], src, S["identb"][:])
                    last.then_inc(turned, 1)
                    if g == 6 and m < 2:
                        total(m + 1)


def mix(nc, A, S):
    with ExitStack() as ctx:
        def sb(name, shape, dt):
            return ctx.enter_context(nc.sbuf_tensor(name, shape, dt))

        def sem(name):
            return ctx.enter_context(nc.semaphore(name))

        side = sb("side", [P, TT, C], F32)
        kt = sb("key", [P, 2, T], F32)
        km = sb("key_min", [P, 2, T], F32)
        ek = sb("exp_key", [P, 2, T], F32)
        ekv = sb("exp_key_value", [P, 2, T], F32)
        ua = sb("bonus_arg", [P, 2, T], F32)
        eu = sb("exp_bonus", [P, 2, T], F32)
        euv = sb("exp_bonus_value", [P, 2, T], F32)
        fwd = [[sb(f"forward{q}{l}", [P, T], F32) for l in range(2)] for q in range(2)]
        bwd = [[sb(f"backward{q}{l}", [P, T + 1], F32) for l in range(2)] for q in range(2)]
        dmax = sb("den_max", [P, 2, T], F32)
        guess = sb("den_reciprocal_guess", [P, 2, T], F32)
        rem = sb("den_times_guess", [P, T], F32)
        corr = sb("guess_correction", [P, T], F32)
        num = sb("numerator", [P, 2, T], F32)
        rden = sb("den_reciprocal", [P, 2, T], F32)
        diag = sb("decay_diagonals", [P, 2, P], F32)
        ps_k = [ctx.enter_context(nc.psum_tensor(f"ps_key{i}", [P, T], F32)) for i in range(2)]
        ps_q = [[ctx.enter_context(nc.psum_tensor(f"ps_sum{q}{l}", [P, T], F32)) for l in range(2)] for q in range(2)]

        side_in = sem("m_side_in")
        turned = sem("m_turned")
        key = sem("m_key")
        keymin = sem("m_keymin")
        expk = sem("m_expk")
        expkv = sem("m_expkv")
        arg = sem("m_arg")
        expu = sem("m_expu")
        expuv = sem("m_expuv")
        scanned = sem("m_scanned")
        summed = sem("m_summed")
        ratio = sem("m_ratio")
        tails = sem("m_tails")
        maxed = sem("m_den_max")
        logged = sem("m_den_log")
        guessed = sem("m_guess")
        timed = sem("m_den_times_guess")
        corrected = sem("m_corrected")
        num_out = sem("m_num_out")
        weights_in = sem("m_weights_in")
        refined = sem("m_refined")

        def batches(eng, unit_pair):
            for ct in range(CT):
                unit_pair(0, ct, first=(ct == 0))
            with eng.Fori(1, B - 1) as b:
                for ct in range(CT):
                    unit_pair(b, ct)
            for ct in range(CT):
                unit_pair(B - 1, ct, last=ct)

        block = ctx.enter_context(nc.Block())

        @block.sync
        def _(sp):
            with sp.Fori(0, B) as b:
                sp.wait_ge(turned, done(b * CT))
                sp.dma_start(side[:], A["fside_BxSxS_0"][bass.ds(b, 1), :, :].rearrange("b (n p) c -> p (b n) c", p=P)).then_inc(side_in, 16)
            sp.dma_start(S["x"][:].rearrange("p a c -> p (a c)").rearrange("p (n h) -> p n h", h=C),
                         A["L0_ffn_w_gate"].rearrange("(n p) h -> p n h", p=P)).then_inc(weights_in, 16)
            sp.wait_ge(weights_in, 16)

        @block.tensor
        def _(pe):
            pe.sem_inc(turned, LEAD)
            pe.sem_inc(summed, LEAD)
            pe.wait_ge(tails, 1)

            def turn(b, ct):
                if ct == 0:
                    pe.wait_ge(side_in, b * 16 + 16)
                pe.wait_ge(key, done(b * CT + ct - 1))
                for tt in range(TT):
                    last = nc.tensor.transpose(ps_k[ct % 2][:, tt * P:(tt + 1) * P], side[:, tt, ct * P:(ct + 1) * P], S["ident"][:])
                last.then_inc(turned, 1)

            def unit_pair(b, ct, first=False, last=None):
                for l in range(LAYERS):
                    u = b * UNITS + ct * LAYERS + l
                    pe.wait_ge(scanned, done(u + 1))
                    pe.wait_ge(expuv, done(u + 1))
                    pe.wait_ge(maxed, done(u - 1))
                    pe.wait_ge(num_out, done(u - 1))
                    for q, extra in ((1, eu), (0, euv)):
                        for tt in range(TT):
                            out = ps_q[q][l][:, tt * P:(tt + 1) * P]
                            at = slice(tt * P, (tt + 1) * P)
                            nc.tensor.matmul(out, fwd[q][l][:, at], S["ident"][:], start=True, stop=False)
                            nc.tensor.matmul(out, bwd[q][l][:, tt * P + 1:(tt + 1) * P + 1], diag[:, l, :], start=False, stop=False)
                            done_ = nc.tensor.matmul(out, extra[:, l, at], S["ident"][:], start=False, stop=True)
                    done_.then_inc(summed, 1)
                    if l == 0 and (last is None or last < CT - 2):
                        turn(b + (ct + 2) // CT, (ct + 2) % CT)

            turn(0, 0)
            turn(0, 1)
            batches(pe, unit_pair)

        @block.scalar
        def _(act):
            nc.scalar.preload_act_table_set("natural_log_exp_and_others")
            for s in (key, expk, expu, guessed, logged, corrected, num_out):
                act.sem_inc(s, LEAD)

            def key_out(c, par):
                act.wait_ge(turned, done(c + 1))
                act.wait_ge(expuv, done(2 * c - 2))
                nc.scalar.activation(kt[:, par, :], ps_k[par][:], ACT.Copy).then_inc(key, 1)

            def exp_key(c, par):
                act.wait_ge(keymin, done(c + 1))
                act.wait_ge(scanned, done(2 * c - 2))
                nc.scalar.activation(ek[:, par, :], km[:, par, :], ACT.Exp).then_inc(expk, 1)

            def guess_of(u, l):
                act.wait_ge(maxed, done(u + 1))
                act.wait_ge(refined, done(u - 1))
                nc.scalar.activation(guess[:, l, :], dmax[:, l, :], ACT.Ln).then_inc(logged, 1)
                act.wait_ge(logged, done(u + 1))
                nc.scalar.activation(guess[:, l, :], guess[:, l, :], ACT.Exp, scale=-1.0).then_inc(guessed, 1)
                act.wait_ge(summed, done(u + 1))
                act.wait_ge(ratio, done(u - 1))
                nc.scalar.activation(num[:, l, :], ps_q[0][l][:], ACT.Copy).then_inc(num_out, 1)
                act.wait_ge(timed, done(u + 1))
                act.wait_ge(refined, done(u))
                nc.scalar.activation(corr[:], rem[:], ACT.Identity, scale=-1.0, bias=S["two"][:, 0:1]).then_inc(corrected, 1)

            def unit_pair(b, ct, first=False, last=None):
                c = b * CT + ct
                for l in range(LAYERS):
                    u = c * LAYERS + l
                    if last != CT - 1:
                        if l == 0:
                            key_out(c + 1, (ct + 1) % 2)
                        else:
                            exp_key(c + 1, (ct + 1) % 2)
                    act.wait_ge(arg, done(u + 1))
                    act.wait_ge(summed, done(u - 1))
                    nc.scalar.activation(eu[:, l, :], ua[:, l, :], ACT.Exp).then_inc(expu, 1)
                    if not first:
                        guess_of(u - 2, l)

            key_out(0, 0)
            exp_key(0, 0)
            batches(act, unit_pair)
            guess_of(B * UNITS - 2, 0)
            guess_of(B * UNITS - 1, 1)

        @block.gpsimd
        def _(pool):
            for s in (expkv, expuv, refined, timed):
                pool.sem_inc(s, LEAD)

            def exp_key_value(c, par):
                pool.wait_ge(scanned, done(2 * c - 2))
                pool.wait_ge(expk, done(c + 1))
                nc.gpsimd.tensor_tensor(ekv[:, par, :], ek[:, par, :], kt[:, par, :], ALU.mult).then_inc(expkv, 1)

            def refine(u, l):
                pool.wait_ge(corrected, done(u))
                pool.wait_ge(guessed, done(u + 1))
                nc.gpsimd.tensor_tensor(rem[:], dmax[:, l, :], guess[:, l, :], ALU.mult).then_inc(timed, 1)
                pool.wait_ge(corrected, done(u + 1))
                pool.wait_ge(ratio, done(u - 1))
                nc.gpsimd.tensor_tensor(rden[:, l, :], corr[:], guess[:, l, :], ALU.mult).then_inc(refined, 1)

            def unit_pair(b, ct, first=False, last=None):
                c = b * CT + ct
                for l in range(LAYERS):
                    u = c * LAYERS + l
                    if l == 1 and last != CT - 1:
                        exp_key_value(c + 1, (ct + 1) % 2)
                    pool.wait_ge(summed, done(u - 1))
                    nc.gpsimd.tensor_tensor(diag[:, l, :], S["ident"][:], S["decay"][:, bass.ds(u, 1)].to_broadcast([P, P]), ALU.mult)
                    pool.wait_ge(expu, done(u + 1))
                    nc.gpsimd.tensor_tensor(euv[:, l, :], eu[:, l, :], kt[:, ct % 2, :], ALU.mult).then_inc(expuv, 1)
                    if not first:
                        refine(u - 2, l)

            exp_key_value(0, 0)
            batches(pool, unit_pair)
            refine(B * UNITS - 2, 0)
            refine(B * UNITS - 1, 1)

        @block.vector
        def _(dve):
            for q in range(2):
                for l in range(2):
                    done_ = nc.vector.memset(bwd[q][l][:, T:T + 1], 0.0)
            done_.then_inc(tails, 1)
            for s in (keymin, arg, scanned, maxed, ratio):
                dve.sem_inc(s, LEAD)

            def key_min(c, par):
                dve.wait_ge(key, done(c + 1))
                dve.wait_ge(expk, done(c - 1))
                nc.vector.tensor_scalar(km[:, par, :], kt[:, par, :], 30.0, None, ALU.min).then_inc(keymin, 1)

            def bonus_args(c, ct):
                for l in range(LAYERS):
                    dve.wait_ge(expu, done(c * LAYERS + l - 1))
                    nc.vector.tensor_scalar(ua[:, l, :], kt[:, ct % 2, :], S["u"][:, l, ct:ct + 1], 30.0, ALU.add, ALU.min).then_inc(arg, 1)

            def den_max(u, l):
                dve.wait_ge(summed, done(u + 1))
                nc.vector.tensor_scalar(dmax[:, l, :], ps_q[1][l][:], 1e-8, None, ALU.max).then_inc(maxed, 1)

            def ratio_of(u, b, n):
                l, ct = n % LAYERS, n // LAYERS
                dve.wait_ge(refined, done(u + 1))
                dve.wait_ge(num_out, done(u + 1))
                nc.vector.tensor_tensor(S["ratio"][l][:, bass.ds(b * TT, TT), ct * P:(ct + 1) * P],
                                        rden[:, l, :].rearrange("p (n c) -> p n c", n=TT),
                                        num[:, l, :].rearrange("p (n c) -> p n c", n=TT), ALU.mult).then_inc(ratio, 1)

            def unit_pair(b, ct, first=False, last=None):
                c = b * CT + ct
                for l in range(LAYERS):
                    n = ct * LAYERS + l
                    u = b * UNITS + n
                    dve.wait_ge(expkv, done(c + 1))
                    dve.wait_ge(summed, done(u - 1))
                    decay = S["decay"][:, bass.ds(u, 1)].to_broadcast([P, T])
                    for q, src in ((0, ekv), (1, ek)):
                        v = src[:, ct % 2, :]
                        nc.vector.tensor_tensor_scan(fwd[q][l][:], decay, v, 0.0, ALU.mult, ALU.add)
                        done_ = nc.vector.tensor_tensor_scan(bwd[q][l][:, 0:T][:, ::-1], decay, v[:, ::-1], 0.0, ALU.mult, ALU.add)
                    done_.then_inc(scanned, 1)
                    if not isinstance(u, int) or u >= 3:
                        ratio_of(u - 3, b if n >= 3 else b - 1, (n - 3) % UNITS)
                    if not first or l:
                        den_max(u - 1, 1 - l)
                    if last != CT - 1:
                        if l == 0:
                            key_min(c + 1, (ct + 1) % 2)
                        else:
                            bonus_args(c + 1, (ct + 1) % CT)

            key_min(0, 0)
            bonus_args(0, 0)
            batches(dve, unit_pair)
            ratio_of(B * UNITS - 3, B - 1, UNITS - 3)
            den_max(B * UNITS - 1, 1)
            ratio_of(B * UNITS - 2, B - 1, UNITS - 2)
            ratio_of(B * UNITS - 1, B - 1, UNITS - 1)


def bitnet(nc, A, S):
    with ExitStack() as ctx:
        def sb(name, shape, dt):
            return ctx.enter_context(nc.sbuf_tensor(name, shape, dt))

        def sem(name):
            return ctx.enter_context(nc.semaphore(name))

        th = sb("f_tanh", [P, C], F32)
        o = sb("f_mixed", [P, 2, C], F32)
        q = sb("f_quant", [P, 2, C], BF16)
        qT = sb("f_quant_T", [P, 2, CT, P], BF16)
        fs = sb("f_scalars", [P, 2, 8], F32)
        sg = sb("silu", [P, 2, 512], F32)
        h = sb("hidden", [P, 2, 512], F32)
        sqj = sb("square_junk", [P, 512], BF16)
        hp = sb("hidden_ln", [P, 2, INNER], F32)
        ss = sb("square_sums", [P, 2, NCH], F32)
        mx = sb("chunk_max", [P, 2, NCH], F32)
        bs = sb("b_scalars", [P, 2, 8], F32)
        q2 = sb("b_quant", [P, INNER], BF16)
        q2T = sb("b_quant_T", [P, IT, P], BF16)

        def ps(name, shape, dt):
            return ctx.enter_context(nc.psum_tensor(name, shape, dt))

        ps_gate = [ps(f"ps_gate{i}", [P, 512], F32) for i in range(2)]
        ps_up = [ps(f"ps_up{i}", [P, 512], F32) for i in range(2)]
        ps_f = ps("ps_front_T", [P, 1024], BF16)
        ps_b = [ps(f"ps_back_T{i}", [P, 1024], BF16) for i in range(2)]
        ps_y = ps("ps_down", [P, 512], F32)

        x_first = sem("b_x_first")
        x_rest = sem("b_x_rest")
        tanh = sem("b_tanh")
        scaled = sem("b_scaled")
        to_done = sem("b_front_rounded")
        q_done = sem("b_front_quant")
        q_turned = sem("b_front_turned")
        qT_done = sem("b_front_T")
        gate_done = sem("b_gate")
        up_done = sem("b_up")
        silu_done = sem("b_silu")
        h_done = sem("b_hidden")
        sq_done = sem("b_squares")
        hp_done = sem("b_hidden_ln")
        var_done = sem("b_var")
        r_done = sem("b_rsqrt")
        bs_done = sem("b_back_scalars")
        t2_done = sem("b_back_rounded")
        q2_done = sem("b_back_quant")
        q2_turned = sem("b_back_turned")
        q2T_done = sem("b_back_T")
        down_done = sem("b_down")
        x_done = sem("b_x")
        chain = sem("b_chain")

        def steps(eng, step):
            step(0, 0, front=True, back=False)
            step(1, 1, front=True, back=True)
            with eng.Fori(1, TILES // 2 - 1) as ii:
                step(ii * 2, 0, front=True, back=True)
                step(ii * 2 + 1, 1, front=True, back=True)
            step(TILES - 2, 0, front=True, back=True)
            step(TILES - 1, 1, front=False, back=True)
            step(TILES, 0, front=False, back=True, mid=False)

        def col(ap, i):
            return ap[:, bass.ds(i, 1), :].rearrange("p a c -> p (a c)")

        block = ctx.enter_context(nc.Block())

        @block.sync
        def _(sp):
            rows = A["x"].rearrange("b (n p) c -> p (b n) c", p=P)
            sp.dma_start(S["x"][:, 0:2, :], rows[:, 0:2, :]).then_inc(x_first, 16)
            sp.dma_start(S["x"][:, 2:TILES, :], rows[:, 2:TILES, :]).then_inc(x_rest, 16)

        @block.tensor
        def _(pe):
            for s in (q_turned, gate_done, up_done, q2_turned, down_done):
                pe.sem_inc(s, LEAD)

            def turn_front(i, par):
                pe.wait_ge(q_done, done(i + 1))
                pe.wait_ge(qT_done, done(i))
                for k in range(CT):
                    last = nc.tensor.transpose(ps_f[:, k * P:(k + 1) * P], q[:, par, k * P:(k + 1) * P], S["identb"][:])
                last.then_inc(q_turned, 1)

            def step(i, par, front, back, mid=True):
                def chunk(n):
                    g = i * NCH + n
                    pe.wait_ge(silu_done, done(g - 1))
                    for k in range(CT):
                        last = nc.tensor.matmul(ps_gate[n % 2][:], qT[:, par, k, :], S["wT"][0][:, k, n * 512:(n + 1) * 512],
                                                start=(k == 0), stop=(k == CT - 1))
                    last.then_inc(gate_done, 1)
                    pe.wait_ge(h_done, done(g - 1))
                    for k in range(CT):
                        last = nc.tensor.matmul(ps_up[n % 2][:], qT[:, par, k, :], S["wT"][1][:, k, n * 512:(n + 1) * 512],
                                                start=(k == 0), stop=(k == CT - 1))
                    last.then_inc(up_done, 1)

                def down(hf):
                    pe.wait_ge(q2T_done, done(j * 2 + hf + 1))
                    for k in range(hf * 8, hf * 8 + 8):
                        last = nc.tensor.matmul(ps_y[:], q2T[:, k, :], S["wT"][2][:, k, :], start=(k == 0), stop=(k == IT - 1))
                    return last

                j = i - 1
                if mid:
                    pe.wait_ge(qT_done, done(i + 1))
                    for n in range(NCH - 1):
                        chunk(n)
                if back:
                    pe.wait_ge(q2_done, done(j + 1))
                    for hf in range(2):
                        pe.wait_ge(q2T_done, done(j * 2 + hf - 1))
                        for a in range(8):
                            k = hf * 8 + a
                            last = nc.tensor.transpose(ps_b[hf][:, a * P:(a + 1) * P], q2[:, k * P:(k + 1) * P], S["identb"][:])
                        last.then_inc(q2_turned, 1)
                if mid:
                    chunk(NCH - 1)
                if back:
                    pe.wait_ge(x_done, done(j))
                    down(0)
                if front:
                    turn_front(i + 1, 1 - par)
                if back:
                    down(1).then_inc(down_done, 1)

            turn_front(0, 0)
            steps(pe, step)

        @block.scalar
        def _(act):
            for s in (tanh, to_done, qT_done, silu_done, sq_done, t2_done, q2T_done):
                act.sem_inc(s, LEAD)

            def front_tanh(i, par):
                act.wait_ge(x_first if isinstance(i, int) and i < 2 else x_rest, 16)
                act.wait_ge(scaled, done(i))
                nc.scalar.activation(th[:], col(S["x"], i), ACT.Tanh, scale=0.5).then_inc(tanh, 1)

            def front_round(i, par):
                act.wait_ge(scaled, done(i + 1))
                act.wait_ge(q_done, done(i - 1))
                nc.scalar.activation(o[:, par, :], o[:, par, :], ACT.Identity, scale=fs[:, par, 3:4],
                                     bias=S["round"][:, 0:1]).then_inc(to_done, 1)

            def front_copy(i, par):
                act.wait_ge(q_turned, done(i + 1))
                act.wait_ge(up_done, done(i * NCH - NCH))
                nc.scalar.activation(qT[:, par, :, :].rearrange("p k t -> p (k t)"), ps_f[:, 0:512], ACT.Copy).then_inc(qT_done, 1)

            def step(i, par, front, back, mid=True):
                def chunk(n):
                    g = i * NCH + n
                    act.wait_ge(gate_done, done(g + 1))
                    act.wait_ge(h_done, done(g - 1))
                    nc.scalar.activation(sg[:, n % 2, :], ps_gate[n % 2][:], ACT.Silu, scale=fs[:, par, 4:5]).then_inc(silu_done, 1)

                def square(n):
                    g = i * NCH + n
                    act.wait_ge(h_done, done(g + 1))
                    act.wait_ge(sq_done, done(g))
                    nc.scalar.activation(sqj[:], h[:, n % 2, :], ACT.Square, accum_out=ss[:, par, n:n + 1]).then_inc(sq_done, 1)

                def back_copy(hf):
                    act.wait_ge(q2_turned, done(j * 2 + hf + 1))
                    act.wait_ge(down_done, done(j))
                    nc.scalar.activation(q2T[:, hf * 8:hf * 8 + 8, :].rearrange("p k t -> p (k t)"), ps_b[hf][:], ACT.Copy).then_inc(q2T_done, 1)

                j = i - 1
                if front:
                    front_tanh(i + 1, 1 - par)
                if mid:
                    chunk(0)
                if back:
                    act.wait_ge(bs_done, done(j + 1))
                    nc.scalar.activation(hp[:, 1 - par, :], hp[:, 1 - par, :], ACT.Identity, scale=bs[:, 1 - par, 6:7],
                                         bias=S["round"][:, 0:1]).then_inc(t2_done, 1)
                if mid:
                    chunk(1)
                    square(0)
                    chunk(2)
                if back:
                    back_copy(0)
                if front:
                    front_round(i + 1, 1 - par)
                if mid:
                    chunk(3)
                if back:
                    back_copy(1)
                if mid:
                    square(1)
                    square(2)
                if front:
                    front_copy(i + 1, 1 - par)
                if mid:
                    square(3)

            front_tanh(0, 0)
            front_round(0, 0)
            front_copy(0, 0)
            steps(act, step)

        @block.gpsimd
        def _(pool):
            pool.sem_inc(hp_done, LEAD)
            pool.sem_inc(r_done, LEAD)

            def step(i, par, front, back, mid=True):
                if not mid:
                    return
                for n in range(NCH):
                    g = i * NCH + n
                    pool.wait_ge(q2_done, done(i - 1))
                    pool.wait_ge(h_done, done(g + 1))
                    nc.gpsimd.tensor_tensor(hp[:, par, n * 512:(n + 1) * 512], h[:, n % 2, :],
                                            S["ln"][:, n * 512:(n + 1) * 512], ALU.mult).then_inc(hp_done, 1)
                pool.wait_ge(var_done, i + 1)
                nc.gpsimd.tensor_tensor(bs[:, par, 3:4], bs[:, par, 2:3], S["mhalf"][:, 0:1], ALU.pow).then_inc(r_done, 1)

            steps(pool, step)

        @block.vector
        def _(dve):
            for s in (scaled, q_done, h_done, bs_done, q2_done, x_done):
                dve.sem_inc(s, LEAD)
            FRONT, MID = 5, 5

            def link(base, n, ins):
                ins.then_inc(chain, 1)
                dve.wait_ge(chain, base + n)

            def front_mix(i, par):
                base = i * FRONT + (i - 1) * MID if not isinstance(i, int) or i else 0
                dve.wait_ge(tanh, done(i + 1))
                dve.wait_ge(q_done, done(i - 1))
                link(base, 1, nc.vector.scalar_tensor_tensor(out=th[:], in0=th[:], scalar=1.0, in1=col(S["ratio"][0], i),
                                                             op0=ALU.add, op1=ALU.mult))
                link(base, 2, nc.vector.tensor_scalar(o[:, par, :], th[:], S["tfs"][:, bass.ds(i, 1)], None, ALU.mult))

            def front_amax(i, par):
                base = i * FRONT + (i - 1) * MID if not isinstance(i, int) or i else 0
                link(base, 3, nc.vector.tensor_reduce(fs[:, par, 0:1], o[:, par, :], AX.X, ALU.max, apply_absolute_value=True))
                link(base, 4, nc.vector.tensor_scalar(fs[:, par, 1:2], fs[:, par, 0:1], EPS, None, ALU.max))
                nc.vector.tensor_scalar(fs[:, par, 4:5], fs[:, par, 1:2], S["wscale"][:, 0:1], 1.0 / QP, ALU.mult, ALU.mult)
                nc.vector.tensor_scalar(fs[:, par, 5:6], fs[:, par, 1:2], S["wscale"][:, 1:2], 1.0 / QP, ALU.mult, ALU.mult)
                link(base, 5, nc.vector.reciprocal(fs[:, par, 2:3], fs[:, par, 1:2]))
                nc.vector.tensor_scalar(fs[:, par, 3:4], fs[:, par, 2:3], QP, None, ALU.mult).then_inc(scaled, 1)

            def front_quant(i, par):
                dve.wait_ge(to_done, done(i + 1))
                dve.wait_ge(q_turned, done(i - 1))
                nc.vector.tensor_scalar(q[:, par, :], o[:, par, :], -ROUND, QP, ALU.add, ALU.min).then_inc(q_done, 1)

            def step(i, par, front, back, mid=True):
                def chunk(n):
                    g = i * NCH + n
                    dve.wait_ge(silu_done, done(g + 1))
                    dve.wait_ge(up_done, done(g + 1))
                    dve.wait_ge(sq_done, done(g - 1))
                    dve.wait_ge(hp_done, done(g - 1))
                    nc.vector.scalar_tensor_tensor(out=h[:, n % 2, :], in0=ps_up[n % 2][:], scalar=fs[:, par, 5:6],
                                                   in1=sg[:, n % 2, :], op0=ALU.mult, op1=ALU.mult).then_inc(h_done, 1)

                def chunk_max(n):
                    dve.wait_ge(hp_done, done(i * NCH + n + 1))
                    return nc.vector.tensor_reduce(mx[:, par, n:n + 1], hp[:, par, n * 512:(n + 1) * 512], AX.X, ALU.max,
                                                   apply_absolute_value=True)

                j = i - 1
                if mid:
                    chunk(0)
                if front:
                    front_mix(i + 1, 1 - par)
                if back:
                    dve.wait_ge(t2_done, done(j + 1))
                    dve.wait_ge(q2_turned, done(j * 2))
                    nc.vector.tensor_scalar(q2[:], hp[:, 1 - par, :], -ROUND, QP, ALU.add, ALU.min).then_inc(q2_done, 1)
                if mid:
                    chunk(1)
                if front:
                    front_amax(i + 1, 1 - par)
                if mid:
                    chunk(2)
                if front:
                    front_quant(i + 1, 1 - par)
                if mid:
                    chunk_max(0)
                    chunk(3)
                    chunk_max(1)
                    chunk_max(2)
                    base = (i + (2 if front else 1)) * FRONT + i * MID
                    dve.wait_ge(sq_done, done(i * NCH + NCH))
                    link(base, 1, nc.vector.tensor_reduce(bs[:, par, 0:1], ss[:, par, :], AX.X, ALU.add))
                    nc.vector.tensor_scalar(bs[:, par, 2:3], bs[:, par, 0:1], 1.0 / INNER, RMS_EPS, ALU.mult, ALU.add).then_inc(var_done, 1)
                    link(base, 2, chunk_max(3))
                    link(base, 3, nc.vector.tensor_reduce(bs[:, par, 1:2], mx[:, par, :], AX.X, ALU.max))
                    dve.wait_ge(r_done, done(i + 1))
                    link(base, 4, nc.vector.tensor_scalar(bs[:, par, 4:5], bs[:, par, 1:2], bs[:, par, 3:4], EPS, ALU.mult, ALU.max))
                    nc.vector.tensor_scalar(bs[:, par, 7:8], bs[:, par, 4:5], S["wscale"][:, 2:3], 1.0 / QP, ALU.mult, ALU.mult)
                    link(base, 5, nc.vector.reciprocal(bs[:, par, 5:6], bs[:, par, 4:5]))
                    nc.vector.tensor_scalar(bs[:, par, 6:7], bs[:, par, 5:6], bs[:, par, 3:4], QP, ALU.mult, ALU.mult).then_inc(bs_done, 1)
                if back:
                    dve.wait_ge(down_done, done(j + 1))
                    nc.vector.scalar_tensor_tensor(out=col(S["x"], j), in0=ps_y[:], scalar=bs[:, 1 - par, 7:8],
                                                   in1=col(S["x"], j), op0=ALU.mult, op1=ALU.add).then_inc(x_done, 1)

            front_mix(0, 0)
            front_amax(0, 0)
            front_quant(0, 0)
            steps(dve, step)


def route(nc, A, S):
    with ExitStack() as ctx:
        def sb(name, shape, dt):
            return ctx.enter_context(nc.sbuf_tensor(name, shape, dt))

        def sem(name):
            return ctx.enter_context(nc.semaphore(name))

        RANK = P * 4
        assert RANK == E * JT
        th = sb("r_tanh", [P, 2, C], F32)
        t1 = sb("r_gated", [P, 2, C], F32)
        o = sb("r_mixed", [P, 2, C], F32)
        oT = sb("r_mixed_T", [P, 2, CT, P], F32)
        score = sb("score", [P, 2, E], F32)
        top = sb("top", [P, 2, 8], F32)
        topi = sb("top_index", [P, 2, 8], U32)
        expert = sb("expert", [P, 2, K], F32)
        hot = sb("one_hot", [P, TILES, K, E], F32)
        hot2 = sb("one_hot_times", [P, TILES, K, E], F32)
        chosen = sb("chosen", [P, 2, E], F32)
        before = sb("before", [P, 2, E], F32)
        rank = sb("rank", [P, TILES, K], I32)
        high = sb("rank_high", [P, 2, K], I32)
        placef = sb("place_f", [P, 2, K], F32)
        place = [sb(f"place{i}", [P, K], U32) for i in range(2)]
        token = [sb(f"token_of{i}", [P, 1], U32) for i in range(2)]
        slotf = sb("slot_f", [P, TILES, K], F32)
        lmax = sb("logit_max", [P, TILES], F32)
        shifted = sb("logit_shifted", [P, TILES, E], F32)
        cnti = sb("count_int", [P, E], I32)
        ntf = sb("tiles_f", [P, E], F32)
        onesr = sb("ones_row", [P, E], F32)
        cum = sb("tiles_until_f", [P, E], F32)
        base = sb("first_row", [P, E], F32)
        tile = sb("tile_number", [P, 1], F32)
        passed = sb("tile_passed", [P, E], F32)
        passed_n = sb("tile_passed_n", [P, E], F32)
        tab = sb("tile_table", [P, 3], F32)
        start = sb("tile_start", [P, 1], F32)
        within = sb("tile_within", [P, 1], F32)
        first = sb("tile_first", [P, 1], F32)
        valid = sb("tile_valid", [P, 1], F32)
        endf = sb("tile_end_f", [1, 1], F32)
        endi = sb("tile_end_int", [1, 1], I32)
        ps_o = [ctx.enter_context(nc.psum_tensor(f"ps_mixed_T{i}", [P, 512], F32)) for i in range(2)]
        ps_l = [ctx.enter_context(nc.psum_tensor(f"ps_logits{i}", [P, E], F32)) for i in range(2)]
        ps_r = [ctx.enter_context(nc.psum_tensor(f"ps_rank{i}", [P, E], F32)) for i in range(2)]
        ps_c = ctx.enter_context(nc.psum_tensor("ps_count", [P, E], F32))
        ps_tab = ctx.enter_context(nc.psum_tensor("ps_table", [P, 3 * P], F32))

        tanh = sem("r_tanh_done")
        gated = sem("r_gated_done")
        mixed = sem("r_mixed_done")
        turned = sem("r_turned")
        oT_done = sem("r_T_done")
        logits = sem("r_logits")
        scored = sem("r_scored")
        routed = sem("r_chosen")
        ranked = sem("r_ranked")
        chain = sem("r_chain")
        passing = sem("r_passing")
        placed = sem("r_placed")
        zeroed = sem("r_lists_zeroed")
        cleared = sem("r_before_cleared")
        named = sem("r_token_named")
        named_ready = sem("r_token_ready")
        stored = [sem(f"r_stored{i}") for i in range(2)]
        scattered = [sem(f"r_scattered{i}") for i in range(2)]
        counted = sem("r_counted")
        shift = sem("r_shift")
        tabled = sem("r_tabled")
        tab_turned = sem("r_table_turned")
        seq = sem("r_seq")
        listed = sem("r_listed")

        def steps(eng, step):
            step(0, 0, 0)
            step(1, 1, 0)
            with eng.Fori(1, TILES // 2 - 2) as ii:
                step(ii * 2, 0, ii)
                step(ii * 2 + 1, 1, ii)
            for left in range(4, 0, -1):
                step(TILES - left, left % 2, TILES // 2 - (left + 1) // 2, ahead=left - 1)

        def col(ap, i):
            return ap[:, bass.ds(i, 1), :].rearrange("p a c -> p (a c)")

        block = ctx.enter_context(nc.Block())

        @block.sync
        def _(sp):
            for s in stored:
                sp.sem_inc(s, 16)
            sp.dma_start(S["lists"].rearrange("(p a) b -> p (a b)", p=P), S["zrow"][:]).then_inc(zeroed, 16)

            def step(i, par, ii):
                sp.wait_ge(mixed, done(i + 1))
                sp.dma_start(S["rows"][bass.ds(i * P, P), :], o[:, par, :]).then_inc(stored[par], 16)

            with sp.Fori(0, TILES // 2) as ii:
                step(ii * 2, 0, ii)
                step(ii * 2 + 1, 1, ii)
            for s in scattered:
                sp.wait_ge(s, 64 * (TILES // 2))
            sp.dma_start(S["list"][:], S["lists"].rearrange("(p a) b -> p (a b)", p=P)).then_inc(listed, 16)
            for s in stored:
                sp.wait_ge(s, 16 + 16 * (TILES // 2))
            sp.wait_ge(listed, 16)

        @block.gpsimd
        def _(pool):
            pool.sem_inc(named, LEAD)
            pool.wait_ge(zeroed, 16)

            def step(i, par, ii):
                if not isinstance(i, int):
                    pool.wait_ge(scattered[par], ii * 64)
                nc.gpsimd.tensor_copy(token[par][:], S["token"][:, bass.ds(i, 1)]).then_inc(named, 1)
                pool.wait_ge(named, done(i + 1))
                pool.wait_ge(placed, done(i + 1))
                pool.sem_inc(named_ready, 1)
                for k in range(K):
                    nc.gpsimd.indirect_dma_start(S["lists"], bass.IndirectOffsetOnAxis(place[par][:, k:k + 1], 0),
                                                 token[par][:], None, bounds_check=P * 512 - 1).then_inc(scattered[par], 16)

            step(0, 0, 0)
            step(1, 1, 0)
            with pool.Fori(1, TILES // 2) as ii:
                step(ii * 2, 0, ii)
                step(ii * 2 + 1, 1, ii)

        @block.scalar
        def _(act):
            for s in (tanh, oT_done, scored):
                act.sem_inc(s, LEAD)

            def gate_tanh(i, par):
                act.wait_ge(gated, done(i - 1))
                nc.scalar.activation(th[:, par, :], col(S["x"], i), ACT.Tanh, scale=0.5).then_inc(tanh, 1)

            def turned_out(i, par):
                act.wait_ge(turned, done(i + 1))
                act.wait_ge(logits, done(i - 1))
                nc.scalar.activation(oT[:, par, :, :].rearrange("p k t -> p (k t)"), ps_o[par][:], ACT.Copy).then_inc(oT_done, 1)

            def score_of(i, par):
                act.wait_ge(logits, done(i + 1))
                act.wait_ge(routed, done(i - 1))
                nc.scalar.activation(score[:, par, :], ps_l[par][:], ACT.Tanh, scale=0.5)
                nc.scalar.activation(col(S["logits"], i), ps_l[par][:], ACT.Copy).then_inc(scored, 1)

            def step(i, par, ii, ahead=3):
                if ahead >= 1:
                    score_of(i + 1, 1 - par)
                if ahead >= 3:
                    gate_tanh(i + 3, 1 - par)
                if ahead >= 2:
                    turned_out(i + 2, par)

            gate_tanh(0, 0)
            gate_tanh(1, 1)
            turned_out(0, 0)
            score_of(0, 0)
            gate_tanh(2, 0)
            turned_out(1, 1)
            steps(act, step)
            act.wait_ge(shift, 1)
            nc.scalar.activation(S["logits"][:], shifted[:], ACT.Exp)

        @block.tensor
        def _(pe):
            for s in (turned, logits, ranked):
                pe.sem_inc(s, LEAD)
            pe.wait_ge(cleared, 1)

            def turn(i, par):
                pe.wait_ge(mixed, done(i + 1))
                pe.wait_ge(oT_done, done(i - 1))
                for k in range(CT):
                    last = nc.tensor.transpose(ps_o[par][:, k * P:(k + 1) * P], o[:, par, k * P:(k + 1) * P], S["ident"][:])
                last.then_inc(turned, 1)

            def logits_of(i, par):
                pe.wait_ge(oT_done, done(i + 1))
                pe.wait_ge(scored, done(i - 1))
                for k in range(CT):
                    last = nc.tensor.matmul(ps_l[par][:], oT[:, par, k, :], S["gate_wT"][:, k, :], start=(k == 0), stop=(k == CT - 1))
                last.then_inc(logits, 1)

            def step(i, par, ii, ahead=3):
                if ahead >= 1:
                    logits_of(i + 1, 1 - par)
                pe.wait_ge(routed, done(i + 1))
                nc.tensor.matmul(ps_r[par][:], S["tri"][:], chosen[:, par, :], start=True, stop=False)
                nc.tensor.matmul(ps_r[par][:], S["ones"][:], before[:, par, :], start=False, stop=True).then_inc(ranked, 1)
                if ahead >= 2:
                    turn(i + 2, par)

            turn(0, 0)
            logits_of(0, 0)
            turn(1, 1)
            steps(pe, step)
            pe.wait_ge(counted, 1)
            nc.tensor.matmul(ps_c[:], S["ones"][:], before[:, 0, :], start=True, stop=True).then_inc(counted, 1)
            pe.wait_ge(tabled, 1)
            for k in range(3):
                last = nc.tensor.transpose(ps_tab[0:1, k * P:(k + 1) * P], tab[:, k:k + 1], S["ident"][:])
            last.then_inc(tab_turned, 1)

        @block.vector
        def _(dve):
            v = nc.vector
            for s in (gated, mixed, routed, placed):
                dve.sem_inc(s, LEAD)
            v.memset(before[:, 0, :], 0.0).then_inc(cleared, 1)
            dve.wait_ge(cleared, 1)

            def gate(i, par, ii):
                dve.wait_ge(tanh, done(i + 1))
                v.scalar_tensor_tensor(out=t1[:, par, :], in0=th[:, par, :], scalar=1.0, in1=col(S["ratio"][1], i),
                                       op0=ALU.add, op1=ALU.mult).then_inc(gated, 1)
                dve.wait_ge(gated, done(i + 1))
                dve.wait_ge(turned, done(i - 1))
                dve.wait_ge(stored[par], ii * 16 + 16)
                v.tensor_scalar(o[:, par, :], t1[:, par, :], S["tfs"][:, bass.ds(i, 1)], None, ALU.mult).then_inc(mixed, 1)

            LINKS = 8

            def step(i, par, ii, ahead=3):
                links = [0]

                def link(ins, bare=True):
                    links[0] += 1
                    ins.then_inc(chain, 1)
                    dve.wait_ge(chain, i * LINKS + links[0])
                    if not bare:
                        dve.sem_inc(passing, 1)

                here = hot[:, bass.ds(i, 1), :, :].rearrange("p a k e -> p (a k) e")
                times = hot2[:, par, :, :]
                ranks = rank[:, bass.ds(i, 1), :].rearrange("p a k -> p (a k)")
                dve.wait_ge(scored, done(i + 1))
                link(v.tensor_scalar(score[:, par, :], score[:, par, :], 0.5, 0.5, ALU.mult, ALU.add), bare=False)
                link(v.max(top[:, par, :], score[:, par, :]), bare=False)
                link(v.max_index(topi[:, par, :], top[:, par, :], score[:, par, :]))
                link(v.tensor_copy(expert[:, par, :], topi[:, par, 0:K]))
                link(v.tensor_tensor(here, S["iota_e"][:].unsqueeze(1).to_broadcast([P, K, E]),
                                     expert[:, par, :].unsqueeze(2).to_broadcast([P, K, E]), ALU.is_equal), bare=False)
                v.tensor_reduce(chosen[:, par, :], here.rearrange("p k e -> p e k"), AX.X, ALU.add).then_inc(routed, 1)
                dve.wait_ge(ranked, done(i))
                dve.wait_ge(routed, done(i + 1))
                v.scalar_tensor_tensor(out=before[:, 1 - par, :], in0=chosen[:, par, :], scalar=float(RANK),
                                       in1=before[:, par, :], op0=ALU.mult, op1=ALU.add)
                if ahead >= 2:
                    gate(i + 2, par, ii + 1)
                dve.wait_ge(ranked, done(i + 1))
                link(v.tensor_tensor(times, here, ps_r[par][:].unsqueeze(1).to_broadcast([P, K, E]), ALU.mult), bare=False)
                with nc.allow_low_precision("one non-zero integer below 2**24 in each sum"):
                    link(v.tensor_reduce(ranks, times, AX.X, ALU.add))
                v.scalar_tensor_tensor(out=placef[:, par, :], in0=expert[:, par, :], scalar=float(JT), in1=ranks,
                                       op0=ALU.mult, op1=ALU.add)
                v.tensor_copy(col(S["expert"], i), expert[:, par, :])
                link(v.tensor_scalar(high[:, par, :], ranks, 16, None, ALU.logical_shift_right))
                if not isinstance(i, int) or i >= 2:
                    dve.wait_ge(scattered[par], ii * 64)
                v.scalar_tensor_tensor(out=place[par][:], in0=high[:, par, :], scalar=-float(P * RANK - 1),
                                       in1=placef[:, par, :], op0=ALU.mult, op1=ALU.add).then_inc(placed, 1)

            gate(0, 0, 0)
            gate(1, 1, 0)
            steps(dve, step)
            dve.wait_ge(placed, done(TILES))
            dve.sem_inc(counted, 1)

            count = [0]

            def then(ins):
                count[0] += 1
                ins.then_inc(seq, 1)
                dve.wait_ge(seq, count[0])

            v.memset(onesr[:], 1.0)
            then(v.tensor_copy(tile[:], S["token"][:, 0:1]))
            dve.wait_ge(counted, 2)
            then(v.tensor_scalar(cnti[:], ps_c[:], 1.0 / RANK, float(P - 1), ALU.mult, ALU.add))
            then(v.tensor_scalar(cnti[:], cnti[:], 7, None, ALU.logical_shift_right))
            then(v.tensor_scalar(ntf[:], cnti[:], 1.0, None, ALU.max))
            then(v.tensor_tensor_scan(cum[:], onesr[:], ntf[:], 0.0, ALU.mult, ALU.add))
            v.tensor_tensor(base[:], cum[:], ntf[:], ALU.subtract)
            then(v.tensor_scalar(passed[:], cum[:], tile[:, 0:1], None, ALU.is_le))
            v.tensor_reduce(tab[:, 0:1], passed[:], AX.X, ALU.add)
            then(v.tensor_tensor(passed_n[:], passed[:], ntf[:], ALU.mult))
            then(v.tensor_reduce(start[:], passed_n[:], AX.X, ALU.add))
            v.tensor_scalar(tab[:, 0:1], tab[:, 0:1], float(E - 1), None, ALU.min)
            then(v.tensor_tensor(within[:], tile[:], start[:], ALU.subtract))
            v.tensor_scalar(first[:], within[:], 0.0, None, ALU.is_equal)
            v.tensor_scalar(valid[:], tab[:, 0:1], float(E - 3), None, ALU.is_le)
            then(v.tensor_scalar(within[:], within[:], float(JT - 1), None, ALU.min))
            v.scalar_tensor_tensor(out=tab[:, 1:2], in0=tab[:, 0:1], scalar=float(JT), in1=within[:], op0=ALU.mult, op1=ALU.add)
            then(v.tensor_tensor(valid[:], valid[:], first[:], ALU.mult))
            v.scalar_tensor_tensor(out=tab[:, 2:3], in0=tab[:, 0:1], scalar=2.0, in1=valid[:], op0=ALU.add, op1=ALU.mult).then_inc(tabled, 1)
            then(v.tensor_scalar(endf[:], cum[0:1, E - 1:E], 1.0, None, ALU.add))
            then(v.tensor_copy(endi[:], endf[:]))
            v.tensor_scalar(S["tile_end"][:], endi[:], 1, 1, ALU.logical_shift_right, ALU.logical_shift_left)
            then(v.tensor_reduce(lmax[:], S["logits"][:], AX.X, ALU.max))
            v.tensor_tensor(shifted[:], S["logits"][:], lmax[:].unsqueeze(2).to_broadcast([P, TILES, E]), ALU.subtract).then_inc(shift, 1)
            dve.wait_ge(tab_turned, 1)
            for k, name in enumerate(("tile_expert", "tile_col", "tile_next")):
                v.tensor_copy(S[name][:], ps_tab[0:1, k * P:(k + 1) * P])

            for i in range(TILES):
                last = v.tensor_tensor(hot2[:, i, :, :], hot[:, i, :, :], base[:].unsqueeze(1).to_broadcast([P, K, E]), ALU.mult)
            then(last)
            then(v.tensor_reduce(slotf[:], hot2[:], AX.X, ALU.add))
            then(v.tensor_scalar(slotf[:], slotf[:], float(P * RANK), None, ALU.mult))
            then(v.tensor_tensor(slotf[:], slotf[:], rank[:], ALU.add))
            v.tensor_scalar(S["slot"][:], slotf[:], 1.0 / RANK, None, ALU.mult)


def experts(nc, A, S):
    with ExitStack() as ctx:
        def sb(name, shape, dt):
            return ctx.enter_context(nc.sbuf_tensor(name, shape, dt))

        def ps(name, shape, dt):
            return ctx.enter_context(nc.psum_tensor(name, shape, dt))

        def sem(name):
            return ctx.enter_context(nc.semaphore(name))

        SLOTS = 3
        REST = LARGE - P
        gu_hi = sb("e_gate_up_high", [P, SLOTS, 2, CT, WIDE], F32R)
        gu_lo = sb("e_gate_up_low", [P, SLOTS, 2, CT, WIDE], F32R)
        d_hi = sb("e_down_high", [P, SLOTS, 3, C], F32R)
        d_lo = sb("e_down_low", [P, SLOTS, 3, C], F32R)
        st_gu = sb("e_stage_gate_up", [P, 2, 2, CT, LARGE], F32)
        st_d = sb("e_stage_down", [P, 2, 2, C], F32)
        st_sgu = sb("e_stage_small_gate_up", [P, 2, 2, CT, SMALL], F32)
        st_sd = sb("e_stage_small_down", [P, 2, C], F32)
        idx = sb("e_index", [P, 2], U32)
        x = sb("e_rows", [P, 2, C], F32)
        xh = sb("e_rows_T_high", [P, 2, CT * P], F32R)
        xl = sb("e_rows_T_low", [P, 2, CT * P], F32R)
        sg = sb("e_silu", [P, 2, WIDE], F32)
        a = sb("e_hidden", [P, 2, WIDE], F32)
        ah = sb("e_hidden_T_high", [P, 2, 3 * P], F32R)
        al = sb("e_hidden_T_low", [P, 2, 3 * P], F32R)
        y = sb("e_out", [P, 2, C], F32)
        ps_x = ps("ps_rows_T", [P, 512], F32)
        ps_g = [ps(f"ps_e_gate{i}", [P, WIDE], F32) for i in range(2)]
        ps_u = [ps(f"ps_e_up{i}", [P, WIDE], F32) for i in range(2)]
        ps_a = ps("ps_hidden_T", [P, 3 * P], F32)
        ps_y = [ps(f"ps_e_out{i}", [P, C], F32) for i in range(2)]

        large_in = [sem(f"e_large_in{i}") for i in range(2)]
        small_in = [sem(f"e_small_in{i}") for i in range(2)]
        staged = sem("e_staged")
        high = [sem(f"e_{n}_high_done") for n in ("gate", "up", "down")]
        low = [sem(f"e_{n}_low_done") for n in ("gate", "up", "down")]
        gate_low, up_low, d_low = low
        indexed = sem("e_indexed")
        index_ready = sem("e_index_ready")
        gathered = [sem(f"e_gathered{i}") for i in range(2)]
        turned = sem("e_turned")
        xh_done = sem("e_rows_T_high_done")
        xl_done = sem("e_rows_T_low_done")
        gate_done = sem("e_gate_done")
        up_done = sem("e_up_done")
        silu_done = sem("e_silu_done")
        a_done = sem("e_hidden_done")
        a_turned = sem("e_hidden_turned")
        ah_done = sem("e_hidden_T_high_done")
        al_done = sem("e_hidden_T_low_done")
        down_done = sem("e_down_done")
        y_done = sem("e_out_done")
        stored = [sem(f"e_stored{i}") for i in range(2)]
        filled = sem("e_filled")
        all_stored = sem("e_all_stored")

        def look(eng, table, t, low, top):
            return eng.value_load(table[0:1, bass.ds(t, 1)], min_val=low, max_val=top)

        def steps(eng, step):
            end = look(eng, S["tile_end"], 0, E, LISTED)
            step(0, 0, 0, prev=False)
            step(1, 1, 0)
            step(2, 0, 1)
            step(3, 1, 1)
            with eng.Fori(1, E // 4) as two:
                for n in range(4):
                    step(two * 4 + n, n % 2, two * 2 + n // 2)
            with eng.Fori(E // 4, LISTED // 4) as two:
                for n in range(2):
                    with eng.If(end > two * 4 + n * 2):
                        for par in range(2):
                            step(two * 4 + n * 2 + par, par, two * 2 + n)
            step(end, 0, end // 2, nxt=False, mid=False)
            return end

        GATE, UP, DOWN = range(3)

        def called_for(eng, t, prepare, part):
            n = look(eng, S["tile_next"], t, 0, E - 1)
            with eng.If(n > 0):
                prepare(n, part, t)

        def pieces(e, part):
            st, slot, sst = e % 2, e % SLOTS, (e // 2) % 2
            if part < DOWN:
                for stage, i, lo, hi in ((st_gu, st, 0, LARGE), (st_sgu, sst, LARGE, WIDE)):
                    yield (stage[:, bass.ds(i, 1), part, :, :].rearrange("p a k n -> p (a k) n"),
                           gu_hi[:, bass.ds(slot, 1), part, :, lo:hi].rearrange("p a k n -> p (a k) n"),
                           gu_lo[:, bass.ds(slot, 1), part, :, lo:hi].rearrange("p a k n -> p (a k) n"))
            else:
                for n, stage, k in ((P, st_d[:, bass.ds(st, 1), 0, :], 0), (P, st_sd[:, bass.ds(sst, 1), :], 1),
                                    (REST, st_d[0:REST, bass.ds(st, 1), 1, :], 2)):
                    yield stage, d_hi[0:n, bass.ds(slot, 1), k, :], d_lo[0:n, bass.ds(slot, 1), k, :]

        block = ctx.enter_context(nc.Block())

        @block.sync
        def _(sp):
            def rows(ap, i):
                return ap[bass.ds(i, 1), :, :].rearrange("a (k p) n -> p (a k) n", p=P)

            def load(e, st, pair, sst, before):
                sp.wait_ge(up_low, done(e - 1))
                if st == 0:
                    for n, name in enumerate(("L1_ffn_cWg", "L1_ffn_cWu")):
                        sp.dma_start(st_sgu[:, sst, n, :, :], rows(A[name], pair)).then_inc(small_in[sst], 16)
                for n, name in enumerate(("L1_ffn_Wg", "L1_ffn_Wu")):
                    sp.dma_start(st_gu[:, st, n, :, :], rows(A[name], e)).then_inc(large_in[st], 16)
                if before:
                    landed(*before)
                sp.wait_ge(d_low, done(e - 1))
                if st == 0:
                    sp.dma_start(st_sd[:, sst, :], A["L1_ffn_cWd"][bass.ds(pair, 1), :, :].rearrange("a i n -> (a i) n")).then_inc(small_in[sst], 16)
                down = A["L1_ffn_Wd"][bass.ds(e, 1), :, :].rearrange("a i n -> (a i) n")
                sp.dma_start(st_d[:, st, 0, :], down[0:P, :]).then_inc(large_in[st], 16)
                sp.dma_start(st_d[0:REST, st, 1, :], down[P:LARGE, :]).then_inc(large_in[st], 16)

            def landed(four, n):
                sp.wait_ge(large_in[n % 2], four * 128 + (n // 2 + 1) * 64)
                sp.wait_ge(small_in[n // 2], four * 48 + 48)
                sp.sem_inc(staged, 1)

            load(0, 0, 0, 0, None)
            for n in range(1, 4):
                load(n, n % 2, n // 2, n // 2, (0, n - 1))
            with sp.Fori(1, E // 4) as four:
                for n in range(4):
                    load(four * 4 + n, n % 2, four * 2 + n // 2, n // 2, (four, n - 1) if n else (four - 1, 3))
            landed(E // 4 - 1, 3)
            end = look(sp, S["tile_end"], 0, E, LISTED)
            with sp.Fori(E // 2, LISTED // 2) as tt:
                with sp.If(end <= tt * 2):
                    for i in range(2):
                        sp.dma_start(S["results"][bass.ds(tt * (2 * P) + i * P, P), :], S["zrow"][:].bitcast(F32)).then_inc(filled, 16)
                with sp.If(end > tt * 2):
                    sp.sem_inc(filled, 32)
            sp.wait_ge(filled, (LISTED - E) * 16)

        @block.gpsimd
        def _(pool):
            pool.sem_inc(indexed, LEAD)

            def gather(t, par):
                c = look(pool, S["tile_col"], t, 0, E * JT - 1)
                pool.wait_ge(turned, done(t - 1))
                nc.gpsimd.tensor_copy(idx[:, par:par + 1], S["list"][:, bass.ds(c, 1)]).then_inc(indexed, 1)
                pool.wait_ge(indexed, done(t + 1))
                pool.sem_inc(index_ready, 1)
                nc.gpsimd.indirect_dma_start(x[:, par, :], None, S["rows"], bass.IndirectOffsetOnAxis(idx[:, par:par + 1], 0),
                                             bounds_check=TOKENS - 1).then_inc(gathered[par], 16)

            end = look(pool, S["tile_end"], 0, E, LISTED)
            gather(0, 0)
            gather(1, 1)
            gather(2, 0)
            with pool.Fori(1, LISTED // 2) as tt:
                with pool.If(end > tt * 2):
                    gather(tt * 2 + 1, 1)
                    gather(tt * 2 + 2, 0)

        @block.tensor
        def _(pe):
            for s in (turned, gate_done, up_done, a_turned, down_done):
                pe.sem_inc(s, LEAD)

            def turn(t, par, tt):
                pe.wait_ge(gathered[par], tt * 16 + 16)
                pe.wait_ge(xl_done, done(t))
                for k in range(CT):
                    last = nc.tensor.transpose(ps_x[:, k * P:(k + 1) * P], x[:, par, k * P:(k + 1) * P], S["ident"][:])
                last.then_inc(turned, 1)

            def products(out, lhs_hi, lhs_lo, rhs_hi, rhs_lo, parts):
                for k, n in enumerate(parts):
                    at = slice(k * P, (k + 1) * P)
                    nc.tensor.matmul(out, lhs_hi[0:n, at], rhs_hi(k, n), start=(k == 0), stop=False)
                    nc.tensor.matmul(out, lhs_hi[0:n, at], rhs_lo(k, n), start=False, stop=False)
                    last = nc.tensor.matmul(out, lhs_lo[0:n, at], rhs_hi(k, n), start=False, stop=(k == len(parts) - 1))
                return last

            def gate_up(w, slot, which):
                return lambda k, n: w[:, bass.ds(slot, 1), which, k, :].rearrange("p a n -> p (a n)")

            def down(w, slot):
                return lambda k, n: w[0:n, bass.ds(slot, 1), k, :].rearrange("p a n -> p (a n)")

            def step(t, par, tt, nxt=True, prev=True, mid=True):
                if mid:
                    e = look(pe, S["tile_expert"], t, 0, E - 1)
                    slot = e % SLOTS
                if prev:
                    e_prev = look(pe, S["tile_expert"], t - 1, 0, E - 1)
                    slot_prev = e_prev % SLOTS
                if nxt:
                    turn(t + 1, 1 - par, tt + par)
                if prev:
                    pe.wait_ge(a_done, done(t))
                    pe.wait_ge(al_done, done(t - 1))
                    nc.tensor.transpose(ps_a[:, 0:P], a[:, 1 - par, 0:P], S["ident"][:])
                    nc.tensor.transpose(ps_a[:, P:2 * P], a[:, 1 - par, LARGE:WIDE], S["ident"][:])
                    nc.tensor.transpose(ps_a[0:REST, 2 * P:3 * P], a[:, 1 - par, P:LARGE], S["ident"][:]).then_inc(a_turned, 1)
                if mid:
                    pe.wait_ge(gate_low, done(e + 1))
                    pe.wait_ge(xl_done, done(t + 1))
                    pe.wait_ge(silu_done, done(t - 1))
                    products(ps_g[par][:], xh[:, par, :], xl[:, par, :], gate_up(gu_hi, slot, 0), gate_up(gu_lo, slot, 0),
                             [P] * CT).then_inc(gate_done, 1)
                    pe.wait_ge(up_low, done(e + 1))
                    pe.wait_ge(a_done, done(t - 1))
                    products(ps_u[par][:], xh[:, par, :], xl[:, par, :], gate_up(gu_hi, slot, 1), gate_up(gu_lo, slot, 1),
                             [P] * CT).then_inc(up_done, 1)
                if prev:
                    pe.wait_ge(d_low, done(e_prev + 1))
                    pe.wait_ge(al_done, done(t))
                    pe.wait_ge(y_done, done(t - 2))
                    products(ps_y[1 - par][:], ah[:, 1 - par, :], al[:, 1 - par, :], down(d_hi, slot_prev), down(d_lo, slot_prev),
                             [P, P, REST]).then_inc(down_done, 1)

            turn(0, 0, 0)
            steps(pe, step)

        @block.scalar
        def _(act):
            for s in (*high, xh_done, silu_done, ah_done, y_done):
                act.sem_inc(s, LEAD)
            for s in stored:
                act.sem_inc(s, 16)

            def prepare_high(e, part, t):
                act.wait_ge(staged, e + 1)
                act.wait_ge(down_done if part == DOWN else up_done, done(t))
                for src, hi, lo in pieces(e, part):
                    last = nc.scalar.activation(hi, src, ACT.Copy)
                last.then_inc(high[part], 1)

            def rows_high(t, par):
                act.wait_ge(turned, done(t + 1))
                act.wait_ge(up_done, done(t - 1))
                nc.scalar.activation(xh[:, par, :], ps_x[:], ACT.Copy).then_inc(xh_done, 1)

            def step(t, par, tt, nxt=True, prev=True, mid=True):
                if nxt:
                    rows_high(t + 1, 1 - par)
                if prev:
                    act.wait_ge(a_turned, done(t))
                    act.wait_ge(down_done, done(t - 2))
                    nc.scalar.activation(ah[:, 1 - par, 0:2 * P], ps_a[:, 0:2 * P], ACT.Copy)
                    nc.scalar.activation(ah[0:REST, 1 - par, 2 * P:3 * P], ps_a[0:REST, 2 * P:3 * P], ACT.Copy).then_inc(ah_done, 1)
                if mid:
                    called_for(act, t, prepare_high, GATE)
                    act.wait_ge(gate_done, done(t + 1))
                    act.wait_ge(a_done, done(t - 1))
                    nc.scalar.activation(sg[:, par, :], ps_g[par][:], ACT.Silu).then_inc(silu_done, 1)
                if mid:
                    called_for(act, t, prepare_high, UP)
                if mid and prev:
                    called_for(act, t - 1, prepare_high, DOWN)
                if prev:
                    act.wait_ge(down_done, done(t))
                    act.wait_ge(stored[1 - par], tt * 16 + par * 16)
                    nc.scalar.activation(y[:, 1 - par, :], ps_y[1 - par][:], ACT.Copy).then_inc(y_done, 1)
                    act.wait_ge(y_done, done(t))
                    act.dma_start(S["results"][bass.ds((t - 1) * P, P), :], y[:, 1 - par, :]).then_inc(stored[1 - par], 16)

            for part in (GATE, UP, DOWN):
                prepare_high(0, part, 0)
            rows_high(0, 0)
            for part in (GATE, UP, DOWN):
                prepare_high(1, part, 0)
            end = steps(act, step)
            for s in stored:
                act.wait_ge(s, 16 + end * 8)
            act.sem_inc(all_stored, 1)

        @block.vector
        def _(dve):
            for s in (*low, xl_done, a_done, al_done):
                dve.sem_inc(s, LEAD)

            def prepare_low(e, part, t):
                dve.wait_ge(high[part], done(e + 1))
                for src, hi, lo in pieces(e, part):
                    last = nc.vector.tensor_tensor(lo, src, hi.bitcast(F32), ALU.subtract)
                last.then_inc(low[part], 1)

            def rows_low(t, par):
                dve.wait_ge(xh_done, done(t + 1))
                nc.vector.tensor_tensor(xl[:, par, :], ps_x[:], xh[:, par, :].bitcast(F32), ALU.subtract).then_inc(xl_done, 1)

            def step(t, par, tt, nxt=True, prev=True, mid=True):
                if nxt:
                    rows_low(t + 1, 1 - par)
                if prev:
                    dve.wait_ge(ah_done, done(t))
                    nc.vector.tensor_tensor(al[:, 1 - par, 0:2 * P], ps_a[:, 0:2 * P], ah[:, 1 - par, 0:2 * P].bitcast(F32), ALU.subtract)
                    nc.vector.tensor_tensor(al[0:REST, 1 - par, 2 * P:3 * P], ps_a[0:REST, 2 * P:3 * P],
                                            ah[0:REST, 1 - par, 2 * P:3 * P].bitcast(F32), ALU.subtract).then_inc(al_done, 1)
                if mid:
                    called_for(dve, t, prepare_low, GATE)
                if mid:
                    dve.wait_ge(silu_done, done(t + 1))
                    dve.wait_ge(up_done, done(t + 1))
                    dve.wait_ge(a_turned, done(t - 1))
                    nc.vector.tensor_tensor(a[:, par, 0:LARGE], ps_u[par][:, 0:LARGE], sg[:, par, 0:LARGE], ALU.mult)
                    nc.vector.scalar_tensor_tensor(out=a[:, par, LARGE:WIDE], in0=ps_u[par][:, LARGE:WIDE], scalar=SMALL_SCALE,
                                                   in1=sg[:, par, LARGE:WIDE], op0=ALU.mult, op1=ALU.mult).then_inc(a_done, 1)
                if mid:
                    called_for(dve, t, prepare_low, UP)
                if mid and prev:
                    called_for(dve, t - 1, prepare_low, DOWN)

            for part in (GATE, UP, DOWN):
                prepare_low(0, part, 0)
            rows_low(0, 0)
            for part in (GATE, UP, DOWN):
                prepare_low(1, part, 0)
            steps(dve, step)


def combine(nc, A, S, out):
    with ExitStack() as ctx:
        def sb(name, shape, dt):
            return ctx.enter_context(nc.sbuf_tensor(name, shape, dt))

        def sem(name):
            return ctx.enter_context(nc.semaphore(name))

        DEPTH = 4
        hot = sb("c_one_hot", [P, TILES, K, E], F32)
        times = sb("c_one_hot_times", [P, TILES, K, E], F32)
        z = sb("c_softmax_sum", [P, TILES], F32)
        rz = sb("c_softmax_rsum", [P, TILES], F32)
        prob = sb("c_prob", [P, TILES, E], F32)
        wsum = sb("c_chosen_sum", [P, TILES], F32)
        rwsum = sb("c_chosen_rsum", [P, TILES], F32)
        weight = sb("c_weight", [P, TILES, K], F32)
        row = [[sb(f"c_row{d}{k}", [P, C], F32) for k in range(K)] for d in range(DEPTH)]
        fetched = [[sem(f"c_fetched{d}{k}") for k in range(K)] for d in range(DEPTH)]
        added = sem("c_added")
        stored = sem("c_stored")
        seq = sem("c_seq")
        flat = out.rearrange("b t c -> (b t) c")
        block = ctx.enter_context(nc.Block())

        @block.gpsimd
        def _(pool):
            for i in range(TILES):
                if i >= DEPTH:
                    pool.wait_ge(added, K * (i - DEPTH + 1))
                for k in range(K):
                    nc.gpsimd.indirect_dma_start(row[i % DEPTH][k][:], None, S["results"],
                                                 bass.IndirectOffsetOnAxis(S["slot"][:, i, k:k + 1], 0),
                                                 bounds_check=LISTED * P - 1).then_inc(fetched[i % DEPTH][k], 16)

        @block.vector
        def _(dve):
            v = nc.vector
            count = [0]

            def then(ins):
                count[0] += 1
                ins.then_inc(seq, 1)
                dve.wait_ge(seq, count[0])

            then(v.tensor_reduce(z[:], S["logits"][:], AX.X, ALU.add))
            then(v.reciprocal(rz[:], z[:]))
            v.tensor_tensor(prob[:], S["logits"][:], rz[:].unsqueeze(2).to_broadcast([P, TILES, E]), ALU.mult)
            for i in range(TILES):
                last = v.tensor_tensor(hot[:, i, :, :], S["iota_e"][:].unsqueeze(1).to_broadcast([P, K, E]),
                                       S["expert"][:, i, :].unsqueeze(2).to_broadcast([P, K, E]), ALU.is_equal)
            then(last)
            for i in range(TILES):
                last = v.tensor_tensor(times[:, i, :, :], hot[:, i, :, :], prob[:, i, :].unsqueeze(1).to_broadcast([P, K, E]), ALU.mult)
            then(last)
            then(v.tensor_reduce(weight[:], times[:], AX.X, ALU.add))
            then(v.tensor_reduce(wsum[:], weight[:], AX.X, ALU.add))
            then(v.reciprocal(rwsum[:], wsum[:]))
            then(v.tensor_tensor(weight[:], weight[:], rwsum[:].unsqueeze(2).to_broadcast([P, TILES, K]), ALU.mult))
            for i in range(TILES):
                for k in range(K):
                    dve.wait_ge(fetched[i % DEPTH][k], 16 * (i // DEPTH + 1))
                    if k:
                        dve.wait_ge(added, K * i + k)
                    nc.vector.scalar_tensor_tensor(out=S["x"][:, i, :], in0=row[i % DEPTH][k][:], scalar=weight[:, i, k:k + 1],
                                                   in1=S["x"][:, i, :], op0=ALU.mult, op1=ALU.add).then_inc(added, 1)

        @block.sync
        def _(sp):
            for i in range(TILES):
                sp.wait_ge(added, K * (i + 1))
                sp.dma_start(flat[i * P:(i + 1) * P, :], S["x"][:, i, :]).then_inc(stored, 16)
            sp.wait_ge(stored, 16 * TILES)


def program(nc, A, out):
    with ExitStack() as ctx:
        S = {}

        def keep(stack, name, shape, dt):
            S[name] = stack.enter_context(nc.sbuf_tensor("s_" + name, shape, dt))

        S["lists"] = nc.dram_tensor("lists", [P * 512, 1], U32, kind="Internal").ap()
        S["rows"] = nc.dram_tensor("rows", [TOKENS, C], F32, kind="Internal").ap()
        S["results"] = nc.dram_tensor("results", [LISTED * P, C], F32, kind="Internal").ap()
        keep(ctx, "x", [P, TILES, C], F32)
        keep(ctx, "ident", [P, P], F32)
        keep(ctx, "identb", [P, P], BF16)
        keep(ctx, "tri", [P, P], F32)
        keep(ctx, "ones", [P, P], F32)
        keep(ctx, "round", [P, 1], F32)
        keep(ctx, "two", [P, 1], F32)
        keep(ctx, "mhalf", [P, 1], F32)
        keep(ctx, "token", [P, TILES], U32)
        keep(ctx, "slot", [P, TILES, K], U32)
        keep(ctx, "expert", [P, TILES, K], F32)
        keep(ctx, "logits", [P, TILES, E], F32)
        keep(ctx, "list", [P, 512], U32)
        keep(ctx, "zrow", [P, 512], U32)
        assert LISTED + 1 <= P
        for name in ("tile_expert", "tile_col", "tile_next"):
            keep(ctx, name, [1, P], I32)
        keep(ctx, "tile_end", [1, 1], I32)
        keep(ctx, "iota_e", [P, E], F32)
        keep(ctx, "gate_wT", [P, CT, E], F32)
        keep(ctx, "tfs", [P, TILES], F32)
        with ExitStack() as front:
            keep(front, "ratio1", [P, TILES, C], F32)
            with ExitStack() as layer0:
                keep(layer0, "ratio0", [P, TILES, C], F32)
                S["ratio"] = [S["ratio0"], S["ratio1"]]
                keep(layer0, "u", [P, LAYERS, CT], F32)
                keep(layer0, "decay", [P, B * UNITS], F32)
                setup(nc, A, S)
                mix(nc, A, S)
                keep(layer0, "wscale", [P, 3], F32)
                keep(layer0, "ln", [P, INNER], F32)
                S["wT"] = [layer0.enter_context(nc.sbuf_tensor(f"s_wT{m}", shape, BF16))
                           for m, shape in enumerate(([P, CT, INNER], [P, CT, INNER], [P, IT, C]))]
                ternary(nc, A, S)
                bitnet(nc, A, S)
            route(nc, A, S)
        experts(nc, A, S)
        combine(nc, A, S, out)


_INS = ["x", "fside_BxSxS_0", "cond_512", "L0_cond_w", "L0_cond_u", "L0_ffn_w_gate", "L0_ffn_w_up", "L0_ffn_w_down",
        "L0_ffn_ln_weight", "L1_cond_w", "L1_cond_u", "L1_ffn_gate_w", "L1_ffn_Wg", "L1_ffn_Wu", "L1_ffn_Wd",
        "L1_ffn_cWg", "L1_ffn_cWu", "L1_ffn_cWd"]


def kernel(**inputs):
    import concourse.bacc as _bacc
    from concourse.bass_utils import run_bass_kernel_spmd as _run

    nc = _bacc.Bacc("TRN2", target_bir_lowering=False, num_devices=1)
    arrays, A = {}, {}
    for name in _INS:
        v = np.ascontiguousarray(inputs[name])
        arrays[f"in_{name}"] = v
        A[name] = nc.dram_tensor(f"in_{name}", v.shape, mybir.dt.from_np(v.dtype), kind="ExternalInput").ap()
    out = nc.dram_tensor("out_0", (B, T, C), F32, kind="ExternalOutput").ap()
    program(nc, A, out)
    r = _run(nc, [arrays], core_ids=[0])
    return r.results[0]["out_0"]
```
